# Optimizing a Trainium2 kernel written in Bass

```python
import numpy as np
import jax
import jax.numpy as jnp

def _softmax(x, axis=-1):
    return jax.nn.softmax(x, axis=axis)

def _gelu(x):
    return jax.nn.gelu(x, approximate=True)

def _silu(x):
    return jax.nn.silu(x)

def _sigmoid(x):
    return jax.nn.sigmoid(x)

def _layernorm(x, axis=-1, eps=1e-05):
    m = jnp.mean(x, axis=axis, keepdims=True)
    v = jnp.var(x, axis=axis, keepdims=True)
    return (x - m) / jnp.sqrt(v + eps)

def _scatter_add(tgt, idx, src, axis=0):
    return tgt.at[idx].add(src)

def _segment_sum(src, seg, n):
    return jax.ops.segment_sum(src, seg, n)
kernel_name = 'mk_decoder_postln_d2_seqx_r4_32e19d'

def setup_inputs(seed: int=0):
    np.random.seed(seed)
    _w = jnp.asarray

    def _rec_inputs():
        import jax
        import jax.numpy as jnp
        _rk = jax.random.key(seed)
        x = 7.22e-05 + 1 * jax.random.normal(jax.random.fold_in(_rk, 1), (32, 100, 256), jnp.float32)
        _lenS = 100 - jax.random.randint(jax.random.fold_in(_rk, 7), (32,), 0, max(1, 100 // 4) + 1, jnp.int32)
        _lenS2 = 361 - jax.random.randint(jax.random.fold_in(_rk, 8), (32,), 0, max(1, 361 // 4) + 1, jnp.int32)
        _ctx_1024P = jax.random.normal(jax.random.fold_in(_rk, 11), (32, 16, 256), jnp.float32)
        _ctx_1024c = jax.random.dirichlet(jax.random.fold_in(_rk, 511), 0.3 * jnp.ones((16,), jnp.float32), (32, 361))
        _ctx_1024t = jnp.einsum('bsk,bkd->bsd', _ctx_1024c, _ctx_1024P)
        _ctx_1024t = _ctx_1024t * jax.lax.rsqrt(jnp.mean(jnp.square(_ctx_1024t)) + 1e-12) * 0.953939
        ctx_1024 = 4.13588e-05 + 0.999923 * (_ctx_1024t + 0.3 * jax.random.normal(jax.random.fold_in(_rk, 611), (32, 361, 256), jnp.float32))
        fside_BxSxS2_0 = jax.random.uniform(jax.random.fold_in(_rk, 12), (32, 100, 361), jnp.float32, 0.0, 10)
        return (x, ctx_1024, fside_BxSxS2_0)
    x, ctx_1024, fside_BxSxS2_0 = _rec_inputs()

    def _L0_attn_setup():
        import jax, jax.numpy as jnp
        import numpy as np
        B, L, D, H = (2, 512, 256, 16)
        C = D // H
        SCALE = 1.0 / np.sqrt(D).astype(np.float32)
        key = jax.random.key(seed)
        ks = jax.random.split(key, 5)
        return {'x': jax.random.normal(ks[0], (B, L, D), dtype=jnp.float32), 'w_qkv': jax.random.normal(ks[1], (3 * D, D), dtype=jnp.float32) * (1.0 / np.sqrt(D)), 'b_qkv': jax.random.normal(ks[2], (3 * D,), dtype=jnp.float32) * 0.02, 'w_o': jax.random.normal(ks[3], (D, D), dtype=jnp.float32) * (1.0 / np.sqrt(D)), 'b_o': jax.random.normal(ks[4], (D,), dtype=jnp.float32) * 0.02}
    _L0_attn_all = _L0_attn_setup()
    _L0_attn_in = {k: v for k, v in _L0_attn_all.items() if k in ('w_qkv', 'b_qkv', 'w_o', 'b_o')}
    del _L0_attn_all

    def _L0_xattn_setup():
        import jax, jax.numpy as jnp
        import numpy as np
        EMBED_DIM = 256
        NUM_HEADS = 16
        HEAD_DIM = EMBED_DIM // NUM_HEADS
        B, SQ, SK = (4, 512, 512)

        def _xavier(key, shape):
            fan_in, fan_out = (shape[1], shape[0])
            limit = float(np.sqrt(6.0 / (fan_in + fan_out)))
            return jax.random.uniform(key, shape, jnp.float32, -limit, limit)
        key = jax.random.key(seed)
        ks = jax.random.split(key, 9)
        return {'query': jax.random.normal(ks[0], (B, SQ, EMBED_DIM), jnp.float32), 'key_': jax.random.normal(ks[1], (B, SK, EMBED_DIM), jnp.float32), 'value': jax.random.normal(ks[2], (B, SK, EMBED_DIM), jnp.float32), 'distances': jax.random.uniform(ks[3], (B, SQ, SK), jnp.float32, 0.01, 10.0), 'Wq': _xavier(ks[4], (EMBED_DIM, EMBED_DIM)), 'bq': jnp.zeros((EMBED_DIM,), jnp.float32), 'Wk': _xavier(ks[5], (EMBED_DIM, EMBED_DIM)), 'bk': jnp.zeros((EMBED_DIM,), jnp.float32), 'Wv': _xavier(ks[6], (EMBED_DIM, EMBED_DIM)), 'bv': jnp.zeros((EMBED_DIM,), jnp.float32), 'Wo': _xavier(ks[7], (EMBED_DIM, EMBED_DIM)), 'bo': jnp.zeros((EMBED_DIM,), jnp.float32), 'distance_scaling': jnp.asarray(1.0, jnp.float32)}
    _L0_xattn_all = _L0_xattn_setup()
    _L0_xattn_in = {k: v for k, v in _L0_xattn_all.items() if k in ('Wq', 'bq', 'Wk', 'bk', 'Wv', 'bv', 'Wo', 'bo', 'distance_scaling')}
    del _L0_xattn_all

    def _L0_ffn_setup():
        import jax, jax.numpy as jnp
        import numpy as np
        LN_EPS = 0.001
        EPS = 1e-05
        QB = 128.0

        def ste_round(x):
            return x + jax.lax.stop_gradient(jnp.round(x) - x)
        key = jax.random.key(seed)
        k1, k2 = jax.random.split(key)
        x = jax.random.normal(k1, (4, 2048, 256), dtype=jnp.float32)
        weight = jax.random.normal(k2, (256, 256), dtype=jnp.float32) * 0.02
        ln_gamma = jnp.ones((256,), dtype=jnp.float32)
        ln_beta = jnp.zeros((256,), dtype=jnp.float32)
        return {'x': x, 'weight': weight, 'ln_gamma': ln_gamma, 'ln_beta': ln_beta}
    _L0_ffn_all = _L0_ffn_setup()
    _L0_ffn_in = {k: v for k, v in _L0_ffn_all.items() if k in ('weight', 'ln_gamma', 'ln_beta')}
    del _L0_ffn_all

    def _L1_attn_setup():
        import jax, jax.numpy as jnp
        import numpy as np
        import math
        B, S, E, H = (2, 512, 256, 16)
        D = E // H
        key = jax.random.key(seed)
        ks = jax.random.split(key, 5)
        scale_p = 1.0 / math.sqrt(D)
        return {'x': jax.random.normal(ks[0], (B, S, E), dtype=jnp.float32), 'Wq': jax.random.normal(ks[1], (D, D), dtype=jnp.float32) * scale_p, 'Wk': jax.random.normal(ks[2], (D, D), dtype=jnp.float32) * scale_p, 'Wv': jax.random.normal(ks[3], (D, D), dtype=jnp.float32) * scale_p, 'W_out': jax.random.normal(ks[4], (E, E), dtype=jnp.float32) * (1.0 / math.sqrt(E)), 'b_out': jnp.zeros((E,), dtype=jnp.float32)}
    _L1_attn_all = _L1_attn_setup()
    _L1_attn_in = {k: v for k, v in _L1_attn_all.items() if k in ('Wq', 'Wk', 'Wv', 'W_out', 'b_out')}
    del _L1_attn_all

    def _L1_xattn_setup():
        import jax, jax.numpy as jnp
        import numpy as np
        B, S, D, H = (2, 512, 256, 16)
        DH = D // H

        def _split_heads(x):
            b, s, _ = x.shape
            return x.reshape(b, s, H, DH).transpose(0, 2, 1, 3)
        key = jax.random.key(seed)
        ks = jax.random.split(key, 11)
        s = 0.02
        return {'queries': jax.random.normal(ks[0], (B, S, D), dtype=jnp.float32), 'keys': jax.random.normal(ks[1], (B, S, D), dtype=jnp.float32), 'values': jax.random.normal(ks[2], (B, S, D), dtype=jnp.float32), 'Wq': jax.random.normal(ks[3], (D, D), dtype=jnp.float32) * s, 'bq': jnp.zeros((D,), dtype=jnp.float32), 'Wk': jax.random.normal(ks[4], (D, D), dtype=jnp.float32) * s, 'bk': jnp.zeros((D,), dtype=jnp.float32), 'Wv': jax.random.normal(ks[5], (D, D), dtype=jnp.float32) * s, 'bv': jnp.zeros((D,), dtype=jnp.float32), 'Wo': jax.random.normal(ks[6], (D, D), dtype=jnp.float32) * s, 'bo': jnp.zeros((D,), dtype=jnp.float32)}
    _L1_xattn_all = _L1_xattn_setup()
    _L1_xattn_in = {k: v for k, v in _L1_xattn_all.items() if k in ('Wq', 'bq', 'Wk', 'bk', 'Wv', 'bv', 'Wo', 'bo')}
    del _L1_xattn_all

    def _L1_ffn_setup():
        import jax, jax.numpy as jnp
        import numpy as np
        D = 256
        E = 8
        key = jax.random.key(seed)
        ks = jax.random.split(key, 7)
        s = 1.0 / np.sqrt(D)
        x = jax.random.normal(ks[0], (4, 512, D), dtype=jnp.float32)
        Wg = jax.random.uniform(ks[1], (D, E), minval=-s, maxval=s, dtype=jnp.float32)
        bg = jax.random.uniform(ks[2], (E,), minval=-s, maxval=s, dtype=jnp.float32)
        W1 = jax.random.uniform(ks[3], (E, D, D), minval=-s, maxval=s, dtype=jnp.float32)
        b1 = jax.random.uniform(ks[4], (E, D), minval=-s, maxval=s, dtype=jnp.float32)
        W2 = jax.random.uniform(ks[5], (E, D, D), minval=-s, maxval=s, dtype=jnp.float32)
        b2 = jax.random.uniform(ks[6], (E, D), minval=-s, maxval=s, dtype=jnp.float32)
        return {'x': x, 'Wg': Wg, 'bg': bg, 'W1': W1, 'b1': b1, 'W2': W2, 'b2': b2}
    _L1_ffn_all = _L1_ffn_setup()
    _L1_ffn_in = {k: v for k, v in _L1_ffn_all.items() if k in ('Wg', 'bg', 'W1', 'b1', 'W2', 'b2')}
    del _L1_ffn_all
    return {'x': x, 'ctx_1024': ctx_1024, 'fside_BxSxS2_0': fside_BxSxS2_0, 'L0_attn_w_qkv': _L0_attn_in['w_qkv'], 'L0_attn_b_qkv': _L0_attn_in['b_qkv'], 'L0_attn_w_o': _L0_attn_in['w_o'], 'L0_attn_b_o': _L0_attn_in['b_o'], 'L0_xattn_Wq': _L0_xattn_in['Wq'], 'L0_xattn_bq': _L0_xattn_in['bq'], 'L0_xattn_Wk': _L0_xattn_in['Wk'], 'L0_xattn_bk': _L0_xattn_in['bk'], 'L0_xattn_Wv': _L0_xattn_in['Wv'], 'L0_xattn_bv': _L0_xattn_in['bv'], 'L0_xattn_Wo': _L0_xattn_in['Wo'], 'L0_xattn_bo': _L0_xattn_in['bo'], 'L0_xattn_distance_scaling': _L0_xattn_in['distance_scaling'], 'L0_ffn_weight': _L0_ffn_in['weight'], 'L0_ffn_ln_gamma': _L0_ffn_in['ln_gamma'], 'L0_ffn_ln_beta': _L0_ffn_in['ln_beta'], 'L1_attn_Wq': _L1_attn_in['Wq'], 'L1_attn_Wk': _L1_attn_in['Wk'], 'L1_attn_Wv': _L1_attn_in['Wv'], 'L1_attn_W_out': _L1_attn_in['W_out'], 'L1_attn_b_out': _L1_attn_in['b_out'], 'L1_xattn_Wq': _L1_xattn_in['Wq'], 'L1_xattn_bq': _L1_xattn_in['bq'], 'L1_xattn_Wk': _L1_xattn_in['Wk'], 'L1_xattn_bk': _L1_xattn_in['bk'], 'L1_xattn_Wv': _L1_xattn_in['Wv'], 'L1_xattn_bv': _L1_xattn_in['bv'], 'L1_xattn_Wo': _L1_xattn_in['Wo'], 'L1_xattn_bo': _L1_xattn_in['bo'], 'L1_ffn_Wg': _L1_ffn_in['Wg'], 'L1_ffn_bg': _L1_ffn_in['bg'], 'L1_ffn_W1': _L1_ffn_in['W1'], 'L1_ffn_b1': _L1_ffn_in['b1'], 'L1_ffn_W2': _L1_ffn_in['W2'], 'L1_ffn_b2': _L1_ffn_in['b2']}

def reference(x, ctx_1024, fside_BxSxS2_0, L0_attn_w_qkv, L0_attn_b_qkv, L0_attn_w_o, L0_attn_b_o, L0_xattn_Wq, L0_xattn_bq, L0_xattn_Wk, L0_xattn_bk, L0_xattn_Wv, L0_xattn_bv, L0_xattn_Wo, L0_xattn_bo, L0_xattn_distance_scaling, L0_ffn_weight, L0_ffn_ln_gamma, L0_ffn_ln_beta, L1_attn_Wq, L1_attn_Wk, L1_attn_Wv, L1_attn_W_out, L1_attn_b_out, L1_xattn_Wq, L1_xattn_bq, L1_xattn_Wk, L1_xattn_bk, L1_xattn_Wv, L1_xattn_bv, L1_xattn_Wo, L1_xattn_bo, L1_ffn_Wg, L1_ffn_bg, L1_ffn_W1, L1_ffn_b1, L1_ffn_W2, L1_ffn_b2):
    import jax
    import jax.numpy as jnp

    def _L0_attn_ref(x, w_qkv, b_qkv, w_o, b_o):
        import jax, jax.numpy as jnp
        import numpy as np
        B, L, D, H = (2, 512, 256, 16)
        C = D // H
        SCALE = 1.0 / np.sqrt(D).astype(np.float32)
        b, l, d = x.shape
        h, c = (H, d // H)
        qkv = jnp.einsum('bld,ed->ble', x, w_qkv) + b_qkv
        q, k, v = jnp.split(qkv, 3, axis=-1)
        q = q.reshape(b, l, h, c)
        k = k.reshape(b, l, h, c)
        v = v.reshape(b, l, h, c)
        attn = jax.nn.softmax(jnp.einsum('blhc,bmhc->bhlm', q, k) * SCALE, axis=-1)
        heads = jnp.einsum('bhlm,bmhc->blhc', attn, v).reshape(b, l, d)
        return jnp.einsum('bld,ed->ble', heads, w_o) + b_o + x

    def _L0_xattn_ref(query, key_, value, distances, Wq, bq, Wk, bk, Wv, bv, Wo, bo, distance_scaling):
        import jax, jax.numpy as jnp
        import numpy as np
        EMBED_DIM = 256
        NUM_HEADS = 16
        HEAD_DIM = EMBED_DIM // NUM_HEADS
        B, SQ, SK = (4, 512, 512)

        def _xavier(key, shape):
            fan_in, fan_out = (shape[1], shape[0])
            limit = float(np.sqrt(6.0 / (fan_in + fan_out)))
            return jax.random.uniform(key, shape, jnp.float32, -limit, limit)
        b, sq, e = query.shape
        sk = key_.shape[1]
        h, d = (NUM_HEADS, HEAD_DIM)
        q = (query @ Wq.T + bq) * d ** (-0.5)
        k = key_ @ Wk.T + bk
        v = value @ Wv.T + bv
        q = q.reshape(b, sq, h, d).transpose(0, 2, 1, 3)
        k = k.reshape(b, sk, h, d).transpose(0, 2, 1, 3)
        v = v.reshape(b, sk, h, d).transpose(0, 2, 1, 3)
        scores = jnp.einsum('bhqd,bhkd->bhqk', q, k)
        distance_bias = -jnp.log(distances + 1e-09) * jnp.abs(distance_scaling)
        scores = scores + distance_bias[:, None, :, :]
        attn = jax.nn.softmax(scores, axis=-1)
        out = jnp.einsum('bhqk,bhkd->bhqd', attn, v)
        out = out.transpose(0, 2, 1, 3).reshape(b, sq, e)
        return out @ Wo.T + bo

    def _L0_ffn_ref(x, weight, ln_gamma, ln_beta):
        import jax, jax.numpy as jnp
        import numpy as np
        LN_EPS = 0.001
        EPS = 1e-05
        QB = 128.0

        def ste_round(x):
            return x + jax.lax.stop_gradient(jnp.round(x) - x)
        mu = jnp.mean(x, axis=-1, keepdims=True)
        var = jnp.var(x, axis=-1, keepdims=True)
        xn = (x - mu) * jax.lax.rsqrt(var + LN_EPS) * ln_gamma + ln_beta
        beta = jnp.mean(jnp.abs(weight))
        w_q = jnp.clip(ste_round(weight / (beta + EPS)), -1.0, 1.0)
        gamma = jnp.max(jnp.abs(xn))
        xq = jnp.clip(xn * QB / gamma, -QB + EPS, QB - EPS)
        y = jnp.einsum('bsd,du->bsu', xq, w_q)
        return y * (gamma * beta / QB)

    def _L1_attn_ref(x, Wq, Wk, Wv, W_out, b_out):
        import jax, jax.numpy as jnp
        import numpy as np
        import math
        B, S, E, H = (2, 512, 256, 16)
        D = E // H
        b, s, e = x.shape
        xh = x.reshape(b, s, H, D)
        q = jnp.einsum('bshd,ed->bshe', xh, Wq)
        k = jnp.einsum('bshd,ed->bshe', xh, Wk)
        v = jnp.einsum('bshd,ed->bshe', xh, Wv)
        energy = jnp.einsum('bqhd,bkhd->bhqk', q, k) / jnp.sqrt(jnp.float32(e))
        attn = jax.nn.softmax(energy, axis=-1)
        out = jnp.einsum('bhqk,bkhd->bqhd', attn, v).reshape(b, s, e)
        return out @ W_out.T + b_out

    def _L1_xattn_ref(queries, keys, values, Wq, bq, Wk, bk, Wv, bv, Wo, bo):
        import jax, jax.numpy as jnp
        import numpy as np
        B, S, D, H = (2, 512, 256, 16)
        DH = D // H

        def _split_heads(x):
            b, s, _ = x.shape
            return x.reshape(b, s, H, DH).transpose(0, 2, 1, 3)
        q = _split_heads(queries @ Wq + bq)
        k = _split_heads(keys @ Wk + bk)
        v = _split_heads(values @ Wv + bv)
        scale = 1.0 / jnp.sqrt(jnp.float32(DH))
        scores = jnp.einsum('bhqd,bhkd->bhqk', q, k) * scale
        weights = jax.nn.softmax(scores, axis=-1)
        o = jnp.einsum('bhqk,bhkd->bhqd', weights, v)
        o = o.transpose(0, 2, 1, 3).reshape(queries.shape[0], queries.shape[1], D)
        return o @ Wo + bo

    def _L1_ffn_ref(x, Wg, bg, W1, b1, W2, b2):
        import jax, jax.numpy as jnp
        import numpy as np
        D = 256
        E = 8
        N, T, d = x.shape
        x_flat = x.reshape(N * T, d)
        logits = x_flat @ Wg + bg
        probs = jax.nn.softmax(logits, axis=-1)
        assignments = jnp.argmax(probs, axis=-1)
        h = jnp.einsum('nd,edh->neh', x_flat, W1) + b1[None]
        h = jax.nn.gelu(h, approximate=False)
        eo = jnp.einsum('neh,ehd->ned', h, W2) + b2[None]
        selected = jnp.take_along_axis(eo, assignments[:, None, None], axis=1)[:, 0, :]
        w = jnp.take_along_axis(probs, assignments[:, None], axis=1)
        out = (w * selected).reshape(N, T, d)
        return out
    x = _layernorm(x + _L0_attn_ref(x, L0_attn_w_qkv, L0_attn_b_qkv, L0_attn_w_o, L0_attn_b_o), axis=-1)
    x = _layernorm(x + _L0_xattn_ref(x, ctx_1024, ctx_1024, fside_BxSxS2_0, L0_xattn_Wq, L0_xattn_bq, L0_xattn_Wk, L0_xattn_bk, L0_xattn_Wv, L0_xattn_bv, L0_xattn_Wo, L0_xattn_bo, L0_xattn_distance_scaling), axis=-1)
    x = _layernorm(x + _L0_ffn_ref(x, L0_ffn_weight, L0_ffn_ln_gamma, L0_ffn_ln_beta), axis=-1)
    x = _layernorm(x + _L1_attn_ref(x, L1_attn_Wq, L1_attn_Wk, L1_attn_Wv, L1_attn_W_out, L1_attn_b_out), axis=-1)
    x = _layernorm(x + _L1_xattn_ref(x, ctx_1024, ctx_1024, L1_xattn_Wq, L1_xattn_bq, L1_xattn_Wk, L1_xattn_bk, L1_xattn_Wv, L1_xattn_bv, L1_xattn_Wo, L1_xattn_bo), axis=-1)
    x = _layernorm(x + _L1_ffn_ref(x, L1_ffn_Wg, L1_ffn_bg, L1_ffn_W1, L1_ffn_b1, L1_ffn_W2, L1_ffn_b2), axis=-1)
    return x

_drawn_inputs = setup_inputs


def setup_inputs(seed=0):
    import zlib

    import numpy as np

    out = dict(_drawn_inputs(seed))
    spreads = {'L0_xattn_bq': (0.0, 0.317),
     'L0_xattn_bk': (0.0, 0.8),
     'L0_xattn_bv': (0.0, 0.1),
     'L0_xattn_bo': (0.0, 0.1),
     'L0_ffn_ln_gamma': (1.0, 0.2),
     'L0_ffn_ln_beta': (0.0, 0.314),
     'L1_attn_b_out': (0.0, 0.1),
     'L1_xattn_bq': (0.0, 0.8),
     'L1_xattn_bk': (0.0, 0.8),
     'L1_xattn_bv': (0.0, 0.1),
     'L1_xattn_bo': (0.0, 0.1)}
    factors = {'L0_attn_b_qkv': 4.013,
     'L0_attn_b_o': 5.002,
     'L1_xattn_Wq': 8.0,
     'L1_xattn_Wk': 8.0,
     'L1_ffn_bg': 5.236,
     'L1_ffn_b1': 8.0,
     'L1_ffn_b2': 5.915}
    for name, (base, spread) in spreads.items():
        noise = np.random.default_rng([zlib.crc32(name.encode()), seed]).standard_normal(out[name].shape)
        drawn = base * np.exp(spread * noise) if base else spread * noise
        out[name] = jnp.asarray(drawn.astype(out[name].dtype))
    for name, factor in factors.items():
        out[name] = (out[name] * factor).astype(out[name].dtype)
    return out
```

```python
from contextlib import ExitStack

import concourse.bass as bass
from concourse import mybir
import numpy as np

F32 = mybir.dt.float32
BF16 = mybir.dt.bfloat16
I32 = mybir.dt.int32
ACT = mybir.ActivationFunctionType
ALU = mybir.AluOpType
AX = mybir.AxisListType

B, S, D, H, SK, E = 32, 100, 256, 16, 361, 8
DH = D // H
P = 128
KC = D // P
TERMS = 3
PRODUCTS = [(0, 3), (1, 2), (2, 1)]
BLOCKS = sum(n for _, n in PRODUCTS)
STACK = BLOCKS * DH
GROUP = 4
P_RING = 8
S_RING = 3
SB_RING = 4
LN_EPS = 1e-5
FFN_LN_EPS = 1e-3
FFN_EPS = 1e-5
QB = 128.0
MB = 4
ROUND = 1.5 * 2.0 ** 23
ROOT_GUESS = float(0x5F3759DF)
ROOT_STEPS = 3 * 4
DIST = B * S * SK // P
DIST_CHUNKS = 7
DIST_CHUNK = -(-DIST // DIST_CHUNKS)
PAIRS = B // 2
WORK = 22400
CONSTANTS = 6 + E
Q_SCALED = 7
W_LOADED = 16 * (30 + 3 * H)

PLAN_SELF = {
    "turn_x": [-38], "copy_xT": [-36], "keys": [-34, -34], "round_keys": [-32, -31], "rest_of_keys": [-30, -29],
    "queries": [-27], "round_queries": [-25], "rest_of_queries": [-23], "third_of_keys": [-28, -27],
    "third_of_queries": [-22], "values": [-6], "copy_values": [-4], "residual": [12],
    "scores": [0, 4, 8, 12], "maximum": [2, 6, 10, 14], "exponentiate": [4 + h for h in range(H)],
    "turn_probs": [10, 14, 18, 22], "copy_probs": [12, 16, 20, 24], "sum_heads": [19, 27],
    "invert": [21], "turn_inv": [23], "copy_inv": [24], "scale_heads": [30], "project": [34],
    "add_residual": [36], "take_stats": [37], "take_moments": [38], "guess_root": [39], "root": [39], "norm": [47]}
PLAN_CROSS = {
    "turn_x": [-32], "copy_xT": [-31], "keys": [-30, -25], "round_keys": [-28, -23], "rest_of_keys": [-27, -22],
    "queries": [-20], "round_queries": [-18], "rest_of_queries": [-17], "third_of_keys": [-26, -21],
    "third_of_queries": [-15], "values": [-10, -8, -6], "copy_values": [-9, -7, -5], "residual": [9],
    "scores": list(range(H)), "maximum": list(range(H)), "exponentiate": [1 + h for h in range(H)],
    "turn_probs": [4 * g + 6 + c for g in range(H // 4) for c in range(3)],
    "copy_probs": [4 * g + 7 + c for g in range(H // 4) for c in range(3)], "sum_heads": [15, 23],
    "invert": [18], "turn_inv": [20], "copy_inv": [21], "scale_heads": [26], "project": [29],
    "add_residual": [31], "take_stats": [32], "take_moments": [33], "guess_root": [34], "root": [34], "norm": [39]}

FFN_STEPS = 6
PLAN_FFN = {"scale": [-10], "turn": [-7], "clip": [-4], "project": [-1], "add": [3], "take_stats": [5],
            "take_moments": [7], "keep_moments": [9]}


def at_least(eng, sem, value):
    if isinstance(value, int) and value <= 0:
        return
    eng.wait_ge(sem, value)


class Steps:

    def __init__(self, plan, steps):
        self.plan, self.steps = plan, steps


class Attention:

    def __init__(self, keys, cross, wq, wk, wv, wo, bq, bk, bo, q_scale, biased, twice):
        self.keys, self.cross, self.biased = keys, cross, biased
        self.wq, self.wk, self.wv, self.wo = wq, wk, wv, wo
        self.bq, self.bk, self.bo, self.q_scale = bq, bk, bo, q_scale
        self.twice = twice
        self.chunks = -(-keys // P)
        size = -(-keys // self.chunks)
        self.spans = [(c * size, min(size, keys - c * size)) for c in range(self.chunks)]
        self.per_unit = GROUP if GROUP * keys <= 512 else 1
        self.units = H // self.per_unit
        self.fills = (H // GROUP) * self.chunks
        self.by_dve = [self.chunks == 1 or f % self.chunks == 1 or f == self.chunks + 2 for f in range(self.fills)]
        self.plan = PLAN_CROSS if cross else PLAN_SELF
        if biased:
            self.plan = self.plan | {"next_stats": [42], "next_moments": [43], "keep_moments": [44]}
        self.steps = H
        self.base = {}


def decoder(nc, d, out):
    ctx = ExitStack()

    def sb(name, shape, dt=F32):
        return ctx.enter_context(nc.sbuf_tensor(name, shape, dt))

    def sem(name):
        return ctx.enter_context(nc.semaphore(name))

    with ctx:
        state = sb("state", [S, B, D])
        ident = sb("ident", [P, P])
        ones = sb("ones", [P, P])
        tiny = sb("tiny", [P, 1])
        scaling = sb("scaling", [P, 1])
        neg_abs_ds = sb("neg_abs_ds", [P, 1])

        work = sb("work", [P, WORK])

        def carve(sizes):
            ends = [sum(sizes[:i + 1]) for i in range(len(sizes))]
            assert ends[-1] <= WORK
            return [work[:, e - n:e] for e, n in zip(ends, sizes)]

        k_stack, probs, probs_T, k_parts, ctxT, biased, k_rest, values, q_stack = carve(
            [H * SK, P_RING * SK, 2 * 3 * 2 * GROUP * S, TERMS * KC * SK, 2 * KC * SK, SB_RING * SK, KC * SK,
             2 * 3 * D, H * S])
        k_stack = k_stack[0:STACK].bitcast(BF16).rearrange("p (s n) -> p s n", s=2)
        probs = probs[0:S].rearrange("p (h n) -> p h n", h=P_RING)
        probs_T = probs_T.rearrange("p (a c h n) -> p a c h n", a=2, c=3, h=2 * GROUP)
        k_parts = k_parts.bitcast(BF16).rearrange("p (s n) -> p s n", s=2)
        ctxT = ctxT.rearrange("p (s k n) -> p s k n", s=2, k=KC)
        biased = biased[0:S].rearrange("p (h n) -> p h n", h=SB_RING)
        k_rest = k_rest.rearrange("p (m n) -> p m n", m=KC)
        values = values.rearrange("p (s c n) -> p s c n", s=2, c=3)
        q_stack = q_stack[0:STACK].bitcast(BF16).rearrange("p (s n) -> p s n", s=2)

        dist = work[:, WORK - 2 * DIST_CHUNK:WORK].rearrange("p (s n) -> p s n", s=2)

        xn = work[0:S, 0:B * D].rearrange("p (b d) -> p b d", b=B)

        w_up, w_down, xT_all, gelu_T, b_down_rows = carve(
            [E * KC * D, E * KC * D, KC * B * S, 2 * KC * MB * S, (P // E) * D])
        w_up = w_up.rearrange("p (e k n) -> p e k n", e=E, k=KC)
        w_down = w_down.rearrange("p (e k n) -> p e k n", e=E, k=KC)
        xT_all = xT_all.rearrange("p (k t) -> p k t", k=KC)
        gelu_T = gelu_T.rearrange("p (e m t) -> p e m t", e=2, m=KC)
        b_down_flat, b_down_rows = b_down_rows, b_down_rows.rearrange("p (b n) -> p b n", b=P // E)

        x_in = sb("x_in", [S, 2, D])
        x_res = sb("x_res", [S, 2, D])
        xT = sb("xT", [P, 2, KC, S])
        q_parts = sb("q_parts", [P, 2, TERMS, KC, S], BF16)
        q_rest = sb("q_rest", [P, KC, S])
        bias = sb("bias", [S, 2, SK])
        neg_max = sb("neg_max", [S, 2, H])
        sums = sb("sums", [S, 2, H])
        inv = sb("inv", [S, H])
        inv_wide = sb("inv_wide", [S, 2, 2, P])
        inv_T = sb("inv_T", [P, 2 * 2 * S])
        heads_par = sb("heads_par", [P, 2, 2, S])
        heads_T = sb("heads_T", [P, KC, S])
        y = sb("y", [S, D])
        stats = sb("stats", [S, 6])
        moments = sb("moments", [S, 2])
        state_stats_of = sb("state_stats", [S, 6])
        state_moments_of = sb("state_moments", [S, 2])
        root_in, root_tmp, rstd = sb("root_in", [S, 1]), sb("root_tmp", [S, 1]), sb("rstd", [S, 1])
        all_moments = sb("all_moments", [S, B, 2])
        all_root_in, all_root_tmp, all_rstd = (sb(n, [S, B]) for n in ("all_root_in", "all_root_tmp", "all_rstd"))

        ps_scores = ctx.enter_context(nc.psum_tensor("ps_scores", [P, S_RING, 512], F32))
        ps_probs = ctx.enter_context(nc.psum_tensor("ps_probs", [P, 2, 512], F32))
        ps_heads = ctx.enter_context(nc.psum_tensor("ps_heads", [P, 512], F32))
        ps_a = ctx.enter_context(nc.psum_tensor("ps_a", [P, 512], F32))
        ps_b = ctx.enter_context(nc.psum_tensor("ps_b", [P, 512], F32))

        w_qkv = sb("w_qkv", [P, KC, 3 * D])
        w = {n: sb("w_" + n, [P, KC, D]) for n in
             ("L0_attn_w_o", "L0_xattn_Wq", "L0_xattn_Wk", "L0_xattn_Wv", "L0_xattn_Wo", "L0_ffn_weight",
              "L1_attn_W_out", "L1_xattn_Wq", "L1_xattn_Wk", "L1_xattn_Wv", "L1_xattn_Wo")}
        w_diag = {n: sb("wd_" + n, [P, KC, D]) for n in ("L1_attn_Wq", "L1_attn_Wk", "L1_attn_Wv")}
        on_diagonal = {n: work[:, i * KC * D:(i + 1) * KC * D].rearrange("p (k n) -> p k n", k=KC)
                       for i, n in enumerate(("L1_attn_Wq", "L1_attn_Wk"))} | {"L1_attn_Wv": w_diag["L1_attn_Wv"]}
        b_qk = sb("b_qk", [P, 2 * KC])
        b_v = sb("b_v", [P, KC])
        b_col = {n: sb("b_" + n, [P, KC]) for n in
                 ("L0_xattn_bq", "L0_xattn_bk", "L0_xattn_bv", "L1_xattn_bq", "L1_xattn_bk", "L1_xattn_bv")}
        b_zero = sb("b_zero", [P, KC])
        b_out = {n: sb("bo_" + n, [S, D]) for n in ("L0_attn_b_o", "L0_xattn_bo", "L1_attn_b_out", "L1_xattn_bo")}
        ffn_gamma = sb("ffn_gamma", [S, D])
        ffn_beta = sb("ffn_beta", [S, D])
        w_gate = sb("w_gate", [P, KC, E])
        b_gate = sb("b_gate", [1, E])
        b_up = sb("b_up", [P, E, KC])

        k_bounce = nc.dram_tensor("k_bounce", [2, TERMS * D * SK], BF16).ap()
        q_bounce = nc.dram_tensor("q_bounce", [2, TERMS * D * S], BF16).ap()

        bias_dram = nc.dram_tensor("bias_dram", [B, S, SK], F32).ap()

        constants = sem("constants")
        state_loaded = sem("state_loaded")
        passed = sem("passed")
        dist_loaded = [sem(f"dist_loaded_{s}") for s in range(2)]
        bias_stored = [sem(f"bias_stored_{s}") for s in range(2)]
        logs_ready = sem("logs_ready")
        bias_scaled = sem("bias_scaled")
        diag_cleared = sem("diag_cleared")
        columns_ordered = sem("columns_ordered")
        w_loaded = sem("w_loaded")
        q_scaled = sem("q_scaled")
        ds_ready = sem("ds_ready")
        bv_out = sem("bv_out")
        b_out_ready = sem("b_out_ready")

        def rows(tile, first=0):
            return lambda k: tile[:, k, first:first + D]

        def by_feature(tile, first=0):
            return lambda k, m: tile[:, k, first + m * P:first + (m + 1) * P]

        sa0 = Attention(S, False, by_feature(w_qkv), by_feature(w_qkv, D), rows(w_qkv, 2 * D), w["L0_attn_w_o"],
                        b_qk[:, 0:KC], b_qk[:, KC:2 * KC], b_out["L0_attn_b_o"],
                        (w_qkv[:, :, 0:D], float(D) ** -0.5), False, True)
        xa0 = Attention(SK, True, by_feature(w["L0_xattn_Wq"]), by_feature(w["L0_xattn_Wk"]), rows(w["L0_xattn_Wv"]),
                        w["L0_xattn_Wo"], b_col["L0_xattn_bq"], b_col["L0_xattn_bk"], b_out["L0_xattn_bo"],
                        (w["L0_xattn_Wq"][:, :, :], DH ** -0.5), True, False)
        sa1 = Attention(S, False, by_feature(w_diag["L1_attn_Wq"]), by_feature(w_diag["L1_attn_Wk"]),
                        rows(w_diag["L1_attn_Wv"]), w["L1_attn_W_out"], b_zero, b_zero, b_out["L1_attn_b_out"],
                        (w_diag["L1_attn_Wq"][:, :, :], float(D) ** -0.5), False, False)
        xa1 = Attention(SK, True, by_feature(w["L1_xattn_Wq"]), by_feature(w["L1_xattn_Wk"]), rows(w["L1_xattn_Wv"]),
                        w["L1_xattn_Wo"], b_col["L1_xattn_bq"], b_col["L1_xattn_bk"], b_out["L1_xattn_bo"],
                        (w["L1_xattn_Wq"][:, :, :], DH ** -0.5), False, False)
        phases = [sa0, xa0, sa1, xa1]
        value_biases = [(b_v, sa0), (b_col["L0_xattn_bv"], xa0), (b_col["L1_xattn_bv"], xa1)]

        once = ["x_turned", "xT_ready", "q_done", "q_second", "q_split", "residual_ready",
                "inv_ready", "inv_turned", "inv_T_ready", "heads_scaled", "heads_ready",
                "out_projected", "y_ready", "stats_ready", "moments_ready", "root_in_ready", "guess_ready", "state_ready"]
        times = {name: lambda ph: 1 for name in once}
        times |= {name: lambda ph: KC for name in
                  ("k_done", "k_rounded", "k_rest_ready", "k_second", "k_split", "q_rounded", "q_rest_ready")}
        times |= {name: lambda ph: ph.chunks for name in ("v_projected", "v_ready")}
        times |= {name: lambda ph: ph.units for name in ("scores_ready", "maxed")}
        times |= {"root_step": lambda ph: ROOT_STEPS}
        times |= {"residual_once": lambda ph: int(ph.twice),
                  "probs_ready": lambda ph: H,
                  "probs_turned": lambda ph: ph.fills,
                  "act_copied": lambda ph: ph.by_dve.count(False),
                  "dve_copied": lambda ph: ph.by_dve.count(True),
                  "heads_summed": lambda ph: 2,
                  "inv_wide_ready": lambda ph: 2}
        signal = {name: sem(name) for name in times}
        dma_times = {"x_loaded": lambda ph: 16, "ctx_loaded": lambda ph: 16 * ph.cross,
                     "bias_loaded": lambda ph: 16 * ph.biased, "bounced": lambda ph: 16 * 2,
                     "stacked": lambda ph: 16 * 2 * len(PRODUCTS)}
        dma_signal = {name: [sem(f"{name}_{s}") for s in range(2)] for name in dma_times}
        for i, ph in enumerate(phases):
            ph.base = {name: sum(B * n(p) for p in phases[:i]) for name, n in times.items()}
            ph.base |= {name: sum(PAIRS * n(p) for p in phases[:i]) for name, n in dma_times.items()}

        def reached(eng, ph, name, count, alone=False):
            if isinstance(count, int) and count <= 0:
                return
            (apart if alone else at_least)(eng, signal[name], ph.base[name] + count)

        def arrived(eng, ph, name, b, back=0, alone=False):
            count = dma_times[name](ph) * (b[0] + 1 - back)
            if isinstance(count, int) and count <= 0:
                return
            (apart if alone else at_least)(eng, dma_signal[name][b[1]], ph.base[name] + count)

        ffn_work = Steps(PLAN_FFN, FFN_STEPS)
        ffn = {name: sem("ffn_" + name) for name in
               ("w_sum", "w_total", "w_mean", "w_beta", "w_scaled", "w_rounded", "w_ready",
                "x_stats", "x_aggregated", "x_moments", "x_root_in", "x_guess", "x_root_step", "gained", "xn_ready", "row_max", "max_turned", "max_one",
                "max_spread", "gamma_ready", "gain_ready", "xq_scaled", "xq_turned", "xqT_ready",
                "projected", "y_ready", "y_stats", "y_aggregated", "y_moments", "y_root_in", "y_guess", "y_root_step", "state_ready",
                "w_inverse", "gamma_inverse")}
        row_max = sb("row_max", [S, 1])
        max_one = sb("max_one", [1, 1])
        gamma = sb("gamma", [S, 3])
        w_sum = sb("w_sum", [P, 1])
        w_beta = sb("w_beta", [P, 3])
        gain = sb("gain", [S, 2])
        xq = sb("xq", [S, 2, D])
        xqT = sb("xqT", [P, 2, KC, S])
        w_tmp = sb("w_tmp", [P, KC, D])

        moe = {name: sem("moe_" + name) for name in
               ("w_loaded", "rows_cleared", "rows_loaded", "x_turned", "xT_ready", "xT_kept", "gated", "logits_ready",
                "top_ready", "shifted", "exp_ready", "sum_ready", "weight_ready", "top_found", "rank_ready", "first_ready",
                "hot_found", "hot_ready", "hot_turned", "hot_T_ready", "b_down_done", "b_down_added",
                "up_done", "gelu_done", "down_done", "added", "y_stats", "y_aggregated", "y_moments", "y_root_in", "y_guess", "y_root_step", "out_ready")}
        moe_x_loaded = [sem(f"moe_x_loaded_{s}") for s in range(2)]
        stored = [sem(f"stored_{s}") for s in range(2)]
        logits = sb("logits", [S, B, E])
        top = sb("top", [S, B])
        shifted = sb("shifted", [S, B, E])
        exps = sb("exps", [S, B, E])
        top_weight = sb("top_weight", [S, B])
        rank = sb("rank", [S, B, E])
        rank_of = sb("rank_of", [S, E])
        hot = sb("hot", [S, B, E])
        hot_T = sb("hot_T", [P, 2, S])
        y_out = sb("y_out", [S, 2, D])

        block = ctx.enter_context(nc.Block())

        def apart(eng, sem, value):
            at_least(eng, sem, value)
            if not isinstance(value, int):
                eng.sem_inc(passed, 1)

        def number(b):
            return b[0] * 2 + b[1]

        def later(b, n):
            return (b[0] + (b[1] + n) // 2, (b[1] + n) % 2)

        def exists(b):
            return not isinstance(b[0], int) or 0 <= number(b) < B

        FIRST, LAST = (0, 0), (PAIRS - 1, 1)

        def over_batches(eng, body, ahead=0, behind=0):
            last = PAIRS - 1 - ahead // 2
            for pair in range(-ahead, 1):
                body((pair, 0))
                body((pair, 1))
            with eng.Fori(1, last) as pair:
                body((pair, 0))
                body((pair, 1))
            for pair in range(last, PAIRS + behind):
                body((pair, 0))
                body((pair, 1))

        def due(ph, name, b, h):
            return [(later(b, -(at // ph.steps)), part) for part, at in enumerate(ph.plan.get(name, []))
                    if at % ph.steps == h and exists(later(b, -(at // ph.steps)))]

        def rounds(eng, ph, step):
            def one(b):
                for h in range(ph.steps):
                    step(b, h)
            first = min(min(steps) for steps in ph.plan.values())
            last = max(max(steps) for steps in ph.plan.values())
            over_batches(eng, one, -(first // (2 * ph.steps)), -(-(last // ph.steps) // 2))

        def k_part(ph, s, t, m):
            first = (t * KC + m) * ph.keys
            return k_parts[:, s, first:first + ph.keys]

        def k_place(ph, m):
            return ps_b[:, 0:SK] if ph.cross else ps_b[:, m * S:(m + 1) * S]

        def no_more(count, most):
            return min(count, most) if isinstance(count, int) else count

        def copies(ph, b, f, dve):
            mine = [i for i in range(ph.fills) if ph.by_dve[i] == dve]
            return len(mine) * number(b) + sum(i <= f for i in mine)

        def wait_copied(eng, ph, b, f):
            dve = ph.by_dve[f]
            reached(eng, ph, "dve_copied" if dve else "act_copied", copies(ph, b, f, dve))

        def inverse_root(pool, step, before_it, value, scratch, result):
            for n in range(ROOT_STEPS // 4):
                at = before_it + 4 * n
                apart(pool, step, at)
                pool.tensor_tensor(scratch, result, result, ALU.mult).then_inc(step, 1)
                pool.wait_ge(step, at + 1)
                pool.tensor_tensor(scratch, scratch, value, ALU.mult).then_inc(step, 1)
                apart(pool, step, at + 2)
                pool.tensor_scalar(scratch, scratch, -0.5, 1.5, ALU.mult, ALU.add).then_inc(step, 1)
                pool.wait_ge(step, at + 3)
                pool.tensor_tensor(result, result, scratch, ALU.mult).then_inc(step, 1)

        def dist_span(c):
            return c * DIST_CHUNK, min(DIST_CHUNK, DIST - c * DIST_CHUNK)

        @block.sync
        def _(sp):
            def row(name, width):
                return d[name].rearrange("(a n) -> a n", a=1).to_broadcast([S, width])

            sp.dma_start(state[:, :, :], d["x"].rearrange("b s d -> s b d")).then_inc(state_loaded, 16)
            loads = [(w_qkv[:, :, :], d["L0_attn_w_qkv"].rearrange("(k p) n -> p k n", p=P))]
            loads += [(t[:, :, :], d[n].rearrange("(k p) n -> p k n", p=P)) for n, t in w.items()]
            loads += [(b_qk[:, :], d["L0_attn_b_qkv"][:, 0:2 * KC]), (b_v[:, :], d["b_v"])]
            loads += [(t[:, :], d[n]) for n, t in b_col.items()]
            loads += [(t[:, :], row(n, D)) for n, t in b_out.items()]
            loads += [(ffn_gamma[:, :], row("L0_ffn_ln_gamma", D)), (ffn_beta[:, :], row("L0_ffn_ln_beta", D)),
                      (w_gate[:, :, :], d["L1_ffn_Wg"].rearrange("(k p) e -> p k e", p=P)),
                      (b_gate[:, :], d["L1_ffn_bg"].rearrange("(a n) -> a n", a=1)),
                      (b_up[:, :, :], d["L1_ffn_b1"]),
                      (scaling[:, :], d["L0_xattn_distance_scaling"].rearrange("(a n) -> a n", a=1).to_broadcast([P, 1]))]
            for tile, source in loads:
                sp.dma_start(tile, source).then_inc(w_loaded, 16)
            sp.wait_ge(diag_cleared, len(w_diag))
            for n, t in on_diagonal.items():
                for h in range(H):
                    at, k = h * DH % P, h * DH // P
                    sp.dma_start(t[at:at + DH, k, h * DH:(h + 1) * DH], d[n]).then_inc(w_loaded, 16)
            assert 16 * (len(loads) + len(w_diag) * H) == W_LOADED

            flat = (d["fside_BxSxS2_0"].rearrange("b s k -> (b s k)").rearrange("(p n) -> p n", p=P),
                    bias_dram.rearrange("b s k -> (b s k)").rearrange("(p n) -> p n", p=P))

            def load_dist(c):
                first, size = dist_span(c)
                at_least(sp, bias_stored[c % 2], 16 * (c // 2))
                sp.dma_start(dist[:, c % 2, 0:size], flat[0][:, first:first + size]).then_inc(dist_loaded[c % 2], 16)

            load_dist(0)
            load_dist(1)
            for c in range(DIST_CHUNKS):
                first, size = dist_span(c)
                sp.wait_ge(bias_scaled, c + 1)
                sp.dma_start(flat[1][:, first:first + size], dist[:, c % 2, 0:size]).then_inc(bias_stored[c % 2], 16)
                if c + 2 < DIST_CHUNKS:
                    load_dist(c + 2)
            for s in range(2):
                sp.wait_ge(bias_stored[s], 16 * len(range(s, DIST_CHUNKS, 2)))

            def load_x(ph, n):
                s, i = n[1], number(n)
                reached(sp, ph, "x_turned", i - 1)
                sp.dma_start(x_in[:, s, :], state[:, i, :]).then_inc(dma_signal["x_loaded"][s], 16)

            def load_context(ph, n):
                s, i = n[1], number(n)
                reached(sp, ph, "v_projected", ph.chunks * (i - 1))
                sp.dma_start(ctxT[:, s, :, :], d["ctx_1024"][i].rearrange("(k p) n -> p k n", p=P))\
                    .then_inc(dma_signal["ctx_loaded"][s], 16)

            def load_bias(ph, n):
                s, i = n[1], number(n)
                reached(sp, ph, "maxed", ph.units * (i - 1))
                sp.dma_start(bias[:, s, :], bias_dram[i]).then_inc(dma_signal["bias_loaded"][s], 16)

            def stack(ph, n):
                s, i = n[1], number(n)
                arrived(sp, ph, "stacked", n, back=1, alone=True)
                reached(sp, ph, "k_split", KC * (i + 1))
                def bounce(dram, parts, n):
                    place = dram[s, 0:TERMS * D * n].rearrange("(t p n) -> p t n", t=TERMS, p=P)
                    sp.dma_start(place, parts).then_inc(dma_signal["bounced"][s], 16)
                    return dram[s, 0:TERMS * D * n].rearrange("(t f n) -> t f n", t=TERMS, f=DH)

                kb = bounce(k_bounce, k_parts[:, s, 0:TERMS * KC * ph.keys].rearrange("p (t n) -> p t n", t=TERMS), ph.keys)
                reached(sp, ph, "q_split", i + 1)
                qb = bounce(q_bounce, q_parts[:, s, :, :, :].rearrange("p t m n -> p t (m n)"), S)
                arrived(sp, ph, "bounced", n, alone=True)
                reached(sp, ph, "scores_ready", ph.units * (i - 1))
                first = 0
                for part, meets in PRODUCTS:
                    rows = slice(first * DH, (first + meets) * DH)
                    sp.dma_start(k_stack[rows, s, 0:H * ph.keys], kb[0:meets].rearrange("t f n -> (t f) n"))\
                        .then_inc(dma_signal["stacked"][s], 16)
                    sp.dma_start(q_stack[rows, s, :], qb[part:part + 1].to_broadcast([meets, DH, H * S]))\
                        .then_inc(dma_signal["stacked"][s], 16)
                    first += meets

            def attend(ph):
                def body(b):
                    if exists(later(b, 3)):
                        load_x(ph, later(b, 3))
                    if exists(later(b, 1)):
                        if ph.biased:
                            load_bias(ph, later(b, 1))
                        stack(ph, later(b, 1))
                    if ph.cross and exists(later(b, 3)):
                        load_context(ph, later(b, 3))

                over_batches(sp, body, 2)
                reached(sp, ph, "state_ready", B)

            sp.wait_ge(state_loaded, 16)
            attend(sa0)
            attend(xa0)
            sp.wait_ge(ffn["state_ready"], B)
            attend(sa1)
            attend(xa1)
            for e in range(E):
                sp.dma_start(w_up[:, e], d["L1_ffn_W1"][e].rearrange("(k p) n -> p k n", p=P)).then_inc(moe["w_loaded"], 16)
                sp.dma_start(w_down[:, e], d["L1_ffn_W2"][e].rearrange("(k p) n -> p k n", p=P)).then_inc(moe["w_loaded"], 16)
            sp.wait_ge(moe["rows_cleared"], 1)
            for bb in range(P // E):
                sp.dma_start(b_down_rows[bb * E:(bb + 1) * E, bb, :], d["L1_ffn_b2"]).then_inc(moe["rows_loaded"], 16)

            def load_for_gate(b):
                s = b[1]
                at_least(sp, moe["x_turned"], number(b) - 1)
                sp.dma_start(x_in[:, s, :], state[:, number(b), :]).then_inc(moe_x_loaded[s], 16)

            over_batches(sp, load_for_gate)

            def store(b):
                sp.wait_ge(moe["out_ready"], number(b) + 1)
                sp.dma_start(out[number(b)], y_out[:, b[1], :]).then_inc(stored[b[1]], 16)

            over_batches(sp, store)
            for s in range(2):
                sp.wait_ge(stored[s], 16 * PAIRS)

        @block.tensor
        def _(pe):
            pe.wait_ge(constants, CONSTANTS)
            pe.wait_ge(w_loaded, W_LOADED)

            for i, (bv, ph) in enumerate(value_biases):
                at_least(pe, b_out_ready, i)
                for k in range(KC):
                    mm = pe.matmul(ps_a[0:S, 0:D], bv[:, k:k + 1].to_broadcast([P, S]), ph.wo[:, k, :],
                                   start=(k == 0), stop=(k == KC - 1))
                mm.then_inc(bv_out, 1)
            pe.wait_ge(b_out_ready, len(value_biases))
            pe.wait_ge(q_scaled, Q_SCALED)

            pe.wait_ge(ffn["w_sum"], 1)
            pe.matmul(ps_b[:, 0:1], ones[:, :], w_sum[:, :], start=True, stop=True).then_inc(ffn["w_total"], 1)
            pe.wait_ge(ffn["w_mean"], 1)

            def turn_x(ph, n):
                s, i = n[1], number(n)
                arrived(pe, ph, "x_loaded", n)
                reached(pe, ph, "q_rest_ready", KC * i)
                for k in range(KC):
                    mm = pe.transpose(ps_b[:, k * S:(k + 1) * S], x_in[:, s, k * P:(k + 1) * P], ident[0:S, 0:S])
                mm.then_inc(signal["x_turned"], 1)

            def keys_of(ph, n, m):
                s, i = n[1], number(n)
                if m == 0:
                    reached(pe, ph, "xT_ready", i + 1)
                    if ph.cross:
                        arrived(pe, ph, "ctx_loaded", n)
                elif ph.cross:
                    reached(pe, ph, "k_rest_ready", KC * i + m)
                source = ctxT if ph.cross else xT
                for k in range(KC):
                    mm = pe.matmul(k_place(ph, m), ph.wk(k, m), source[:, s, k, :], start=(k == 0), stop=(k == KC - 1))
                mm.then_inc(signal["k_done"], 1)

            def queries_of(ph, n):
                s, i = n[1], number(n)
                reached(pe, ph, "k_rest_ready", KC * (i + 1))
                for m in range(KC):
                    for k in range(KC):
                        mm = pe.matmul(ps_b[:, m * S:(m + 1) * S], ph.wq(k, m), xT[:, s, k, :],
                                       start=(k == 0), stop=(k == KC - 1))
                mm.then_inc(signal["q_done"], 1)

            def values_of(ph, n, c):
                s, i = n[1], number(n)
                source = ctxT if ph.cross else xT
                first, size = ph.spans[c]
                if c == 0:
                    reached(pe, ph, "xT_ready", i + 1)
                    if ph.cross:
                        arrived(pe, ph, "ctx_loaded", n)
                    reached(pe, ph, "inv_T_ready", i - 1)
                reached(pe, ph, "v_ready", ph.chunks * i + c)
                for k in range(KC):
                    lhsT = source[:, s, k, first:first + size]
                    mm = pe.matmul(ps_a[0:size, 0:D], lhsT, ph.wv(k), start=(k == 0), stop=(k == KC - 1))
                mm.then_inc(signal["v_projected"], 1)

            def scores_of(ph, b, u):
                s, i = b[1], number(b)
                if u == 0:
                    arrived(pe, ph, "stacked", b)
                if u >= S_RING:
                    held, at = u - S_RING, i
                else:
                    held, at = max(v for v in range(ph.units) if v % S_RING == u % S_RING), i - 1
                if ph.biased:
                    reached(pe, ph, "maxed", at * ph.units + held + 1)
                else:
                    reached(pe, ph, "probs_ready", at * H + (held + 1) * ph.per_unit)
                for j in range(ph.per_unit):
                    h = u * ph.per_unit + j
                    mm = pe.matmul(ps_scores[0:S, u % S_RING, j * ph.keys:(j + 1) * ph.keys],
                                   q_stack[:, s, h * S:(h + 1) * S], k_stack[:, s, h * ph.keys:(h + 1) * ph.keys], start=True, stop=True)
                mm.then_inc(signal["scores_ready"], 1)

            def turn_probs(ph, b, g, c):
                f = g * ph.chunks + c
                first, size = ph.spans[c]
                reached(pe, ph, "probs_ready", H * number(b) + GROUP * (g + 1))
                if f >= 2:
                    wait_copied(pe, ph, b, f - 2)
                else:
                    wait_copied(pe, ph, later(b, -1), ph.fills + f - 2)
                for j in range(GROUP):
                    mm = pe.transpose(ps_probs[0:size, f % 2, j * S:(j + 1) * S],
                                      probs[:, (g * GROUP + j) % P_RING, first:first + size], ident[0:S, 0:S])
                mm.then_inc(signal["probs_turned"], 1)

            def sum_heads(ph, b, half):
                s, i = b[1], number(b)
                last = (half + 1) * ph.fills // 2 - 1
                for dve in (False, True):
                    if dve in ph.by_dve:
                        reached(pe, ph, "dve_copied" if dve else "act_copied", copies(ph, b, last, dve))
                if half == 0:
                    reached(pe, ph, "v_ready", ph.chunks * (i + 1))
                    reached(pe, ph, "heads_scaled", i)
                for c, (first, size) in enumerate(ph.spans):
                    for j in range(4):
                        at = (4 * half + j) * 2 * DH
                        mm = pe.matmul(ps_heads[32 * j:32 * j + 32, half * 2 * S:(half + 1) * 2 * S],
                                       values[0:size, s, c, at:at + 2 * DH], probs_T[0:size, half, c, 2 * j:2 * j + 2, :],
                                       start=(c == 0), stop=(c == ph.chunks - 1))
                mm.then_inc(signal["heads_summed"], 1)

            def turn_inv(ph, b):
                i = number(b)
                reached(pe, ph, "inv_wide_ready", 2 * (i + 1))
                reached(pe, ph, "y_ready", i)
                reached(pe, ph, "v_ready", no_more(ph.chunks * (i + 2), ph.chunks * B))
                for j in range(4):
                    mm = pe.transpose(ps_a[:, j * S:(j + 1) * S], inv_wide[:, j // 2, j % 2, :], ident[0:S, 0:S])
                mm.then_inc(signal["inv_turned"], 1)

            def project(ph, b):
                i = number(b)
                reached(pe, ph, "heads_ready", i + 1)
                reached(pe, ph, "v_ready", no_more(ph.chunks * (i + 3), ph.chunks * B))
                for k in range(KC):
                    mm = pe.matmul(ps_a[0:S, 0:D], heads_T[:, k, :], ph.wo[:, k, :], start=(k == 0), stop=(k == KC - 1))
                mm.then_inc(signal["out_projected"], 1)

            def attend(ph):
                def step(b, h):
                    for n, u in due(ph, "scores", b, h):
                        scores_of(ph, n, u)
                    for n, f in due(ph, "turn_probs", b, h):
                        turn_probs(ph, n, f // ph.chunks, f % ph.chunks)
                    for n, _ in due(ph, "turn_inv", b, h):
                        turn_inv(ph, n)
                    for n, half in due(ph, "sum_heads", b, h):
                        sum_heads(ph, n, half)
                    for n, c in due(ph, "values", b, h):
                        values_of(ph, n, c)
                    for n, _ in due(ph, "turn_x", b, h):
                        turn_x(ph, n)
                    for n, m in due(ph, "keys", b, h):
                        keys_of(ph, n, m)
                    for n, _ in due(ph, "queries", b, h):
                        queries_of(ph, n)
                    for n, _ in due(ph, "project", b, h):
                        project(ph, n)

                rounds(pe, ph, step)
                reached(pe, ph, "state_ready", B)

            attend(sa0)
            attend(xa0)

            pe.wait_ge(ffn["row_max"], 1)
            pe.transpose(ps_a[0:1, 0:S], row_max[:, :], ident[0:S, 0:S]).then_inc(ffn["max_turned"], 1)
            pe.wait_ge(ffn["max_one"], 1)
            pe.matmul(ps_a[0:S, 0:1], ones[0:1, 0:S], max_one[:, :], start=True, stop=True).then_inc(ffn["max_spread"], 1)
            pe.wait_ge(ffn["w_ready"], 1)

            def ffn_turn(b):
                s, i = b[1], number(b)
                pe.wait_ge(ffn["xq_scaled"], i + 1)
                at_least(pe, ffn["xqT_ready"], i - 1)
                for k in range(KC):
                    mm = pe.transpose(ps_probs[:, s, k * S:(k + 1) * S], xq[:, s, k * P:(k + 1) * P], ident[0:S, 0:S])
                mm.then_inc(ffn["xq_turned"], 1)

            def ffn_project(b):
                s, i = b[1], number(b)
                pe.wait_ge(ffn["xqT_ready"], i + 1)
                at_least(pe, ffn["y_ready"], i - 1)
                for k in range(KC):
                    mm = pe.matmul(ps_scores[0:S, s, 0:D], xqT[:, s, k, :], w["L0_ffn_weight"][:, k, :],
                                   start=(k == 0), stop=(k == KC - 1))
                mm.then_inc(ffn["projected"], 1)

            def ffn_step(b, h):
                for n, _ in due(ffn_work, "turn", b, h):
                    ffn_turn(n)
                for n, _ in due(ffn_work, "project", b, h):
                    ffn_project(n)

            rounds(pe, ffn_work, ffn_step)
            pe.wait_ge(ffn["state_ready"], B)
            attend(sa1)
            attend(xa1)

            def gate_turn(b):
                s, i = b[1], number(b)
                pe.wait_ge(moe_x_loaded[s], 16 * (b[0] + 1))
                at_least(pe, moe["xT_ready"], i - 1)
                for k in range(KC):
                    mm = pe.transpose(ps_probs[:, s, k * S:(k + 1) * S], x_in[:, s, k * P:(k + 1) * P], ident[0:S, 0:S])
                mm.then_inc(moe["x_turned"], 1)

            gate_turn(FIRST)

            def gate(b):
                s, i = b[1], number(b)
                if exists(later(b, 1)):
                    gate_turn(later(b, 1))
                pe.wait_ge(moe["xT_ready"], i + 1)
                at_least(pe, moe["logits_ready"], i - 1)
                for k in range(KC):
                    pe.matmul(ps_scores[0:S, s, 0:E], xT[:, s, k, :], w_gate[:, k, :], start=(k == 0), stop=False)
                pe.matmul(ps_scores[0:S, s, 0:E], ones[0:1, 0:S], b_gate[:, :], start=False, stop=True)\
                    .then_inc(moe["gated"], 1)

            over_batches(pe, gate)

            pe.wait_ge(moe["hot_ready"], 1)
            for half in range(2):
                mm = pe.transpose(ps_a[:, half * S:(half + 1) * S],
                                  hot[:, half * (B // 2):(half + 1) * (B // 2), :].rearrange("p b e -> p (b e)"),
                                  ident[0:S, 0:S])
            mm.then_inc(moe["hot_turned"], 1)
            pe.wait_ge(moe["hot_T_ready"], 1)
            pe.wait_ge(moe["rows_loaded"], 16 * (P // E))

            def second_bias(bb):
                for half in range(2):
                    at_least(pe, moe["b_down_added"], 2 * bb + half - 1)
                    pe.matmul(ps_scores[0:S, half, 0:D], hot_T[:, half, :], b_down_rows[:, bb, :], start=True, stop=True)\
                        .then_inc(moe["b_down_done"], 1)

            second_bias(0)
            with pe.Fori(1, B // 2) as bb:
                second_bias(bb)
            pe.wait_ge(moe["b_down_added"], B)
            pe.wait_ge(moe["w_loaded"], 2 * 16 * E)
            pe.wait_ge(moe["xT_kept"], B)

            def up(q, e):
                for m in range(KC):
                    at_least(pe, moe["gelu_done"], KC * (E * q + e) + m - 1)
                    for k in range(KC):
                        mm = pe.matmul(ps_scores[:, m, 0:MB * S], w_up[:, e, k, m * P:(m + 1) * P],
                                       xT_all[:, k, bass.ds(q * (MB * S), MB * S)], start=(k == 0), stop=(k == KC - 1))
                    mm.then_inc(moe["up_done"], 1)

            def down(q, e):
                pe.wait_ge(moe["gelu_done"], KC * (E * q + e + 1))
                for j in range(MB):
                    at_least(pe, moe["added"], MB * (E * q + e) + j - 1)
                    for m in range(KC):
                        mm = pe.matmul(ps_probs[0:S, j % 2, 0:D], gelu_T[:, e % 2, m, j * S:(j + 1) * S],
                                       w_down[:, e, m, :], start=(m == 0), stop=(m == KC - 1))
                    mm.then_inc(moe["down_done"], 1)

            def experts(q):
                up(q, 0)
                for e in range(E):
                    if e + 1 < E:
                        up(q, e + 1)
                    down(q, e)

            experts(0)
            with pe.Fori(1, B // MB) as q:
                experts(q)

        @block.scalar
        def _(act):
            def copy_xT(ph, n):
                s, i = n[1], number(n)
                reached(act, ph, "x_turned", i + 1)
                reached(act, ph, "q_done", i - 1)
                if not ph.cross:
                    reached(act, ph, "v_projected", ph.chunks * (i - 1))
                act.activation(xT[:, s, :, :], ps_b[:, 0:KC * S].rearrange("p (k t) -> p k t", k=KC), ACT.Copy)\
                    .then_inc(signal["xT_ready"], 1)

            def round_keys(ph, n, m):
                s, i = n[1], number(n)
                if m == 0:
                    arrived(act, ph, "bounced", n, back=1)
                reached(act, ph, "k_done", KC * i + m + 1 if ph.cross else KC * (i + 1))
                act.activation(k_part(ph, s, 0, m), k_place(ph, m), ACT.Identity, bias=ph.bk[:, m:m + 1])\
                    .then_inc(signal["k_rounded"], 1)

            def round_queries(ph, n):
                s, i = n[1], number(n)
                reached(act, ph, "q_done", i + 1)
                for m in range(KC):
                    act.activation(q_parts[:, s, 0, m, :], ps_b[:, m * S:(m + 1) * S], ACT.Identity, bias=ph.bq[:, m:m + 1])\
                        .then_inc(signal["q_rounded"], 1)

            def copy_values(ph, n, c):
                s, i = n[1], number(n)
                first, size = ph.spans[c]
                reached(act, ph, "v_projected", ph.chunks * i + c + 1)
                reached(act, ph, "heads_summed", 2 * (i - 1))
                act.activation(values[0:size, s, c, :], ps_a[0:size, 0:D], ACT.Copy).then_inc(signal["v_ready"], 1)

            def exponentiate(ph, b, h):
                s, i = b[1], number(b)
                u, j = divmod(h, ph.per_unit)
                reached(act, ph, "maxed", ph.units * i + u + 1)
                if h % GROUP == 0:
                    if h >= P_RING:
                        reached(act, ph, "probs_turned", ph.fills * i + ph.chunks * ((h - P_RING) // GROUP + 1))
                    else:
                        reached(act, ph, "probs_turned", ph.fills * (i - 1) + ph.chunks * ((h + P_RING) // GROUP + 1))
                if ph.biased:
                    source, sign = biased[:, h % SB_RING, :], -1.0
                else:
                    source, sign = ps_scores[0:S, u % S_RING, j * ph.keys:(j + 1) * ph.keys], 1.0
                act.activation(probs[:, h % P_RING, 0:ph.keys], source, ACT.Exp, bias=neg_max[:, s, h:h + 1], scale=sign,
                               accum_out=sums[:, s, h:h + 1]).then_inc(signal["probs_ready"], 1)

            def copy_probs(ph, b, g, c):
                f, half = g * ph.chunks + c, g // 2
                first, size = ph.spans[c]
                if ph.by_dve[f]:
                    return
                reached(act, ph, "probs_turned", ph.fills * number(b) + f + 1)
                reached(act, ph, "heads_summed", 2 * (number(b) - 1) + half + 1)
                act.activation(probs_T[0:size, half, c, (g % 2) * GROUP:(g % 2 + 1) * GROUP, :],
                               ps_probs[0:size, f % 2, 0:GROUP * S].rearrange("p (h t) -> p h t", h=GROUP), ACT.Copy)\
                    .then_inc(signal["act_copied"], 1)

            def copy_inv(ph, b):
                reached(act, ph, "inv_turned", number(b) + 1)
                reached(act, ph, "heads_scaled", number(b))
                act.activation(inv_T[:, :], ps_a[:, 0:4 * S], ACT.Copy).then_inc(signal["inv_T_ready"], 1)

            def attend(ph):
                def step(b, h):
                    for n, f in due(ph, "copy_probs", b, h):
                        copy_probs(ph, n, f // ph.chunks, f % ph.chunks)
                    for n, _ in due(ph, "copy_inv", b, h):
                        copy_inv(ph, n)
                    for n, c in due(ph, "copy_values", b, h):
                        copy_values(ph, n, c)
                    for n, _ in due(ph, "copy_xT", b, h):
                        copy_xT(ph, n)
                    for n, m in due(ph, "round_keys", b, h):
                        round_keys(ph, n, m)
                    for n, _ in due(ph, "round_queries", b, h):
                        round_queries(ph, n)
                    for n, head in due(ph, "exponentiate", b, h):
                        exponentiate(ph, n, head)

                rounds(act, ph, step)

            act.wait_ge(constants, CONSTANTS)
            for c in range(DIST_CHUNKS):
                first, size = dist_span(c)
                act.wait_ge(dist_loaded[c % 2], 16 * (c // 2 + 1))
                act.activation(dist[:, c % 2, 0:size], dist[:, c % 2, 0:size], ACT.Ln, bias=tiny[:, :]).then_inc(logs_ready, 1)
            act.wait_ge(w_loaded, W_LOADED)
            act.wait_ge(q_scaled, Q_SCALED)
            attend(sa0)
            attend(xa0)

            def ffn_scale(b):
                s, i = b[1], number(b)
                at_least(act, ffn["xq_turned"], i - 1)
                act.activation(xq[:, s, :], xn[:, i, :], ACT.Copy, scale=gamma[:, 2:3]).then_inc(ffn["xq_scaled"], 1)

            def ffn_step(b, h):
                for n, _ in due(ffn_work, "scale", b, h):
                    ffn_scale(n)

            act.wait_ge(ffn["gamma_inverse"], 2)
            rounds(act, ffn_work, ffn_step)
            attend(sa1)
            attend(xa1)

            def gate_copy(b):
                s, i = b[1], number(b)
                act.wait_ge(moe["x_turned"], i + 1)
                at_least(act, moe["gated"], i - 1)
                at_least(act, moe["xT_kept"], i - 1)
                act.activation(xT[:, s, :, :], ps_probs[:, s, 0:KC * S].rearrange("p (k t) -> p k t", k=KC), ACT.Copy)\
                    .then_inc(moe["xT_ready"], 1)

            over_batches(act, gate_copy)
            act.wait_ge(moe["shifted"], 1)
            act.activation(exps[:, :, :], shifted[:, :, :], ACT.Exp).then_inc(moe["exp_ready"], 1)

            def gelu(q):
                for e in range(E):
                    for m in range(KC):
                        act.wait_ge(moe["up_done"], KC * (E * q + e) + m + 1)
                        at_least(act, moe["down_done"], MB * (E * q + e - 1))
                        act.activation(gelu_T[:, e % 2, m, :], ps_scores[:, m, 0:MB * S], ACT.Gelu, bias=b_up[:, e, m:m + 1])\
                            .then_inc(moe["gelu_done"], 1)

            gelu(0)
            with act.Fori(1, B // MB) as q:
                gelu(q)

        @block.vector
        def _(dve):
            dve.wait_ge(w_loaded, W_LOADED)
            dve.wait_ge(constants, CONSTANTS)
            for n in ("L1_attn_Wq", "L1_attn_Wk"):
                for k in range(KC):
                    for m in range(KC):
                        dve.tensor_copy(w_diag[n][:, k, m * P:(m + 1) * P].rearrange("p (f h) -> p f h", f=DH),
                                        on_diagonal[n][:, k, :].rearrange("p (h r f) -> p r f h", r=KC, f=DH)[:, m])\
                            .then_inc(columns_ordered, 1)
            dve.wait_ge(columns_ordered, 2 * KC * KC)
            scaled = [ph.q_scale for ph in phases] + [(ph.bq[:, :], ph.q_scale[1]) for ph in (sa0, xa0, xa1)]
            for tile, scale in scaled:
                dve.tensor_scalar(tile, tile, float(scale), None, ALU.mult).then_inc(q_scaled, 1)
            assert len(scaled) == Q_SCALED
            dve.scalar_tensor_tensor(neg_abs_ds[:, :], scaling[:, :], -1.0, scaling[:, :], ALU.mult, ALU.min).then_inc(ds_ready, 1)
            dve.wait_ge(ds_ready, 1)
            for c in range(DIST_CHUNKS):
                first, size = dist_span(c)
                dve.wait_ge(logs_ready, c + 1)
                dve.tensor_scalar(dist[:, c % 2, 0:size], dist[:, c % 2, 0:size], neg_abs_ds[:, :], None, ALU.mult)\
                    .then_inc(bias_scaled, 1)
            for i, (bv, ph) in enumerate(value_biases):
                dve.wait_ge(bv_out, i + 1)
                dve.tensor_tensor(ph.bo[:, :], ph.bo[:, :], ps_a[0:S, 0:D], ALU.add).then_inc(b_out_ready, 1)

            wf = w["L0_ffn_weight"][:, :, :].rearrange("p k n -> p (k n)")
            wt = w_tmp[:, :, :].rearrange("p k n -> p (k n)")
            dve.tensor_reduce(w_sum[:, :], wf, AX.X, ALU.add, apply_absolute_value=True).then_inc(ffn["w_sum"], 1)
            dve.wait_ge(ffn["w_total"], 1)
            dve.tensor_scalar(w_beta[:, 0:1], ps_b[:, 0:1], 1.0 / (D * D), None, ALU.mult).then_inc(ffn["w_mean"], 1)
            dve.wait_ge(ffn["w_mean"], 1)
            dve.tensor_scalar(w_beta[:, 1:2], w_beta[:, 0:1], FFN_EPS, None, ALU.add).then_inc(ffn["w_beta"], 1)
            dve.wait_ge(ffn["w_beta"], 1)
            dve.reciprocal(w_beta[:, 2:3], w_beta[:, 1:2]).then_inc(ffn["w_inverse"], 1)
            dve.wait_ge(ffn["w_inverse"], 1)
            dve.tensor_scalar(wt, wf, w_beta[:, 2:3], None, ALU.mult).then_inc(ffn["w_scaled"], 1)
            dve.wait_ge(ffn["w_scaled"], 1)
            dve.tensor_scalar(wf, wt, ROUND, -ROUND, ALU.add, ALU.add).then_inc(ffn["w_rounded"], 1)
            dve.wait_ge(ffn["w_rounded"], 1)
            dve.tensor_scalar(wf, wf, -1.0, 1.0, ALU.max, ALU.min).then_inc(ffn["w_ready"], 1)

            def state_stats(b, stats_ready, aggregated):
                apart(dve, aggregated, b)
                dve.bn_stats(state_stats_of[:, :], state[:, b, :]).then_inc(stats_ready, 1)

            def state_moments(b, stats_ready, aggregated, kept):
                at_least(dve, kept, b)
                apart(dve, stats_ready, b + 1)
                dve.bn_aggr(state_moments_of[:, :], state_stats_of[:, :]).then_inc(aggregated, 1)

            def keep_moments(b, aggregated, kept):
                dve.wait_ge(aggregated, b + 1)
                dve.tensor_scalar(all_moments[:, b, :], state_moments_of[:, :], 1.0, None, ALU.mult).then_inc(kept, 1)

            def maximum(ph, b, u):
                s, i = b[1], number(b)
                if ph.biased:
                    if u == 0:
                        arrived(dve, ph, "bias_loaded", b)
                    reached(dve, ph, "probs_ready", H * i + u - SB_RING + 1)
                reached(dve, ph, "scores_ready", ph.units * i + u + 1, alone=ph.biased)
                if ph.biased:
                    dve.tensor_tensor_reduce(biased[:, u % SB_RING, :], ps_scores[0:S, u % S_RING, 0:ph.keys], bias[:, s, :],
                                             -1.0, 3.0e38, ALU.add, ALU.min, neg_max[:, s, u:u + 1])\
                        .then_inc(signal["maxed"], 1)
                else:
                    dve.tensor_reduce(neg_max[:, s, u * ph.per_unit:(u + 1) * ph.per_unit],
                                      ps_scores[0:S, u % S_RING, 0:ph.per_unit * ph.keys]
                                      .rearrange("p (h k) -> p h k", h=ph.per_unit),
                                      AX.X, ALU.max, negate=True).then_inc(signal["maxed"], 1)

            def copy_probs(ph, b, g, c):
                f, half = g * ph.chunks + c, g // 2
                first, size = ph.spans[c]
                if not ph.by_dve[f]:
                    return
                reached(dve, ph, "probs_turned", ph.fills * number(b) + f + 1)
                reached(dve, ph, "heads_summed", 2 * (number(b) - 1) + half + 1)
                dve.tensor_copy(probs_T[0:size, half, c, (g % 2) * GROUP:(g % 2 + 1) * GROUP, :],
                                ps_probs[0:size, f % 2, 0:GROUP * S].rearrange("p (h t) -> p h t", h=GROUP))\
                    .then_inc(signal["dve_copied"], 1)

            def rest_of_keys(ph, n, m):
                s, i = n[1], number(n)
                reached(dve, ph, "k_rounded", KC * i + m + 1 if ph.cross else KC * (i + 1))
                reached(dve, ph, "k_split", KC * (i - 1) + m + 1)
                dve.scalar_tensor_tensor(k_rest[:, m, 0:ph.keys], k_place(ph, m), ph.bk[:, m:m + 1],
                                         k_part(ph, s, 0, m), ALU.add, ALU.subtract)\
                    .then_inc(signal["k_rest_ready"], 1)
                reached(dve, ph, "k_rest_ready", KC * i + m + 1)
                dve.tensor_copy(k_part(ph, s, 1, m), k_rest[:, m, 0:ph.keys]).then_inc(signal["k_second"], 1)

            def rest_of_queries(ph, n):
                s, i = n[1], number(n)
                reached(dve, ph, "q_split", i)
                reached(dve, ph, "q_rounded", KC * (i + 1))
                for m in range(KC):
                    dve.scalar_tensor_tensor(q_rest[:, m, :], ps_b[:, m * S:(m + 1) * S], ph.bq[:, m:m + 1],
                                             q_parts[:, s, 0, m, :], ALU.add, ALU.subtract)\
                        .then_inc(signal["q_rest_ready"], 1)
                reached(dve, ph, "q_rest_ready", KC * (i + 1))
                dve.tensor_copy(q_parts[:, s, 1, :, :], q_rest[:, :, :]).then_inc(signal["q_second"], 1)

            def invert(ph, b):
                s, i = b[1], number(b)
                reached(dve, ph, "probs_ready", H * (i + 1))
                dve.reciprocal(inv[:, :], sums[:, s, :]).then_inc(signal["inv_ready"], 1)
                reached(dve, ph, "inv_ready", i + 1)
                reached(dve, ph, "inv_turned", i)
                for parity in range(2):
                    rows = inv_wide[:, :, parity, :].rearrange("p a (j r f) -> p a j r f", j=4, r=2)[:, :, :, parity, :]
                    by_head = inv[:, :].rearrange("p (a j r) -> p a j r", a=2, j=4)[:, :, :, parity:parity + 1]
                    dve.tensor_copy(rows, by_head.to_broadcast([S, 2, 4, DH])).then_inc(signal["inv_wide_ready"], 1)

            def scale_heads(ph, b):
                i = number(b)
                reached(dve, ph, "heads_summed", 2 * (i + 1))
                reached(dve, ph, "inv_T_ready", i + 1)
                reached(dve, ph, "heads_ready", i)
                wide = heads_par[:, :, :, :].rearrange("p a r t -> p (a r t)")
                dve.tensor_tensor(wide, ps_heads[:, 0:4 * S], inv_T[:, :], ALU.mult).then_inc(signal["heads_scaled"], 1)
                reached(dve, ph, "heads_scaled", i + 1)
                reached(dve, ph, "out_projected", i)
                dve.tensor_tensor(heads_T[:, :, :], heads_par[:, :, 0, :], heads_par[:, :, 1, :], ALU.add)\
                    .then_inc(signal["heads_ready"], 1)

            def add_residual(ph, b):
                s, i = b[1], number(b)
                reached(dve, ph, "out_projected", i + 1)
                reached(dve, ph, "residual_ready", i + 1)
                reached(dve, ph, "state_ready", i)
                dve.tensor_tensor(y[:, :], ps_a[0:S, 0:D], x_res[:, s, :], ALU.add).then_inc(signal["y_ready"], 1)

            def take_stats(ph, b):
                reached(dve, ph, "y_ready", number(b) + 1)
                dve.bn_stats(stats[:, :], y[:, :]).then_inc(signal["stats_ready"], 1)

            def take_moments(ph, b):
                reached(dve, ph, "stats_ready", number(b) + 1, alone=True)
                dve.bn_aggr(moments[:, :], stats[:, :]).then_inc(signal["moments_ready"], 1)

            def guess_root(ph, b):
                i = number(b)
                reached(dve, ph, "moments_ready", i + 1)
                reached(dve, ph, "root_step", ROOT_STEPS * i)
                dve.tensor_scalar(root_in[:, :], moments[:, 1:2], LN_EPS, None, ALU.add).then_inc(signal["root_in_ready"], 1)
                reached(dve, ph, "root_in_ready", i + 1)
                dve.tensor_scalar(rstd[:, :].bitcast(I32), root_in[:, :].bitcast(I32), -0.5, ROOT_GUESS, ALU.mult, ALU.add)\
                    .then_inc(signal["guess_ready"], 1)

            def norm(ph, b):
                i = number(b)
                reached(dve, ph, "root_step", ROOT_STEPS * (i + 1))
                dve.tensor_scalar(state[:, i, :], y[:, :], moments[:, 0:1], rstd[:, :], ALU.subtract, ALU.mult)\
                    .then_inc(signal["state_ready"], 1)

            def attend(ph):
                def step(b, h):
                    for n, u in due(ph, "maximum", b, h):
                        maximum(ph, n, u)
                    for n, f in due(ph, "copy_probs", b, h):
                        copy_probs(ph, n, f // ph.chunks, f % ph.chunks)
                    for n, _ in due(ph, "invert", b, h):
                        invert(ph, n)
                    for n, _ in due(ph, "scale_heads", b, h):
                        scale_heads(ph, n)
                    for n, m in due(ph, "rest_of_keys", b, h):
                        rest_of_keys(ph, n, m)
                    for n, _ in due(ph, "rest_of_queries", b, h):
                        rest_of_queries(ph, n)
                    for n, _ in due(ph, "add_residual", b, h):
                        add_residual(ph, n)
                    for n, _ in due(ph, "take_stats", b, h):
                        take_stats(ph, n)
                    for n, _ in due(ph, "take_moments", b, h):
                        take_moments(ph, n)
                    for n, _ in due(ph, "guess_root", b, h):
                        guess_root(ph, n)
                    for n, _ in due(ph, "norm", b, h):
                        norm(ph, n)
                    for n, _ in due(ph, "next_stats", b, h):
                        reached(dve, ph, "state_ready", number(n) + 1)
                        state_stats(number(n), ffn["x_stats"], ffn["x_aggregated"])
                    for n, _ in due(ph, "next_moments", b, h):
                        state_moments(number(n), ffn["x_stats"], ffn["x_aggregated"], ffn["x_moments"])
                    for n, _ in due(ph, "keep_moments", b, h):
                        keep_moments(number(n), ffn["x_aggregated"], ffn["x_moments"])

                rounds(dve, ph, step)

            def guess(root_in_ready, count, guess_ready, variance, eps, value, result):
                dve.tensor_scalar(value, variance, eps, None, ALU.add).then_inc(root_in_ready, 1)
                dve.wait_ge(root_in_ready, count)
                dve.tensor_scalar(result.bitcast(I32), value.bitcast(I32), -0.5, ROOT_GUESS, ALU.mult, ALU.add)\
                    .then_inc(guess_ready, 1)

            attend(sa0)
            attend(xa0)

            reached(dve, xa0, "state_ready", B)

            dve.wait_ge(ffn["x_moments"], B)
            guess(ffn["x_root_in"], 1, ffn["x_guess"], all_moments[:, :, 1], FFN_LN_EPS, all_root_in[:, :], all_rstd[:, :])
            dve.wait_ge(ffn["x_root_step"], ROOT_STEPS)

            def center(b):
                dve.scalar_tensor_tensor(xn[:, b, :], state[:, b, :], all_moments[:, b, 0:1], ffn_gamma[:, :], ALU.subtract,
                                         ALU.mult).then_inc(ffn["gained"], 1)

            def normalise(b):
                dve.wait_ge(ffn["gained"], b + 1)
                dve.scalar_tensor_tensor(xn[:, b, :], xn[:, b, :], all_rstd[:, bass.ds(b, 1)], ffn_beta[:, :], ALU.mult,
                                         ALU.add).then_inc(ffn["xn_ready"], 1)

            with dve.Fori(0, B // 4) as quad:
                for j in range(4):
                    center(quad * 4 + j)
                for j in range(4):
                    normalise(quad * 4 + j)
            dve.wait_ge(ffn["xn_ready"], B)
            dve.tensor_reduce(row_max[:, :], xn.rearrange("p b d -> p (b d)"), AX.X, ALU.max, apply_absolute_value=True)\
                .then_inc(ffn["row_max"], 1)
            dve.wait_ge(ffn["max_turned"], 1)
            dve.tensor_reduce(max_one[:, :], ps_a[0:1, 0:S], AX.X, ALU.max).then_inc(ffn["max_one"], 1)
            dve.wait_ge(ffn["max_spread"], 1)
            dve.tensor_copy(gamma[:, 0:1], ps_a[0:S, 0:1]).then_inc(ffn["gamma_ready"], 1)
            dve.wait_ge(ffn["gamma_ready"], 1)
            dve.reciprocal(gamma[:, 1:2], gamma[:, 0:1]).then_inc(ffn["gamma_inverse"], 1)
            dve.wait_ge(ffn["gamma_inverse"], 1)
            dve.tensor_scalar(gamma[:, 2:3], gamma[:, 1:2], QB, None, ALU.mult).then_inc(ffn["gamma_inverse"], 1)
            dve.tensor_scalar(gain[:, 0:1], gamma[:, 0:1], w_beta[0:S, 0:1], 1.0 / QB, ALU.mult, ALU.mult)\
                .then_inc(ffn["gain_ready"], 1)
            dve.wait_ge(ffn["gain_ready"], 1)
            dve.wait_ge(ffn["gamma_inverse"], 1)

            def ffn_clip(b):
                s, i = b[1], number(b)
                dve.wait_ge(ffn["xq_turned"], i + 1)
                at_least(dve, ffn["projected"], i - 1)
                dve.tensor_scalar(xqT[:, s, :, :], ps_probs[:, s, 0:KC * S].rearrange("p (k t) -> p k t", k=KC),
                                  -QB + FFN_EPS, QB - FFN_EPS, ALU.max, ALU.min).then_inc(ffn["xqT_ready"], 1)

            def ffn_add(b):
                s, i = b[1], number(b)
                dve.wait_ge(ffn["projected"], i + 1)
                dve.scalar_tensor_tensor(state[:, i, :], ps_scores[0:S, s, 0:D], gain[:, 0:1], state[:, i, :], ALU.mult, ALU.add)\
                    .then_inc(ffn["y_ready"], 1)

            def ffn_step(b, h):
                for n, _ in due(ffn_work, "clip", b, h):
                    ffn_clip(n)
                for n, _ in due(ffn_work, "add", b, h):
                    ffn_add(n)
                for n, _ in due(ffn_work, "take_stats", b, h):
                    dve.wait_ge(ffn["y_ready"], number(n) + 1)
                    state_stats(number(n), ffn["y_stats"], ffn["y_aggregated"])
                for n, _ in due(ffn_work, "take_moments", b, h):
                    state_moments(number(n), ffn["y_stats"], ffn["y_aggregated"], ffn["y_moments"])
                for n, _ in due(ffn_work, "keep_moments", b, h):
                    keep_moments(number(n), ffn["y_aggregated"], ffn["y_moments"])

            rounds(dve, ffn_work, ffn_step)
            dve.wait_ge(ffn["y_moments"], B)
            guess(ffn["y_root_in"], 1, ffn["y_guess"], all_moments[:, :, 1], LN_EPS, all_root_in[:, :], all_rstd[:, :])
            dve.wait_ge(ffn["y_root_step"], ROOT_STEPS)

            def ffn_out(b):
                dve.tensor_scalar(state[:, b, :], state[:, b, :], all_moments[:, b, 0:1], all_rstd[:, bass.ds(b, 1)],
                                  ALU.subtract, ALU.mult).then_inc(ffn["state_ready"], 1)

            with dve.Fori(0, B) as b:
                ffn_out(b)
            attend(sa1)
            attend(xa1)

            def keep_logits(b):
                s, i = b[1], number(b)
                dve.wait_ge(moe["gated"], i + 1)
                dve.tensor_copy(logits[:, i, :], ps_scores[0:S, s, 0:E]).then_inc(moe["logits_ready"], 1)

            over_batches(dve, keep_logits)

            def per_token(t):
                return t[:, :].rearrange("p (b a) -> p b a", a=1).to_broadcast([S, B, E])

            dve.wait_ge(moe["logits_ready"], B)
            dve.tensor_reduce(top[:, :], logits[:, :, :], AX.X, ALU.max).then_inc(moe["top_ready"], 1)
            dve.wait_ge(moe["top_ready"], 1)
            dve.tensor_tensor(shifted[:, :, :], logits[:, :, :], per_token(top), ALU.subtract).then_inc(moe["shifted"], 1)
            dve.tensor_tensor(rank[:, :, :], logits[:, :, :], per_token(top), ALU.is_ge).then_inc(moe["top_found"], 1)
            dve.wait_ge(moe["exp_ready"], 1)
            dve.tensor_reduce(top_weight[:, :], exps[:, :, :], AX.X, ALU.add).then_inc(moe["sum_ready"], 1)
            dve.wait_ge(moe["top_found"], 1)
            by_expert = rank_of[:, :].rearrange("p (a e) -> p a e", a=1).to_broadcast([S, B, E])
            dve.tensor_tensor(hot[:, :, :], rank[:, :, :], by_expert, ALU.mult).then_inc(moe["rank_ready"], 1)
            dve.wait_ge(moe["sum_ready"], 1)
            dve.reciprocal(top_weight[:, :], top_weight[:, :]).then_inc(moe["weight_ready"], 1)
            dve.wait_ge(moe["rank_ready"], 1)
            dve.tensor_reduce(top[:, :], hot[:, :, :], AX.X, ALU.max).then_inc(moe["first_ready"], 1)
            dve.wait_ge(moe["first_ready"], 1)
            dve.tensor_tensor(rank[:, :, :], hot[:, :, :], per_token(top), ALU.is_equal).then_inc(moe["hot_found"], 1)
            dve.wait_ge(moe["hot_found"], 1)
            dve.wait_ge(moe["weight_ready"], 1)
            dve.tensor_tensor(hot[:, :, :], rank[:, :, :], per_token(top_weight), ALU.mult).then_inc(moe["hot_ready"], 1)
            dve.wait_ge(moe["hot_turned"], 1)
            dve.tensor_copy(hot_T[:, :, :], ps_a[:, 0:2 * S].rearrange("p (a t) -> p a t", a=2)).then_inc(moe["hot_T_ready"], 1)

            def add_second_bias(bb):
                for half in range(2):
                    at = half * (B // 2) + bb
                    dve.wait_ge(moe["b_down_done"], 2 * bb + half + 1)
                    dve.tensor_tensor(state[:, at, :], state[:, at, :], ps_scores[0:S, half, 0:D], ALU.add)\
                        .then_inc(moe["b_down_added"], 1)

            with dve.Fori(0, B // 2) as bb:
                add_second_bias(bb)
            dve.wait_ge(moe["b_down_added"], B)

            def add_experts(q):
                for e in range(E):
                    for j in range(MB):
                        at = q * MB + j
                        dve.wait_ge(moe["down_done"], MB * (E * q + e) + j + 1)
                        at_least(dve, moe["added"], MB * (E * q + e) + j + 1 - MB)
                        dve.scalar_tensor_tensor(state[:, at, :], ps_probs[0:S, j % 2, 0:D], hot[:, at, e:e + 1],
                                                 state[:, at, :], ALU.mult, ALU.add).then_inc(moe["added"], 1)
                for j in range(MB):
                    at = q * MB + j
                    dve.wait_ge(moe["added"], MB * E * (q + 1) - MB + j + 1)
                    state_stats(at, moe["y_stats"], moe["y_aggregated"])
                    state_moments(at, moe["y_stats"], moe["y_aggregated"], moe["y_moments"])
                    keep_moments(at, moe["y_aggregated"], moe["y_moments"])

            def start_root(q):
                dve.wait_ge(moe["y_moments"], MB * (q + 1))
                at_least(dve, moe["out_ready"], MB * q)
                guess(moe["y_root_in"], q + 1, moe["y_guess"], all_moments[:, bass.ds(q * MB, MB), 1], LN_EPS,
                      all_root_in[:, 0:MB], all_rstd[:, 0:MB])

            def norm_out(q):
                dve.wait_ge(moe["y_root_step"], ROOT_STEPS * (q + 1))
                for j in range(MB):
                    at = q * MB + j
                    at_least(dve, stored[j % 2], 16 * (q * (MB // 2) + j // 2))
                    dve.tensor_scalar(y_out[:, j % 2, :], state[:, at, :], all_moments[:, at, 0:1], all_rstd[:, j:j + 1],
                                      ALU.subtract, ALU.mult).then_inc(moe["out_ready"], 1)

            add_experts(0)
            start_root(0)
            with dve.Fori(1, B // MB) as q:
                add_experts(q)
                norm_out(q - 1)
                start_root(q)
            norm_out(B // MB - 1)

        @block.gpsimd
        def _(pool):
            for t in on_diagonal.values():
                pool.memset(t[:, :, :], 0.0).then_inc(diag_cleared, 1)
            pool.memset(ident[:, :], 0.0).then_inc(constants, 1)
            pool.memset(ones[:, :], 1.0).then_inc(constants, 1)
            pool.memset(b_zero[:, :], 0.0).then_inc(constants, 1)
            pool.memset(tiny[:, :], 1e-9).then_inc(constants, 1)
            pool.memset(inv_wide[:, :, :, :], 0.0).then_inc(constants, 1)
            for e in range(E):
                pool.memset(rank_of[:, e:e + 1], float(E - e)).then_inc(constants, 1)
            pool.wait_ge(constants, CONSTANTS - 1)
            pool.affine_select(out=ident[:, :], in_=ident[:, :], compare_op=ALU.not_equal, fill=1.0, base=0,
                               pattern=[[-1, P]], channel_multiplier=1).then_inc(constants, 1)

            def third_of_keys(ph, n, m):
                s, i = n[1], number(n)
                reached(pool, ph, "k_second", KC * i + m + 1)
                pool.tensor_tensor(k_part(ph, s, 2, m), k_rest[:, m, 0:ph.keys], k_part(ph, s, 1, m),
                                   ALU.subtract).then_inc(signal["k_split"], 1)

            def third_of_queries(ph, n):
                s, i = n[1], number(n)
                reached(pool, ph, "q_second", i + 1)
                pool.tensor_tensor(q_parts[:, s, 2, :, :], q_rest[:, :, :], q_parts[:, s, 1, :, :], ALU.subtract)\
                    .then_inc(signal["q_split"], 1)

            def residual(ph, n):
                s, i = n[1], number(n)
                reached(pool, ph, "y_ready", i - 1, alone=True)
                first = pool.tensor_tensor(x_res[:, s, :], state[:, i, :], ph.bo[:, :], ALU.add)
                if ph.twice:
                    first.then_inc(signal["residual_once"], 1)
                    reached(pool, ph, "residual_once", i + 1, alone=True)
                    first = pool.tensor_tensor(x_res[:, s, :], x_res[:, s, :], state[:, i, :], ALU.add)
                first.then_inc(signal["residual_ready"], 1)

            def root(ph, b):
                i = number(b)
                reached(pool, ph, "guess_ready", i + 1)
                inverse_root(pool, signal["root_step"], ph.base["root_step"] + ROOT_STEPS * i, root_in[:, :], root_tmp[:, :], rstd[:, :])

            def attend(ph):
                def step(b, h):
                    for n, _ in due(ph, "root", b, h):
                        root(ph, n)
                    for n, _ in due(ph, "residual", b, h):
                        residual(ph, n)
                    for n, m in due(ph, "third_of_keys", b, h):
                        third_of_keys(ph, n, m)
                    for n, _ in due(ph, "third_of_queries", b, h):
                        third_of_queries(ph, n)

                rounds(pool, ph, step)

            pool.wait_ge(b_out_ready, len(value_biases))
            pool.wait_ge(state_loaded, 16)
            attend(sa0)
            attend(xa0)

            pool.wait_ge(ffn["x_guess"], 1)
            inverse_root(pool, ffn["x_root_step"], 0, all_root_in[:, :], all_root_tmp[:, :], all_rstd[:, :])
            pool.wait_ge(ffn["y_guess"], 1)
            inverse_root(pool, ffn["y_root_step"], 0, all_root_in[:, :], all_root_tmp[:, :], all_rstd[:, :])
            attend(sa1)
            attend(xa1)
            reached(pool, xa1, "state_ready", B)
            pool.memset(b_down_flat, 0.0).then_inc(moe["rows_cleared"], 1)

            def keep_xT(b):
                s, i = b[1], number(b)
                pool.wait_ge(moe["xT_ready"], i + 1)
                pool.tensor_copy(xT_all[:, :, bass.ds(i * S, S)], xT[:, s, :, :]).then_inc(moe["xT_kept"], 1)

            over_batches(pool, keep_xT)

            def group_root(q):
                pool.wait_ge(moe["y_guess"], q + 1)
                inverse_root(pool, moe["y_root_step"], ROOT_STEPS * q, all_root_in[:, 0:MB], all_root_tmp[:, 0:MB],
                             all_rstd[:, 0:MB])

            group_root(0)
            with pool.Fori(1, B // MB) as q:
                group_root(q)


TURNED = ("L0_attn_w_qkv", "L0_attn_w_o", "L0_xattn_Wq", "L0_xattn_Wk", "L0_xattn_Wv", "L0_xattn_Wo",
          "L1_attn_Wq", "L1_attn_Wk", "L1_attn_Wv", "L1_attn_W_out")
COLUMNS = ("b_v", "L0_xattn_bv", "L1_xattn_bv", "L1_ffn_b1")
STACKED = ("L0_attn_b_qkv", "L0_xattn_bq", "L0_xattn_bk", "L1_xattn_bq", "L1_xattn_bk")
ORDERED = ("L0_attn_w_qkv", "L0_xattn_Wq", "L0_xattn_Wk", "L1_xattn_Wq", "L1_xattn_Wk")
NAMES = ("x", "ctx_1024", "fside_BxSxS2_0", "L0_attn_w_qkv", "L0_attn_b_qkv", "L0_attn_w_o", "L0_attn_b_o", "L0_xattn_Wq",
         "L0_xattn_bq", "L0_xattn_Wk", "L0_xattn_bk", "L0_xattn_Wv", "L0_xattn_bv", "L0_xattn_Wo", "L0_xattn_bo",
         "L0_xattn_distance_scaling", "L0_ffn_weight", "L0_ffn_ln_gamma", "L0_ffn_ln_beta", "L1_attn_Wq", "L1_attn_Wk",
         "L1_attn_Wv", "L1_attn_W_out", "L1_attn_b_out", "L1_xattn_Wq", "L1_xattn_bq", "L1_xattn_Wk", "L1_xattn_bk",
         "L1_xattn_Wv", "L1_xattn_bv", "L1_xattn_Wo", "L1_xattn_bo", "L1_ffn_Wg", "L1_ffn_bg", "L1_ffn_W1", "L1_ffn_b1",
         "L1_ffn_W2", "L1_ffn_b2", "b_v")


def kernel(**inputs):
    from concourse import bacc
    from concourse.bass_utils import run_bass_kernel_spmd

    nc = bacc.Bacc("TRN2", target_bir_lowering=False, num_devices=1)
    arrays, d = {}, {}
    for name in NAMES:
        a = np.asarray(inputs["L0_attn_b_qkv"][2 * D:] if name == "b_v" else inputs[name])
        if name in TURNED:
            a = a.T
        if name in COLUMNS:
            a = np.moveaxis(a.reshape(*a.shape[:-1], -1, P), -1, 0)
        if name in STACKED:
            a = a.reshape(-1, H // KC, KC, DH).transpose(3, 1, 0, 2).reshape(P, -1)
        if name in ORDERED:
            n = 2 * D if name == "L0_attn_w_qkv" else D
            turned = a[:, 0:n].reshape(D, -1, H // KC, KC, DH).transpose(0, 1, 3, 4, 2).reshape(D, n)
            a = np.concatenate([turned, a[:, n:]], axis=1)
        if name == "ctx_1024":
            a = a.transpose(0, 2, 1)
        a = np.ascontiguousarray(a if a.ndim else a.reshape(1))
        arrays["in_" + name] = a
        d[name] = nc.dram_tensor("in_" + name, a.shape, mybir.dt.from_np(a.dtype), kind="ExternalInput").ap()
    out = nc.dram_tensor("out", (B, S, D), F32, kind="ExternalOutput").ap()
    decoder(nc, d, out)
    return run_bass_kernel_spmd(nc, [arrays], core_ids=[0]).results[0]["out"]
```

```python
from contextlib import ExitStack

import concourse.bass as bass
from concourse import mybir
import numpy as np

F32 = mybir.dt.float32
BF16 = mybir.dt.bfloat16
I32 = mybir.dt.int32
ACT = mybir.ActivationFunctionType
ALU = mybir.AluOpType
AX = mybir.AxisListType

B, S, D, H, SK, E = 32, 100, 256, 16, 361, 8
DH = D // H
P = 128
KC = D // P
TERMS = 3
PRODUCTS = [(0, 3), (1, 2), (2, 1)]
BLOCKS = sum(n for _, n in PRODUCTS)
STACK = BLOCKS * DH
GROUP = 4
P_RING = 8
S_RING = 3
SB_RING = 4
LN_EPS = 1e-5
FFN_LN_EPS = 1e-3
FFN_EPS = 1e-5
QB = 128.0
QUAD = 4
QUADS = B // QUAD
TILES = (B * S + E * (P - 1)) // P
ROWS = TILES * P
ROUND = 1.5 * 2.0 ** 23
ROOT_GUESS = float(0x5F3759DF)
ROOT_STEPS = 3 * 4
DIST = B * S * SK // P
DIST_CHUNKS = 7
DIST_CHUNK = -(-DIST // DIST_CHUNKS)
PAIRS = B // 2
WORK = 22400
CONSTANTS = 8 + E + TILES
Q_SCALED = 7
W_LOADED = 16 * (29 + 3 * H)

PLAN_SELF = {
    "turn_x": [-38], "copy_xT": [-36], "keys": [-34, -34], "round_keys": [-32, -31], "rest_of_keys": [-30, -29],
    "queries": [-27], "round_queries": [-25], "rest_of_queries": [-23], "third_of_keys": [-28, -27],
    "third_of_queries": [-22], "values": [-6], "copy_values": [-4], "residual": [12],
    "scores": [0, 4, 8, 12], "maximum": [2, 6, 10, 14], "exponentiate": [4 + h for h in range(H)],
    "turn_probs": [10, 14, 18, 22], "copy_probs": [12, 16, 20, 24], "sum_heads": [19, 27],
    "invert": [21], "turn_inv": [23], "copy_inv": [24], "scale_heads": [30], "project": [34],
    "add_residual": [36], "take_stats": [37], "take_moments": [38], "guess_root": [39], "root": [39], "norm": [47]}
PLAN_CROSS = {
    "turn_x": [-32], "copy_xT": [-31], "keys": [-30, -25], "round_keys": [-28, -23], "rest_of_keys": [-27, -22],
    "queries": [-20], "round_queries": [-18], "rest_of_queries": [-17], "third_of_keys": [-26, -21],
    "third_of_queries": [-15], "values": [-10, -8, -6], "copy_values": [-9, -7, -5], "residual": [9],
    "scores": list(range(H)), "maximum": list(range(H)), "exponentiate": [1 + h for h in range(H)],
    "turn_probs": [4 * g + 6 + c for g in range(H // 4) for c in range(3)],
    "copy_probs": [4 * g + 7 + c for g in range(H // 4) for c in range(3)], "sum_heads": [15, 23],
    "invert": [18], "turn_inv": [20], "copy_inv": [21], "scale_heads": [26], "project": [29],
    "add_residual": [31], "take_stats": [32], "take_moments": [33], "guess_root": [34], "root": [34], "norm": [39]}
LAG = 6
FFN_STEPS = 6
PLAN_FFN = {"scale": [-10], "turn": [-7], "clip": [-4], "project": [-1], "add": [3], "take_stats": [5],
            "take_moments": [7], "keep_moments": [9]}

TILE_STEPS = 8
PLAN_TILES = {"turn": [-10], "copy_T": [-8], "up": [-5], "gelu": [-3], "turn_act": [0], "copy_act_T": [2], "down": [7],
              "keep": [10]}
FETCH_STEPS = 4
PLAN_FETCH = {"place": [-8], "fetch": [-7], "add": [0], "take_stats": [2], "take_moments": [3], "keep_moments": [4]}


def at_least(eng, sem, value):
    if isinstance(value, int) and value <= 0:
        return
    eng.wait_ge(sem, value)


class Steps:

    def __init__(self, plan, steps):
        self.plan, self.steps = plan, steps


class Attention:

    def __init__(self, keys, cross, wq, wk, wv, wo, bq, bk, bo, q_scale, biased, twice):
        self.keys, self.cross, self.biased = keys, cross, biased
        self.wq, self.wk, self.wv, self.wo = wq, wk, wv, wo
        self.bq, self.bk, self.bo, self.q_scale = bq, bk, bo, q_scale
        self.twice = twice
        self.chunks = -(-keys // P)
        size = -(-keys // self.chunks)
        self.spans = [(c * size, min(size, keys - c * size)) for c in range(self.chunks)]
        self.per_unit = GROUP if GROUP * keys <= 512 else 1
        self.units = H // self.per_unit
        self.fills = (H // GROUP) * self.chunks
        self.by_dve = [self.chunks == 1 or f % self.chunks == 1 or f == self.chunks + 2 for f in range(self.fills)]
        self.plan = PLAN_CROSS if cross else PLAN_SELF
        if biased:
            self.plan = self.plan | {"next_stats": [42], "next_moments": [43], "keep_moments": [44]}
        self.steps = H
        self.prev = self.next = None
        self.base = {}


def decoder(nc, d, out):
    ctx = ExitStack()

    def sb(name, shape, dt=F32):
        return ctx.enter_context(nc.sbuf_tensor(name, shape, dt))

    def sem(name):
        return ctx.enter_context(nc.semaphore(name))

    with ctx:
        state = sb("state", [S, B, D])
        ident = sb("ident", [P, P])
        ones = sb("ones", [P, P])
        tiny = sb("tiny", [P, 1])
        scaling = sb("scaling", [P, 1])
        neg_abs_ds = sb("neg_abs_ds", [P, 1])

        work = sb("work", [P, WORK])

        def carve(sizes):
            ends = [sum(sizes[:i + 1]) for i in range(len(sizes))]
            assert ends[-1] <= WORK
            return [work[:, e - n:e] for e, n in zip(ends, sizes)]

        k_stack, probs, probs_T, k_parts, ctxT, biased, k_rest, values, q_stack = carve(
            [H * SK, P_RING * SK, 2 * 3 * 2 * GROUP * S, TERMS * KC * SK, 2 * KC * SK, SB_RING * SK, KC * SK,
             2 * 3 * D, H * S])
        zeros = k_stack[:, H * SK - D:]
        k_stack = k_stack[0:STACK].bitcast(BF16).rearrange("p (s n) -> p s n", s=2)
        probs = probs[0:S].rearrange("p (h n) -> p h n", h=P_RING)
        probs_T = probs_T.rearrange("p (a c h n) -> p a c h n", a=2, c=3, h=2 * GROUP)
        k_parts = k_parts.bitcast(BF16).rearrange("p (s n) -> p s n", s=2)
        ctxT = ctxT.rearrange("p (s k n) -> p s k n", s=2, k=KC)
        biased = biased[0:S].rearrange("p (h n) -> p h n", h=SB_RING)
        k_rest = k_rest.rearrange("p (m n) -> p m n", m=KC)
        values = values.rearrange("p (s c n) -> p s c n", s=2, c=3)
        q_stack = q_stack[0:STACK].bitcast(BF16).rearrange("p (s n) -> p s n", s=2)

        dist = work[:, WORK - 2 * DIST_CHUNK:WORK].rearrange("p (s n) -> p s n", s=2)

        xn = work[0:S, 0:B * D].rearrange("p (b d) -> p b d", b=B)

        (w_up, w_down, b_rows, x_quad, xT_quad, x_tile, tile_T, act_tile, act_T, y_tile, prefix, place, x_out, y_in) = carve(
            [E * KC * D, E * KC * D, 2 * E * D, 2 * QUAD * D, KC * QUAD * S] + 5 * [2 * D] + [2 * B * E, B * E, 2 * D, 2 * D])
        w_up = w_up.rearrange("p (e k n) -> p e k n", e=E, k=KC)
        w_down = w_down.rearrange("p (e k n) -> p e k n", e=E, k=KC)
        b_rows = b_rows[0:1].rearrange("p (w e n) -> p w e n", w=2, e=E)
        x_quad = x_quad[0:S].rearrange("p (s n) -> p s n", s=2)
        xT_quad = xT_quad.rearrange("p (k n) -> p k n", k=KC)
        x_tile, act_tile, y_tile = (t.rearrange("p (s n) -> p s n", s=2) for t in (x_tile, act_tile, y_tile))
        x_out, y_in = (t[0:S].rearrange("p (s n) -> p s n", s=2) for t in (x_out, y_in))
        tile_T, act_T = (t.rearrange("p (s k n) -> p s k n", s=2, k=KC) for t in (tile_T, act_T))
        prefix = prefix[0:S].rearrange("p (a b e) -> p a b e", a=2, b=B)
        place = place[0:S].rearrange("p (b e) -> p b e", b=B)

        x_in = sb("x_in", [S, 2, D])
        x_res = sb("x_res", [S, 2, D])
        xT = sb("xT", [P, 2, KC, S])
        q_parts = sb("q_parts", [P, 2, TERMS, KC, S], BF16)
        q_rest = sb("q_rest", [P, KC, S])
        bias = sb("bias", [S, 2, SK])
        neg_max = sb("neg_max", [S, 2, H])
        sums = sb("sums", [S, 2, H])
        inv = sb("inv", [S, H])
        inv_wide = sb("inv_wide", [S, 2, 2, P])
        inv_T = sb("inv_T", [P, 2 * 2 * S])
        heads_par = sb("heads_par", [P, 2, 2, S])
        heads_T = sb("heads_T", [P, KC, S])
        y = sb("y", [S, D])
        stats = sb("stats", [S, 6])
        moments = sb("moments", [S, 2])
        state_stats_of = sb("state_stats", [S, 6])
        state_moments_of = sb("state_moments", [S, 2])
        root_in, root_tmp, rstd = sb("root_in", [S, 1]), sb("root_tmp", [S, 1]), sb("rstd", [S, 1])
        all_moments = sb("all_moments", [S, B, 2])
        all_root_in, all_root_tmp, all_rstd = (sb(n, [S, B]) for n in ("all_root_in", "all_root_tmp", "all_rstd"))

        ps_scores = ctx.enter_context(nc.psum_tensor("ps_scores", [P, S_RING, 512], F32))
        ps_probs = ctx.enter_context(nc.psum_tensor("ps_probs", [P, 2, 512], F32))
        ps_heads = ctx.enter_context(nc.psum_tensor("ps_heads", [P, 512], F32))
        ps_a = ctx.enter_context(nc.psum_tensor("ps_a", [P, 512], F32))
        ps_b = ctx.enter_context(nc.psum_tensor("ps_b", [P, 512], F32))

        w_qkv = sb("w_qkv", [P, KC, 3 * D])
        w = {n: sb("w_" + n, [P, KC, D]) for n in
             ("L0_attn_w_o", "L0_xattn_Wq", "L0_xattn_Wk", "L0_xattn_Wv", "L0_xattn_Wo", "L0_ffn_weight",
              "L1_attn_W_out", "L1_xattn_Wq", "L1_xattn_Wk", "L1_xattn_Wv", "L1_xattn_Wo")}
        w_diag = {n: sb("wd_" + n, [P, KC, D]) for n in ("L1_attn_Wq", "L1_attn_Wk", "L1_attn_Wv")}
        on_diagonal = {n: work[:, i * KC * D:(i + 1) * KC * D].rearrange("p (k n) -> p k n", k=KC)
                       for i, n in enumerate(("L1_attn_Wq", "L1_attn_Wk"))} | {"L1_attn_Wv": w_diag["L1_attn_Wv"]}
        b_qk = sb("b_qk", [P, 2 * KC])
        b_v = sb("b_v", [P, KC])
        b_col = {n: sb("b_" + n, [P, KC]) for n in
                 ("L0_xattn_bq", "L0_xattn_bk", "L0_xattn_bv", "L1_xattn_bq", "L1_xattn_bk", "L1_xattn_bv")}
        b_zero = sb("b_zero", [P, KC])
        b_out = {n: sb("bo_" + n, [S, D]) for n in ("L0_attn_b_o", "L0_xattn_bo", "L1_attn_b_out", "L1_xattn_bo")}
        ffn_gamma = sb("ffn_gamma", [S, D])
        ffn_beta = sb("ffn_beta", [S, D])
        w_gate = sb("w_gate", [P, KC, E])
        b_gate = sb("b_gate", [1, E])

        k_bounce = nc.dram_tensor("k_bounce", [2, TERMS * D * SK], BF16).ap()
        q_bounce = nc.dram_tensor("q_bounce", [2, TERMS * D * S], BF16).ap()

        bias_dram = nc.dram_tensor("bias_dram", [B, S, SK], F32).ap()

        constants = sem("constants")
        state_loaded = sem("state_loaded")
        passed = sem("passed")
        dist_loaded = [sem(f"dist_loaded_{s}") for s in range(2)]
        bias_stored = [sem(f"bias_stored_{s}") for s in range(2)]
        logs_ready = sem("logs_ready")
        bias_scaled = sem("bias_scaled")
        diag_cleared = sem("diag_cleared")
        columns_ordered = sem("columns_ordered")
        w_loaded = sem("w_loaded")
        q_scaled = sem("q_scaled")
        ds_ready = sem("ds_ready")
        bv_out = sem("bv_out")
        b_out_ready = sem("b_out_ready")

        def rows(tile, first=0):
            return lambda k: tile[:, k, first:first + D]

        def by_feature(tile, first=0):
            return lambda k, m: tile[:, k, first + m * P:first + (m + 1) * P]

        sa0 = Attention(S, False, by_feature(w_qkv), by_feature(w_qkv, D), rows(w_qkv, 2 * D), w["L0_attn_w_o"],
                        b_qk[:, 0:KC], b_qk[:, KC:2 * KC], b_out["L0_attn_b_o"],
                        (w_qkv[:, :, 0:D], float(D) ** -0.5), False, True)
        xa0 = Attention(SK, True, by_feature(w["L0_xattn_Wq"]), by_feature(w["L0_xattn_Wk"]), rows(w["L0_xattn_Wv"]),
                        w["L0_xattn_Wo"], b_col["L0_xattn_bq"], b_col["L0_xattn_bk"], b_out["L0_xattn_bo"],
                        (w["L0_xattn_Wq"][:, :, :], DH ** -0.5), True, False)
        sa1 = Attention(S, False, by_feature(w_diag["L1_attn_Wq"]), by_feature(w_diag["L1_attn_Wk"]),
                        rows(w_diag["L1_attn_Wv"]), w["L1_attn_W_out"], b_zero, b_zero, b_out["L1_attn_b_out"],
                        (w_diag["L1_attn_Wq"][:, :, :], float(D) ** -0.5), False, False)
        xa1 = Attention(SK, True, by_feature(w["L1_xattn_Wq"]), by_feature(w["L1_xattn_Wk"]), rows(w["L1_xattn_Wv"]),
                        w["L1_xattn_Wo"], b_col["L1_xattn_bq"], b_col["L1_xattn_bk"], b_out["L1_xattn_bo"],
                        (w["L1_xattn_Wq"][:, :, :], DH ** -0.5), False, False)
        phases = [sa0, xa0, sa1, xa1]
        for first, second in ((sa0, xa0), (sa1, xa1)):
            first.next, second.prev = second, first
        value_biases = [(b_v, sa0), (b_col["L0_xattn_bv"], xa0), (b_col["L1_xattn_bv"], xa1)]

        once = ["x_turned", "xT_ready", "q_done", "q_second", "q_split", "residual_ready",
                "inv_ready", "inv_turned", "inv_T_ready", "heads_scaled", "heads_ready",
                "out_projected", "y_ready", "stats_ready", "moments_ready", "root_in_ready", "guess_ready", "state_ready"]
        times = {name: lambda ph: 1 for name in once}
        times |= {name: lambda ph: KC for name in
                  ("k_done", "k_rounded", "k_rest_ready", "k_second", "k_split", "q_rounded", "q_rest_ready")}
        times |= {name: lambda ph: ph.chunks for name in ("v_projected", "v_ready")}
        times |= {name: lambda ph: ph.units for name in ("scores_ready", "maxed")}
        times |= {"root_step": lambda ph: ROOT_STEPS}
        times |= {"residual_once": lambda ph: int(ph.twice),
                  "probs_ready": lambda ph: H,
                  "probs_turned": lambda ph: ph.fills,
                  "act_copied": lambda ph: ph.by_dve.count(False),
                  "dve_copied": lambda ph: ph.by_dve.count(True),
                  "heads_summed": lambda ph: 2,
                  "inv_wide_ready": lambda ph: 2}
        signal = {name: sem(name) for name in times}
        dma_times = {"x_loaded": lambda ph: 16, "ctx_loaded": lambda ph: 16 * ph.cross,
                     "bias_loaded": lambda ph: 16 * ph.biased, "bounced": lambda ph: 16 * 2,
                     "stacked": lambda ph: 16 * 2 * len(PRODUCTS)}
        dma_signal = {name: [sem(f"{name}_{s}") for s in range(2)] for name in dma_times}
        for i, ph in enumerate(phases):
            ph.base = {name: sum(B * n(p) for p in phases[:i]) for name, n in times.items()}
            ph.base |= {name: sum(PAIRS * n(p) for p in phases[:i]) for name, n in dma_times.items()}

        def reached(eng, ph, name, count, alone=False, own=False):
            if isinstance(count, int) and count <= 0:
                if own or not ph.prev:
                    return
                mine, its = times[name](ph), times[name](ph.prev)
                count = count if mine == its else its * -(-count // mine) if mine else 0
            (apart if alone else at_least)(eng, signal[name], ph.base[name] + count)

        def arrived(eng, ph, name, b, back=0, alone=False):
            count = dma_times[name](ph) * (b[0] + 1 - back)
            (apart if alone else at_least)(eng, dma_signal[name][b[1]], ph.base[name] + count)

        def values_taken(eng, ph, i):
            if isinstance(i, int) and i > B:
                ph, i = (ph.next, i - B) if ph.next else (ph, B)
            reached(eng, ph, "v_ready", ph.chunks * i)

        ffn_work = Steps(PLAN_FFN, FFN_STEPS)
        ffn = {name: sem("ffn_" + name) for name in
               ("w_sum", "w_total", "w_mean", "w_beta", "w_scaled", "w_rounded", "w_ready",
                "x_stats", "x_aggregated", "x_moments", "x_root_in", "x_guess", "x_root_step", "gained", "xn_ready", "row_max", "max_turned", "max_one",
                "max_spread", "gamma_ready", "gain_ready", "xq_scaled", "xq_turned", "xqT_ready",
                "projected", "y_ready", "y_stats", "y_aggregated", "y_moments", "y_root_in", "y_guess", "y_root_step", "state_ready",
                "w_inverse", "gamma_inverse")}
        row_max = sb("row_max", [S, 1])
        max_one = sb("max_one", [1, 1])
        gamma = sb("gamma", [S, 3])
        w_sum = sb("w_sum", [P, 1])
        w_beta = sb("w_beta", [P, 3])
        gain = sb("gain", [S, 2])
        xq = sb("xq", [S, 2, D])
        xqT = sb("xqT", [P, 2, KC, S])
        w_tmp = sb("w_tmp", [P, KC, D])

        moe_tiles, moe_fetch = Steps(PLAN_TILES, TILE_STEPS), Steps(PLAN_FETCH, FETCH_STEPS)
        moe = {name: sem("moe_" + name) for name in
               ("w_loaded", "cleared", "x_cleared", "x_turned", "xT_ready", "gated", "logits_ready",
                "top_ready", "shifted", "exp_ready", "sum_ready", "weight_ready", "top_found", "rank_ready", "first_ready",
                "hot_found", "counted", "prefixed", "routed", "placed", "experts_known", "put", "tile_turned", "tile_T_ready",
                "up_done", "gelu_done", "act_turned", "act_T_ready", "down_done", "tile_kept", "slot_placed", "added",
                "y_stats", "y_aggregated", "y_moments", "y_root_in", "y_guess", "y_root_step", "out_ready")}
        quad_loaded, scattered, tile_loaded, tile_stored, fetched = (
            [sem(f"moe_{n}_{s}") for s in range(2)] for n in ("quad_loaded", "scattered", "tile_loaded", "tile_stored", "fetched"))
        stored = sem("stored")
        logits = sb("logits", [S, B, E])
        top = sb("top", [S, B])
        shifted = sb("shifted", [S, B, E])
        exps = sb("exps", [S, B, E])
        top_weight = sb("top_weight", [S, B])
        rank = sb("rank", [S, B, E])
        rank_of = sb("rank_of", [S, E])
        hot = sb("hot", [S, B, E])
        below = sb("below", [S, S])
        room, room_tmp = sb("room", [S, 2, E]), sb("room_tmp", [S, 2, E])
        slot_of = sb("slot_of", [S, B])
        slot_now = sb("slot_now", [S, 2], I32)
        tile_first = sb("tile_first", [1, TILES])
        passed_by = sb("passed_by", [1, TILES, E])
        tile_expert = sb("tile_expert", [1, TILES])
        tile_expert_i = sb("tile_expert_i", [1, TILES], I32)

        x_sorted = nc.dram_tensor("x_sorted", [ROWS, D], F32).ap()
        y_sorted = nc.dram_tensor("y_sorted", [ROWS, D], F32).ap()

        block = ctx.enter_context(nc.Block())

        def apart(eng, sem, value):
            at_least(eng, sem, value)
            if not isinstance(value, int):
                eng.sem_inc(passed, 1)

        def number(b):
            return b[0] * 2 + b[1]

        def later(b, n):
            return (b[0] + (b[1] + n) // 2, (b[1] + n) % 2)

        def exists(b):
            return not isinstance(b[0], int) or 0 <= number(b) < B

        FIRST, LAST = (0, 0), (PAIRS - 1, 1)

        def over_batches(eng, body, ahead=0, behind=0, pairs=PAIRS):
            last = pairs - 1 - ahead // 2
            for pair in range(-ahead, 1):
                body((pair, 0))
                body((pair, 1))
            with eng.Fori(1, last) as pair:
                body((pair, 0))
                body((pair, 1))
            for pair in range(last, pairs + behind):
                body((pair, 0))
                body((pair, 1))

        def due(ph, name, b, h):
            return [(later(b, -(at // ph.steps)), part) for part, at in enumerate(ph.plan.get(name, []))
                    if at % ph.steps == h and exists(later(b, -(at // ph.steps)))]

        def rounds_of(ph):
            first = min(min(steps) for steps in ph.plan.values())
            last = max(max(steps) for steps in ph.plan.values())
            return -(first // (2 * ph.steps)), -(-(last // ph.steps) // 2)

        def rounds(eng, work, step):
            def one(b):
                for h in range(work.steps):
                    step(work, b, h)
            over_batches(eng, one, *rounds_of(work))

        def over_two(eng, first, second, body, meeting, ahead, behind):
            def over(ph, pairs):
                for pair in pairs:
                    for s in range(2):
                        body(ph, (pair, s))

            over(first, range(-ahead[0], 1))
            meet, last = PAIRS - max(2, *ahead), PAIRS - 1 - ahead[1] // 2
            with eng.Fori(1, meet) as pair:
                over(first, [pair])
            meeting([(pair, s) for pair in range(meet, PAIRS + behind[0]) for s in range(2)])
            with eng.Fori(max(1, behind[0]), last) as pair:
                over(second, [pair])
            over(second, range(last, PAIRS + behind[1]))

        def attentions(eng, first, second, step):
            def one(ph, b):
                for h in range(H):
                    step(ph, b, h)

            def meeting(turns):
                for t in range(H * len(turns) + LAG):
                    for ph, back, lag in ((first, 0, 0), (second, B, LAG)):
                        turn, h = divmod(t - lag, H)
                        if 0 <= turn < len(turns):
                            step(ph, later(turns[turn], -back), h)

            ends = [rounds_of(ph) for ph in (first, second)]
            over_two(eng, first, second, one, meeting, [e[0] for e in ends], [max(1, e[1]) for e in ends])

        def bank_of(s, u):
            return (u + s) % S_RING

        def k_part(ph, s, t, m):
            first = (t * KC + m) * ph.keys
            return k_parts[:, s, first:first + ph.keys]

        def k_place(ph, m):
            return ps_b[:, 0:SK] if ph.cross else ps_b[:, m * S:(m + 1) * S]

        def copies(ph, b, f, dve):
            mine = [i for i in range(ph.fills) if ph.by_dve[i] == dve]
            return len(mine) * number(b) + sum(i <= f for i in mine)

        def wait_copied(eng, ph, b, f):
            if not exists(b) and ph.prev:
                reached(eng, ph, "dve_copied", 0)
                reached(eng, ph, "act_copied", 0)
                return
            dve = ph.by_dve[f]
            reached(eng, ph, "dve_copied" if dve else "act_copied", copies(ph, b, f, dve))

        def inverse_root(pool, step, before_it, value, scratch, result):
            for n in range(ROOT_STEPS // 4):
                at = before_it + 4 * n
                apart(pool, step, at)
                pool.tensor_tensor(scratch, result, result, ALU.mult).then_inc(step, 1)
                pool.wait_ge(step, at + 1)
                pool.tensor_tensor(scratch, scratch, value, ALU.mult).then_inc(step, 1)
                apart(pool, step, at + 2)
                pool.tensor_scalar(scratch, scratch, -0.5, 1.5, ALU.mult, ALU.add).then_inc(step, 1)
                pool.wait_ge(step, at + 3)
                pool.tensor_tensor(result, result, scratch, ALU.mult).then_inc(step, 1)

        def dist_span(c):
            return c * DIST_CHUNK, min(DIST_CHUNK, DIST - c * DIST_CHUNK)

        @block.sync
        def _(sp):
            def row(name, width):
                return d[name].rearrange("(a n) -> a n", a=1).to_broadcast([S, width])

            sp.dma_start(state[:, :, :], d["x"].rearrange("b s d -> s b d")).then_inc(state_loaded, 16)
            loads = [(w_qkv[:, :, :], d["L0_attn_w_qkv"].rearrange("(k p) n -> p k n", p=P))]
            loads += [(t[:, :, :], d[n].rearrange("(k p) n -> p k n", p=P)) for n, t in w.items()]
            loads += [(b_qk[:, :], d["L0_attn_b_qkv"][:, 0:2 * KC]), (b_v[:, :], d["b_v"])]
            loads += [(t[:, :], d[n]) for n, t in b_col.items()]
            loads += [(t[:, :], row(n, D)) for n, t in b_out.items()]
            loads += [(ffn_gamma[:, :], row("L0_ffn_ln_gamma", D)), (ffn_beta[:, :], row("L0_ffn_ln_beta", D)),
                      (w_gate[:, :, :], d["L1_ffn_Wg"].rearrange("(k p) e -> p k e", p=P)),
                      (b_gate[:, :], d["L1_ffn_bg"].rearrange("(a n) -> a n", a=1)),
                      (scaling[:, :], d["L0_xattn_distance_scaling"].rearrange("(a n) -> a n", a=1).to_broadcast([P, 1]))]
            for tile, source in loads:
                sp.dma_start(tile, source).then_inc(w_loaded, 16)
            sp.wait_ge(diag_cleared, len(w_diag))
            for n, t in on_diagonal.items():
                for h in range(H):
                    at, k = h * DH % P, h * DH // P
                    sp.dma_start(t[at:at + DH, k, h * DH:(h + 1) * DH], d[n]).then_inc(w_loaded, 16)
            assert 16 * (len(loads) + len(w_diag) * H) == W_LOADED

            flat = (d["fside_BxSxS2_0"].rearrange("b s k -> (b s k)").rearrange("(p n) -> p n", p=P),
                    bias_dram.rearrange("b s k -> (b s k)").rearrange("(p n) -> p n", p=P))

            def load_dist(c):
                first, size = dist_span(c)
                at_least(sp, bias_stored[c % 2], 16 * (c // 2))
                sp.dma_start(dist[:, c % 2, 0:size], flat[0][:, first:first + size]).then_inc(dist_loaded[c % 2], 16)

            load_dist(0)
            load_dist(1)
            for c in range(DIST_CHUNKS):
                first, size = dist_span(c)
                sp.wait_ge(bias_scaled, c + 1)
                sp.dma_start(flat[1][:, first:first + size], dist[:, c % 2, 0:size]).then_inc(bias_stored[c % 2], 16)
                if c + 2 < DIST_CHUNKS:
                    load_dist(c + 2)
            for s in range(2):
                sp.wait_ge(bias_stored[s], 16 * len(range(s, DIST_CHUNKS, 2)))

            def load_x(ph, n):
                s, i = n[1], number(n)
                if ph.prev:
                    reached(sp, ph.prev, "state_ready", i + 1, alone=True)
                reached(sp, ph, "x_turned", i - 1)
                sp.dma_start(x_in[:, s, :], state[:, i, :]).then_inc(dma_signal["x_loaded"][s], 16)

            def load_context(ph, n):
                s, i = n[1], number(n)
                reached(sp, ph, "v_projected", ph.chunks * (i - 1), own=True)
                sp.dma_start(ctxT[:, s, :, :], d["ctx_1024"][i].rearrange("(k p) n -> p k n", p=P))\
                    .then_inc(dma_signal["ctx_loaded"][s], 16)

            def load_bias(ph, n):
                s, i = n[1], number(n)
                reached(sp, ph, "maxed", ph.units * (i - 1), own=True)
                sp.dma_start(bias[:, s, :], bias_dram[i]).then_inc(dma_signal["bias_loaded"][s], 16)

            def stack(ph, n):
                s, i = n[1], number(n)
                arrived(sp, ph, "stacked", n, back=1, alone=True)
                reached(sp, ph, "k_split", KC * (i + 1))
                def bounce(dram, parts, n):
                    place = dram[s, 0:TERMS * D * n].rearrange("(t p n) -> p t n", t=TERMS, p=P)
                    sp.dma_start(place, parts).then_inc(dma_signal["bounced"][s], 16)
                    return dram[s, 0:TERMS * D * n].rearrange("(t f n) -> t f n", t=TERMS, f=DH)

                kb = bounce(k_bounce, k_parts[:, s, 0:TERMS * KC * ph.keys].rearrange("p (t n) -> p t n", t=TERMS), ph.keys)
                reached(sp, ph, "q_split", i + 1)
                qb = bounce(q_bounce, q_parts[:, s, :, :, :].rearrange("p t m n -> p t (m n)"), S)
                arrived(sp, ph, "bounced", n, alone=True)
                reached(sp, ph, "scores_ready", ph.units * (i - 1))
                first = 0
                for part, meets in PRODUCTS:
                    rows = slice(first * DH, (first + meets) * DH)
                    sp.dma_start(k_stack[rows, s, 0:H * ph.keys], kb[0:meets].rearrange("t f n -> (t f) n"))\
                        .then_inc(dma_signal["stacked"][s], 16)
                    sp.dma_start(q_stack[rows, s, :], qb[part:part + 1].to_broadcast([meets, DH, H * S]))\
                        .then_inc(dma_signal["stacked"][s], 16)
                    first += meets

            def attend(first, second):
                def body(ph, b):
                    if exists(later(b, 3)):
                        load_x(ph, later(b, 3))
                    if exists(later(b, 1)):
                        if ph.biased:
                            load_bias(ph, later(b, 1))
                        stack(ph, later(b, 1))
                    if ph.cross and exists(later(b, 3)):
                        load_context(ph, later(b, 3))

                def meeting(turns):
                    for b in turns:
                        body(first, b)
                        body(second, later(b, -B))

                over_two(sp, first, second, body, meeting, (2, 2), (1, 0))
                reached(sp, second, "state_ready", B)

            sp.wait_ge(state_loaded, 16)
            sp.wait_ge(moe["cleared"], 1)
            sp.dma_start(x_sorted.rearrange("(p t) n -> p t n", p=P),
                         zeros.rearrange("p (a n) -> p a n", a=1).to_broadcast([P, TILES, D])).then_inc(moe["x_cleared"], 16)
            sp.wait_ge(moe["x_cleared"], 16)
            attend(sa0, xa0)
            sp.wait_ge(ffn["state_ready"], B)
            attend(sa1, xa1)
            def load_quad(q):
                s = q[1]
                at_least(sp, moe["x_turned"], number(q) - 1)
                sp.dma_start(x_quad[:, s, :], state[:, bass.ds(number(q) * QUAD, QUAD), :].rearrange("p b d -> p (b d)"))\
                    .then_inc(quad_loaded[s], 16)

            load_quad((0, 0))
            load_quad((0, 1))
            with sp.Fori(1, QUADS // 2) as pair:
                load_quad((pair, 0))
                load_quad((pair, 1))
            for e in range(E):
                sp.dma_start(w_up[:, e], d["L1_ffn_W1"][e].rearrange("(k p) n -> p k n", p=P)).then_inc(moe["w_loaded"], 16)
                sp.dma_start(w_down[:, e], d["L1_ffn_W2"][e].rearrange("(k p) n -> p k n", p=P)).then_inc(moe["w_loaded"], 16)
            for i, name in enumerate(("L1_ffn_b1", "L1_ffn_b2")):
                sp.dma_start(b_rows[:, i], d[name].rearrange("(a e) n -> a e n", a=1)).then_inc(moe["w_loaded"], 16)

            for s in range(2):
                sp.wait_ge(scattered[s], 16 * PAIRS)

            def load_tile(t):
                at_least(sp, moe["tile_turned"], number(t) - 1)
                sp.dma_start(x_tile[:, t[1], :], x_sorted[bass.ds(number(t) * P, P), :]).then_inc(tile_loaded[t[1]], 16)

            def store_tile(t):
                sp.wait_ge(moe["tile_kept"], number(t) + 1)
                sp.dma_start(y_sorted[bass.ds(number(t) * P, P), :], y_tile[:, t[1], :]).then_inc(tile_stored[t[1]], 16)

            def tiles(t):
                if exists(later(t, 2)):
                    load_tile(later(t, 2))
                if exists(later(t, -1)):
                    store_tile(later(t, -1))

            over_batches(sp, tiles, 1, 1)

            def store(q):
                sp.wait_ge(moe["out_ready"], QUAD * (q + 1))
                those = bass.ds(q * QUAD, QUAD)
                sp.dma_start(out[those].rearrange("b s d -> s b d"), state[:, those, :]).then_inc(stored, 16)

            with sp.Fori(0, QUADS) as q:
                store(q)
            sp.wait_ge(stored, 16 * QUADS)

        @block.tensor
        def _(pe):
            pe.wait_ge(constants, CONSTANTS)
            pe.wait_ge(w_loaded, W_LOADED)

            for i, (bv, ph) in enumerate(value_biases):
                at_least(pe, b_out_ready, i)
                for k in range(KC):
                    mm = pe.matmul(ps_a[0:S, 0:D], bv[:, k:k + 1].to_broadcast([P, S]), ph.wo[:, k, :],
                                   start=(k == 0), stop=(k == KC - 1))
                mm.then_inc(bv_out, 1)
            pe.wait_ge(b_out_ready, len(value_biases))
            pe.wait_ge(q_scaled, Q_SCALED)

            pe.wait_ge(ffn["w_sum"], 1)
            pe.matmul(ps_b[:, 0:1], ones[:, :], w_sum[:, :], start=True, stop=True).then_inc(ffn["w_total"], 1)
            pe.wait_ge(ffn["w_mean"], 1)

            def turn_x(ph, n):
                s, i = n[1], number(n)
                arrived(pe, ph, "x_loaded", n)
                reached(pe, ph, "q_rest_ready", KC * i)
                for k in range(KC):
                    mm = pe.transpose(ps_b[:, k * S:(k + 1) * S], x_in[:, s, k * P:(k + 1) * P], ident[0:S, 0:S])
                mm.then_inc(signal["x_turned"], 1)

            def keys_of(ph, n, m):
                s, i = n[1], number(n)
                if m == 0:
                    reached(pe, ph, "xT_ready", i + 1)
                    if ph.cross:
                        arrived(pe, ph, "ctx_loaded", n)
                elif ph.cross:
                    reached(pe, ph, "k_rest_ready", KC * i + m)
                source = ctxT if ph.cross else xT
                for k in range(KC):
                    mm = pe.matmul(k_place(ph, m), ph.wk(k, m), source[:, s, k, :], start=(k == 0), stop=(k == KC - 1))
                mm.then_inc(signal["k_done"], 1)

            def queries_of(ph, n):
                s, i = n[1], number(n)
                reached(pe, ph, "k_rest_ready", KC * (i + 1))
                for m in range(KC):
                    for k in range(KC):
                        mm = pe.matmul(ps_b[:, m * S:(m + 1) * S], ph.wq(k, m), xT[:, s, k, :],
                                       start=(k == 0), stop=(k == KC - 1))
                mm.then_inc(signal["q_done"], 1)

            def values_of(ph, n, c):
                s, i = n[1], number(n)
                source = ctxT if ph.cross else xT
                first, size = ph.spans[c]
                if c == 0:
                    reached(pe, ph, "xT_ready", i + 1)
                    if ph.cross:
                        arrived(pe, ph, "ctx_loaded", n)
                    reached(pe, ph, "inv_T_ready", i - 1)
                reached(pe, ph, "v_ready", ph.chunks * i + c)
                for k in range(KC):
                    lhsT = source[:, s, k, first:first + size]
                    mm = pe.matmul(ps_a[0:size, 0:D], lhsT, ph.wv(k), start=(k == 0), stop=(k == KC - 1))
                mm.then_inc(signal["v_projected"], 1)

            def scores_of(ph, b, u):
                s, i = b[1], number(b)
                if u == 0:
                    arrived(pe, ph, "stacked", b)
                if u >= S_RING:
                    held, at = u - S_RING, i
                else:
                    held, at = max(v for v in range(ph.units) if bank_of(1 - s, v) == bank_of(s, u)), i - 1
                if isinstance(at, int) and at < 0 and ph.prev:
                    held = max(v for v in range(ph.prev.units) if bank_of(1 - s, v) == bank_of(s, u))
                    reached(pe, ph.prev, "probs_ready", (B - 1) * H + (held + 1) * ph.prev.per_unit)
                elif ph.biased:
                    reached(pe, ph, "maxed", at * ph.units + held + 1)
                else:
                    reached(pe, ph, "probs_ready", at * H + (held + 1) * ph.per_unit)
                for j in range(ph.per_unit):
                    h = u * ph.per_unit + j
                    mm = pe.matmul(ps_scores[0:S, bank_of(s, u), j * ph.keys:(j + 1) * ph.keys],
                                   q_stack[:, s, h * S:(h + 1) * S], k_stack[:, s, h * ph.keys:(h + 1) * ph.keys], start=True, stop=True)
                mm.then_inc(signal["scores_ready"], 1)

            def turn_probs(ph, b, g, c):
                f = g * ph.chunks + c
                first, size = ph.spans[c]
                reached(pe, ph, "probs_ready", H * number(b) + GROUP * (g + 1))
                if f >= 2:
                    wait_copied(pe, ph, b, f - 2)
                else:
                    wait_copied(pe, ph, later(b, -1), ph.fills + f - 2)
                for j in range(GROUP):
                    mm = pe.transpose(ps_probs[0:size, f % 2, j * S:(j + 1) * S],
                                      probs[:, (g * GROUP + j) % P_RING, first:first + size], ident[0:S, 0:S])
                mm.then_inc(signal["probs_turned"], 1)

            def sum_heads(ph, b, half):
                s, i = b[1], number(b)
                last = (half + 1) * ph.fills // 2 - 1
                for dve in (False, True):
                    if dve in ph.by_dve:
                        reached(pe, ph, "dve_copied" if dve else "act_copied", copies(ph, b, last, dve))
                if half == 0:
                    reached(pe, ph, "v_ready", ph.chunks * (i + 1))
                    reached(pe, ph, "heads_scaled", i)
                for c, (first, size) in enumerate(ph.spans):
                    for j in range(4):
                        at = (4 * half + j) * 2 * DH
                        mm = pe.matmul(ps_heads[32 * j:32 * j + 32, half * 2 * S:(half + 1) * 2 * S],
                                       values[0:size, s, c, at:at + 2 * DH], probs_T[0:size, half, c, 2 * j:2 * j + 2, :],
                                       start=(c == 0), stop=(c == ph.chunks - 1))
                mm.then_inc(signal["heads_summed"], 1)

            def turn_inv(ph, b):
                i = number(b)
                reached(pe, ph, "inv_wide_ready", 2 * (i + 1))
                reached(pe, ph, "y_ready", i)
                values_taken(pe, ph, i + 2)
                for j in range(4):
                    mm = pe.transpose(ps_a[:, j * S:(j + 1) * S], inv_wide[:, j // 2, j % 2, :], ident[0:S, 0:S])
                mm.then_inc(signal["inv_turned"], 1)

            def project(ph, b):
                i = number(b)
                reached(pe, ph, "heads_ready", i + 1)
                values_taken(pe, ph, i + 3)
                for k in range(KC):
                    mm = pe.matmul(ps_a[0:S, 0:D], heads_T[:, k, :], ph.wo[:, k, :], start=(k == 0), stop=(k == KC - 1))
                mm.then_inc(signal["out_projected"], 1)

            def attend_step(ph, b, h):
                for n, u in due(ph, "scores", b, h):
                    scores_of(ph, n, u)
                for n, f in due(ph, "turn_probs", b, h):
                    turn_probs(ph, n, f // ph.chunks, f % ph.chunks)
                for n, _ in due(ph, "turn_inv", b, h):
                    turn_inv(ph, n)
                for n, half in due(ph, "sum_heads", b, h):
                    sum_heads(ph, n, half)
                for n, c in due(ph, "values", b, h):
                    values_of(ph, n, c)
                for n, _ in due(ph, "turn_x", b, h):
                    turn_x(ph, n)
                for n, m in due(ph, "keys", b, h):
                    keys_of(ph, n, m)
                for n, _ in due(ph, "queries", b, h):
                    queries_of(ph, n)
                for n, _ in due(ph, "project", b, h):
                    project(ph, n)

            def attend(first, second):
                attentions(pe, first, second, attend_step)
                reached(pe, second, "state_ready", B)

            attend(sa0, xa0)

            pe.wait_ge(ffn["row_max"], 1)
            pe.transpose(ps_a[0:1, 0:S], row_max[:, :], ident[0:S, 0:S]).then_inc(ffn["max_turned"], 1)
            pe.wait_ge(ffn["max_one"], 1)
            pe.matmul(ps_a[0:S, 0:1], ones[0:1, 0:S], max_one[:, :], start=True, stop=True).then_inc(ffn["max_spread"], 1)
            pe.wait_ge(ffn["w_ready"], 1)

            def ffn_turn(b):
                s, i = b[1], number(b)
                pe.wait_ge(ffn["xq_scaled"], i + 1)
                at_least(pe, ffn["xqT_ready"], i - 1)
                for k in range(KC):
                    mm = pe.transpose(ps_probs[:, s, k * S:(k + 1) * S], xq[:, s, k * P:(k + 1) * P], ident[0:S, 0:S])
                mm.then_inc(ffn["xq_turned"], 1)

            def ffn_project(b):
                s, i = b[1], number(b)
                pe.wait_ge(ffn["xqT_ready"], i + 1)
                at_least(pe, ffn["y_ready"], i - 1)
                for k in range(KC):
                    mm = pe.matmul(ps_scores[0:S, s, 0:D], xqT[:, s, k, :], w["L0_ffn_weight"][:, k, :],
                                   start=(k == 0), stop=(k == KC - 1))
                mm.then_inc(ffn["projected"], 1)

            def ffn_step(work, b, h):
                for n, _ in due(work, "turn", b, h):
                    ffn_turn(n)
                for n, _ in due(work, "project", b, h):
                    ffn_project(n)

            rounds(pe, ffn_work, ffn_step)
            pe.wait_ge(ffn["state_ready"], B)
            attend(sa1, xa1)

            def gate(q):
                s, i = q[1], number(q)
                pe.wait_ge(quad_loaded[s], 16 * (q[0] + 1))
                at_least(pe, moe["xT_ready"], KC * i)
                for k in range(KC):
                    for j in range(QUAD):
                        at = j * D + k * P
                        mm = pe.transpose(ps_scores[:, k, j * S:(j + 1) * S], x_quad[:, s, at:at + P], ident[0:S, 0:S])
                mm.then_inc(moe["x_turned"], 1)
                pe.wait_ge(moe["xT_ready"], KC * (i + 1))
                at_least(pe, moe["logits_ready"], i)
                for j in range(QUAD):
                    at = ps_heads[0:S, j * E:(j + 1) * E]
                    for k in range(KC):
                        pe.matmul(at, xT_quad[:, k, j * S:(j + 1) * S], w_gate[:, k, :], start=(k == 0), stop=False)
                    mm = pe.matmul(at, ones[0:1, 0:S], b_gate[:, :], start=False, stop=True)
                mm.then_inc(moe["gated"], 1)

            over_batches(pe, gate, pairs=QUADS // 2)

            pe.wait_ge(moe["hot_found"], 1)
            chosen = hot[:, :, :].rearrange("p b e -> p (b e)")
            pe.matmul(ps_a[0:S, 0:B * E], ones[0:S, 0:S], chosen, start=True, stop=True)
            pe.matmul(ps_b[0:S, 0:B * E], below[:, :], chosen, start=True, stop=True).then_inc(moe["counted"], 1)
            pe.wait_ge(moe["placed"], 1)
            pe.wait_ge(moe["w_loaded"], 16 * (2 * E + 2))
            pe.wait_ge(moe["experts_known"], 1)

            def turn_tile(t):
                s, i = t[1], number(t)
                pe.wait_ge(tile_loaded[s], 16 * (t[0] + 1))
                at_least(pe, moe["tile_T_ready"], i)
                for k in range(KC):
                    mm = pe.transpose(ps_b[:, k * P:(k + 1) * P], x_tile[:, s, k * P:(k + 1) * P], ident[:, :])
                mm.then_inc(moe["tile_turned"], 1)

            def expert_of(t):
                return pe.value_load(tile_expert_i[0:1, bass.ds(number(t), 1)], min_val=0, max_val=E - 1)

            def through(place, source_T, weight, layer, t, e):
                for k in range(KC):
                    pe.matmul(place, source_T[:, t[1], k, :], weight[:, bass.ds(e, 1), k, :].rearrange("p a n -> p (a n)"),
                              start=(k == 0), stop=False)
                return pe.matmul(place, ones[0:1, :], b_rows[:, layer, bass.ds(e, 1), :].rearrange("p a n -> p (a n)"),
                                 start=False, stop=True)

            def up(t):
                e = expert_of(t)
                pe.wait_ge(moe["tile_T_ready"], number(t) + 1)
                at_least(pe, moe["gelu_done"], number(t) - 1)
                through(ps_scores[:, t[1], 0:D], tile_T, w_up, 0, t, e).then_inc(moe["up_done"], 1)

            def turn_act(t):
                s, i = t[1], number(t)
                pe.wait_ge(moe["gelu_done"], i + 1)
                at_least(pe, moe["act_T_ready"], i - 1)
                for k in range(KC):
                    mm = pe.transpose(ps_probs[:, s, k * P:(k + 1) * P], act_tile[:, s, k * P:(k + 1) * P], ident[:, :])
                mm.then_inc(moe["act_turned"], 1)

            def down(t):
                e = expert_of(t)
                pe.wait_ge(moe["act_T_ready"], number(t) + 1)
                at_least(pe, moe["tile_kept"], number(t) - 1)
                through((ps_heads if t[1] else ps_a)[:, 0:D], act_T, w_down, 1, t, e).then_inc(moe["down_done"], 1)

            def tile_step(work, b, h):
                for t, _ in due(work, "turn_act", b, h):
                    turn_act(t)
                for t, _ in due(work, "up", b, h):
                    up(t)
                for t, _ in due(work, "turn", b, h):
                    turn_tile(t)
                for t, _ in due(work, "down", b, h):
                    down(t)

            rounds(pe, moe_tiles, tile_step)

        @block.scalar
        def _(act):
            def copy_xT(ph, n):
                s, i = n[1], number(n)
                reached(act, ph, "x_turned", i + 1)
                reached(act, ph, "q_done", i - 1)
                if not ph.cross or (ph.prev and isinstance(i, int)):
                    reached(act, ph, "v_projected", ph.chunks * (i - 1))
                act.activation(xT[:, s, :, :], ps_b[:, 0:KC * S].rearrange("p (k t) -> p k t", k=KC), ACT.Copy)\
                    .then_inc(signal["xT_ready"], 1)

            def round_keys(ph, n, m):
                s, i = n[1], number(n)
                if m == 0:
                    arrived(act, ph, "bounced", n, back=1)
                reached(act, ph, "k_done", KC * i + m + 1 if ph.cross else KC * (i + 1))
                act.activation(k_part(ph, s, 0, m), k_place(ph, m), ACT.Identity, bias=ph.bk[:, m:m + 1])\
                    .then_inc(signal["k_rounded"], 1)

            def round_queries(ph, n):
                s, i = n[1], number(n)
                reached(act, ph, "q_done", i + 1)
                for m in range(KC):
                    act.activation(q_parts[:, s, 0, m, :], ps_b[:, m * S:(m + 1) * S], ACT.Identity, bias=ph.bq[:, m:m + 1])\
                        .then_inc(signal["q_rounded"], 1)

            def copy_values(ph, n, c):
                s, i = n[1], number(n)
                first, size = ph.spans[c]
                reached(act, ph, "v_projected", ph.chunks * i + c + 1)
                reached(act, ph, "heads_summed", 2 * (i - 1))
                act.activation(values[0:size, s, c, :], ps_a[0:size, 0:D], ACT.Copy).then_inc(signal["v_ready"], 1)

            def exponentiate(ph, b, h):
                s, i = b[1], number(b)
                u, j = divmod(h, ph.per_unit)
                reached(act, ph, "maxed", ph.units * i + u + 1)
                if h % GROUP == 0:
                    if h >= P_RING:
                        reached(act, ph, "probs_turned", ph.fills * i + ph.chunks * ((h - P_RING) // GROUP + 1))
                    elif isinstance(i, int) and i == 0 and ph.prev:
                        reached(act, ph.prev, "probs_turned", ph.prev.fills * (B - 1) + ph.prev.chunks * ((h + P_RING) // GROUP + 1))
                    else:
                        reached(act, ph, "probs_turned", ph.fills * (i - 1) + ph.chunks * ((h + P_RING) // GROUP + 1))
                if ph.biased:
                    source, sign = biased[:, h % SB_RING, :], -1.0
                else:
                    source, sign = ps_scores[0:S, bank_of(s, u), j * ph.keys:(j + 1) * ph.keys], 1.0
                act.activation(probs[:, h % P_RING, 0:ph.keys], source, ACT.Exp, bias=neg_max[:, s, h:h + 1], scale=sign,
                               accum_out=sums[:, s, h:h + 1]).then_inc(signal["probs_ready"], 1)

            def copy_probs(ph, b, g, c):
                f, half = g * ph.chunks + c, g // 2
                first, size = ph.spans[c]
                if ph.by_dve[f]:
                    return
                reached(act, ph, "probs_turned", ph.fills * number(b) + f + 1)
                reached(act, ph, "heads_summed", 2 * (number(b) - 1) + half + 1)
                act.activation(probs_T[0:size, half, c, (g % 2) * GROUP:(g % 2 + 1) * GROUP, :],
                               ps_probs[0:size, f % 2, 0:GROUP * S].rearrange("p (h t) -> p h t", h=GROUP), ACT.Copy)\
                    .then_inc(signal["act_copied"], 1)

            def copy_inv(ph, b):
                reached(act, ph, "inv_turned", number(b) + 1)
                reached(act, ph, "heads_scaled", number(b))
                act.activation(inv_T[:, :], ps_a[:, 0:4 * S], ACT.Copy).then_inc(signal["inv_T_ready"], 1)

            def attend_step(ph, b, h):
                for n, f in due(ph, "copy_probs", b, h):
                    copy_probs(ph, n, f // ph.chunks, f % ph.chunks)
                for n, _ in due(ph, "copy_inv", b, h):
                    copy_inv(ph, n)
                for n, c in due(ph, "copy_values", b, h):
                    copy_values(ph, n, c)
                for n, _ in due(ph, "copy_xT", b, h):
                    copy_xT(ph, n)
                for n, m in due(ph, "round_keys", b, h):
                    round_keys(ph, n, m)
                for n, _ in due(ph, "round_queries", b, h):
                    round_queries(ph, n)
                for n, head in due(ph, "exponentiate", b, h):
                    exponentiate(ph, n, head)

            def attend(first, second):
                attentions(act, first, second, attend_step)

            act.wait_ge(constants, CONSTANTS)
            for c in range(DIST_CHUNKS):
                first, size = dist_span(c)
                act.wait_ge(dist_loaded[c % 2], 16 * (c // 2 + 1))
                act.activation(dist[:, c % 2, 0:size], dist[:, c % 2, 0:size], ACT.Ln, bias=tiny[:, :]).then_inc(logs_ready, 1)
            act.wait_ge(w_loaded, W_LOADED)
            act.wait_ge(q_scaled, Q_SCALED)
            attend(sa0, xa0)

            def ffn_scale(b):
                s, i = b[1], number(b)
                at_least(act, ffn["xq_turned"], i - 1)
                act.activation(xq[:, s, :], xn[:, i, :], ACT.Copy, scale=gamma[:, 2:3]).then_inc(ffn["xq_scaled"], 1)

            def ffn_step(work, b, h):
                for n, _ in due(work, "scale", b, h):
                    ffn_scale(n)

            act.wait_ge(ffn["gamma_inverse"], 2)
            rounds(act, ffn_work, ffn_step)
            attend(sa1, xa1)

            def copy_quad(q):
                i = number(q)
                act.wait_ge(moe["x_turned"], i + 1)
                at_least(act, moe["gated"], i)
                for k in range(KC):
                    act.activation(xT_quad[:, k, :], ps_scores[:, k, 0:QUAD * S], ACT.Copy).then_inc(moe["xT_ready"], 1)

            over_batches(act, copy_quad, pairs=QUADS // 2)
            act.wait_ge(moe["shifted"], 1)
            act.activation(exps[:, :, :], shifted[:, :, :], ACT.Exp).then_inc(moe["exp_ready"], 1)

            def copy_tile(t):
                s, i = t[1], number(t)
                act.wait_ge(moe["tile_turned"], i + 1)
                at_least(act, moe["up_done"], i - 1)
                act.activation(tile_T[:, s, :, :], ps_b[:, 0:D].rearrange("p (k t) -> p k t", k=KC), ACT.Copy)\
                    .then_inc(moe["tile_T_ready"], 1)

            def gelu(t):
                s, i = t[1], number(t)
                act.wait_ge(moe["up_done"], i + 1)
                at_least(act, moe["act_turned"], i - 1)
                act.activation(act_tile[:, s, :], ps_scores[:, s, 0:D], ACT.Gelu).then_inc(moe["gelu_done"], 1)

            def tile_step(work, b, h):
                for t, _ in due(work, "copy_T", b, h):
                    copy_tile(t)
                for t, _ in due(work, "gelu", b, h):
                    gelu(t)

            rounds(act, moe_tiles, tile_step)

        @block.vector
        def _(dve):
            dve.wait_ge(w_loaded, W_LOADED)
            dve.wait_ge(constants, CONSTANTS)
            for n in ("L1_attn_Wq", "L1_attn_Wk"):
                for k in range(KC):
                    for m in range(KC):
                        dve.tensor_copy(w_diag[n][:, k, m * P:(m + 1) * P].rearrange("p (f h) -> p f h", f=DH),
                                        on_diagonal[n][:, k, :].rearrange("p (h r f) -> p r f h", r=KC, f=DH)[:, m])\
                            .then_inc(columns_ordered, 1)
            dve.wait_ge(columns_ordered, 2 * KC * KC)
            scaled = [ph.q_scale for ph in phases] + [(ph.bq[:, :], ph.q_scale[1]) for ph in (sa0, xa0, xa1)]
            for tile, scale in scaled:
                dve.tensor_scalar(tile, tile, float(scale), None, ALU.mult).then_inc(q_scaled, 1)
            assert len(scaled) == Q_SCALED
            dve.scalar_tensor_tensor(neg_abs_ds[:, :], scaling[:, :], -1.0, scaling[:, :], ALU.mult, ALU.min).then_inc(ds_ready, 1)
            dve.wait_ge(ds_ready, 1)
            for c in range(DIST_CHUNKS):
                first, size = dist_span(c)
                dve.wait_ge(logs_ready, c + 1)
                dve.tensor_scalar(dist[:, c % 2, 0:size], dist[:, c % 2, 0:size], neg_abs_ds[:, :], None, ALU.mult)\
                    .then_inc(bias_scaled, 1)
            for i, (bv, ph) in enumerate(value_biases):
                dve.wait_ge(bv_out, i + 1)
                dve.tensor_tensor(ph.bo[:, :], ph.bo[:, :], ps_a[0:S, 0:D], ALU.add).then_inc(b_out_ready, 1)

            wf = w["L0_ffn_weight"][:, :, :].rearrange("p k n -> p (k n)")
            wt = w_tmp[:, :, :].rearrange("p k n -> p (k n)")
            dve.tensor_reduce(w_sum[:, :], wf, AX.X, ALU.add, apply_absolute_value=True).then_inc(ffn["w_sum"], 1)
            dve.wait_ge(ffn["w_total"], 1)
            dve.tensor_scalar(w_beta[:, 0:1], ps_b[:, 0:1], 1.0 / (D * D), None, ALU.mult).then_inc(ffn["w_mean"], 1)
            dve.wait_ge(ffn["w_mean"], 1)
            dve.tensor_scalar(w_beta[:, 1:2], w_beta[:, 0:1], FFN_EPS, None, ALU.add).then_inc(ffn["w_beta"], 1)
            dve.wait_ge(ffn["w_beta"], 1)
            dve.reciprocal(w_beta[:, 2:3], w_beta[:, 1:2]).then_inc(ffn["w_inverse"], 1)
            dve.wait_ge(ffn["w_inverse"], 1)
            dve.tensor_scalar(wt, wf, w_beta[:, 2:3], None, ALU.mult).then_inc(ffn["w_scaled"], 1)
            dve.wait_ge(ffn["w_scaled"], 1)
            dve.tensor_scalar(wf, wt, ROUND, -ROUND, ALU.add, ALU.add).then_inc(ffn["w_rounded"], 1)
            dve.wait_ge(ffn["w_rounded"], 1)
            dve.tensor_scalar(wf, wf, -1.0, 1.0, ALU.max, ALU.min).then_inc(ffn["w_ready"], 1)

            def state_stats(b, stats_ready, aggregated):
                apart(dve, aggregated, b)
                dve.bn_stats(state_stats_of[:, :], state[:, b, :]).then_inc(stats_ready, 1)

            def state_moments(b, stats_ready, aggregated, kept):
                at_least(dve, kept, b)
                apart(dve, stats_ready, b + 1)
                dve.bn_aggr(state_moments_of[:, :], state_stats_of[:, :]).then_inc(aggregated, 1)

            def keep_moments(b, aggregated, kept):
                dve.wait_ge(aggregated, b + 1)
                dve.tensor_scalar(all_moments[:, b, :], state_moments_of[:, :], 1.0, None, ALU.mult).then_inc(kept, 1)

            def maximum(ph, b, u):
                s, i = b[1], number(b)
                if ph.biased:
                    if u == 0:
                        arrived(dve, ph, "bias_loaded", b)
                    reached(dve, ph, "probs_ready", H * i + u - SB_RING + 1, own=True)
                reached(dve, ph, "scores_ready", ph.units * i + u + 1, alone=ph.biased)
                if ph.biased:
                    dve.tensor_tensor_reduce(biased[:, u % SB_RING, :], ps_scores[0:S, bank_of(s, u), 0:ph.keys], bias[:, s, :],
                                             -1.0, 3.0e38, ALU.add, ALU.min, neg_max[:, s, u:u + 1])\
                        .then_inc(signal["maxed"], 1)
                else:
                    dve.tensor_reduce(neg_max[:, s, u * ph.per_unit:(u + 1) * ph.per_unit],
                                      ps_scores[0:S, bank_of(s, u), 0:ph.per_unit * ph.keys]
                                      .rearrange("p (h k) -> p h k", h=ph.per_unit),
                                      AX.X, ALU.max, negate=True).then_inc(signal["maxed"], 1)

            def copy_probs(ph, b, g, c):
                f, half = g * ph.chunks + c, g // 2
                first, size = ph.spans[c]
                if not ph.by_dve[f]:
                    return
                reached(dve, ph, "probs_turned", ph.fills * number(b) + f + 1)
                reached(dve, ph, "heads_summed", 2 * (number(b) - 1) + half + 1)
                dve.tensor_copy(probs_T[0:size, half, c, (g % 2) * GROUP:(g % 2 + 1) * GROUP, :],
                                ps_probs[0:size, f % 2, 0:GROUP * S].rearrange("p (h t) -> p h t", h=GROUP))\
                    .then_inc(signal["dve_copied"], 1)

            def rest_of_keys(ph, n, m):
                s, i = n[1], number(n)
                reached(dve, ph, "k_rounded", KC * i + m + 1 if ph.cross else KC * (i + 1))
                reached(dve, ph, "k_split", KC * (i - 1) + m + 1)
                dve.scalar_tensor_tensor(k_rest[:, m, 0:ph.keys], k_place(ph, m), ph.bk[:, m:m + 1],
                                         k_part(ph, s, 0, m), ALU.add, ALU.subtract)\
                    .then_inc(signal["k_rest_ready"], 1)
                reached(dve, ph, "k_rest_ready", KC * i + m + 1)
                dve.tensor_copy(k_part(ph, s, 1, m), k_rest[:, m, 0:ph.keys]).then_inc(signal["k_second"], 1)

            def rest_of_queries(ph, n):
                s, i = n[1], number(n)
                reached(dve, ph, "q_split", i)
                reached(dve, ph, "q_rounded", KC * (i + 1))
                for m in range(KC):
                    dve.scalar_tensor_tensor(q_rest[:, m, :], ps_b[:, m * S:(m + 1) * S], ph.bq[:, m:m + 1],
                                             q_parts[:, s, 0, m, :], ALU.add, ALU.subtract)\
                        .then_inc(signal["q_rest_ready"], 1)
                reached(dve, ph, "q_rest_ready", KC * (i + 1))
                dve.tensor_copy(q_parts[:, s, 1, :, :], q_rest[:, :, :]).then_inc(signal["q_second"], 1)

            def invert(ph, b):
                s, i = b[1], number(b)
                reached(dve, ph, "probs_ready", H * (i + 1))
                dve.reciprocal(inv[:, :], sums[:, s, :]).then_inc(signal["inv_ready"], 1)
                reached(dve, ph, "inv_ready", i + 1)
                reached(dve, ph, "inv_turned", i)
                for parity in range(2):
                    rows = inv_wide[:, :, parity, :].rearrange("p a (j r f) -> p a j r f", j=4, r=2)[:, :, :, parity, :]
                    by_head = inv[:, :].rearrange("p (a j r) -> p a j r", a=2, j=4)[:, :, :, parity:parity + 1]
                    dve.tensor_copy(rows, by_head.to_broadcast([S, 2, 4, DH])).then_inc(signal["inv_wide_ready"], 1)

            def scale_heads(ph, b):
                i = number(b)
                reached(dve, ph, "heads_summed", 2 * (i + 1))
                reached(dve, ph, "inv_T_ready", i + 1)
                reached(dve, ph, "heads_ready", i)
                wide = heads_par[:, :, :, :].rearrange("p a r t -> p (a r t)")
                dve.tensor_tensor(wide, ps_heads[:, 0:4 * S], inv_T[:, :], ALU.mult).then_inc(signal["heads_scaled"], 1)
                reached(dve, ph, "heads_scaled", i + 1)
                reached(dve, ph, "out_projected", i)
                dve.tensor_tensor(heads_T[:, :, :], heads_par[:, :, 0, :], heads_par[:, :, 1, :], ALU.add)\
                    .then_inc(signal["heads_ready"], 1)

            def add_residual(ph, b):
                s, i = b[1], number(b)
                reached(dve, ph, "out_projected", i + 1)
                reached(dve, ph, "residual_ready", i + 1)
                reached(dve, ph, "state_ready", i)
                dve.tensor_tensor(y[:, :], ps_a[0:S, 0:D], x_res[:, s, :], ALU.add).then_inc(signal["y_ready"], 1)

            def take_stats(ph, b):
                reached(dve, ph, "y_ready", number(b) + 1)
                dve.bn_stats(stats[:, :], y[:, :]).then_inc(signal["stats_ready"], 1)

            def take_moments(ph, b):
                reached(dve, ph, "stats_ready", number(b) + 1, alone=True)
                dve.bn_aggr(moments[:, :], stats[:, :]).then_inc(signal["moments_ready"], 1)

            def guess_root(ph, b):
                i = number(b)
                reached(dve, ph, "moments_ready", i + 1)
                reached(dve, ph, "root_step", ROOT_STEPS * i)
                dve.tensor_scalar(root_in[:, :], moments[:, 1:2], LN_EPS, None, ALU.add).then_inc(signal["root_in_ready"], 1)
                reached(dve, ph, "root_in_ready", i + 1)
                dve.tensor_scalar(rstd[:, :].bitcast(I32), root_in[:, :].bitcast(I32), -0.5, ROOT_GUESS, ALU.mult, ALU.add)\
                    .then_inc(signal["guess_ready"], 1)

            def norm(ph, b):
                i = number(b)
                reached(dve, ph, "root_step", ROOT_STEPS * (i + 1))
                dve.tensor_scalar(state[:, i, :], y[:, :], moments[:, 0:1], rstd[:, :], ALU.subtract, ALU.mult)\
                    .then_inc(signal["state_ready"], 1)

            def attend_step(ph, b, h):
                for n, u in due(ph, "maximum", b, h):
                    maximum(ph, n, u)
                for n, f in due(ph, "copy_probs", b, h):
                    copy_probs(ph, n, f // ph.chunks, f % ph.chunks)
                for n, _ in due(ph, "invert", b, h):
                    invert(ph, n)
                for n, _ in due(ph, "scale_heads", b, h):
                    scale_heads(ph, n)
                for n, m in due(ph, "rest_of_keys", b, h):
                    rest_of_keys(ph, n, m)
                for n, _ in due(ph, "rest_of_queries", b, h):
                    rest_of_queries(ph, n)
                for n, _ in due(ph, "add_residual", b, h):
                    add_residual(ph, n)
                for n, _ in due(ph, "take_stats", b, h):
                    take_stats(ph, n)
                for n, _ in due(ph, "take_moments", b, h):
                    take_moments(ph, n)
                for n, _ in due(ph, "guess_root", b, h):
                    guess_root(ph, n)
                for n, _ in due(ph, "norm", b, h):
                    norm(ph, n)
                for n, _ in due(ph, "next_stats", b, h):
                    reached(dve, ph, "state_ready", number(n) + 1)
                    state_stats(number(n), ffn["x_stats"], ffn["x_aggregated"])
                for n, _ in due(ph, "next_moments", b, h):
                    state_moments(number(n), ffn["x_stats"], ffn["x_aggregated"], ffn["x_moments"])
                for n, _ in due(ph, "keep_moments", b, h):
                    keep_moments(number(n), ffn["x_aggregated"], ffn["x_moments"])

            def attend(first, second):
                attentions(dve, first, second, attend_step)

            def guess(root_in_ready, count, guess_ready, variance, eps, value, result):
                dve.tensor_scalar(value, variance, eps, None, ALU.add).then_inc(root_in_ready, 1)
                dve.wait_ge(root_in_ready, count)
                dve.tensor_scalar(result.bitcast(I32), value.bitcast(I32), -0.5, ROOT_GUESS, ALU.mult, ALU.add)\
                    .then_inc(guess_ready, 1)

            attend(sa0, xa0)

            reached(dve, xa0, "state_ready", B)

            dve.wait_ge(ffn["x_moments"], B)
            guess(ffn["x_root_in"], 1, ffn["x_guess"], all_moments[:, :, 1], FFN_LN_EPS, all_root_in[:, :], all_rstd[:, :])
            dve.wait_ge(ffn["x_root_step"], ROOT_STEPS)

            def center(b):
                dve.scalar_tensor_tensor(xn[:, b, :], state[:, b, :], all_moments[:, b, 0:1], ffn_gamma[:, :], ALU.subtract,
                                         ALU.mult).then_inc(ffn["gained"], 1)

            def normalise(b):
                dve.wait_ge(ffn["gained"], b + 1)
                dve.scalar_tensor_tensor(xn[:, b, :], xn[:, b, :], all_rstd[:, bass.ds(b, 1)], ffn_beta[:, :], ALU.mult,
                                         ALU.add).then_inc(ffn["xn_ready"], 1)

            with dve.Fori(0, QUADS) as q:
                for j in range(QUAD):
                    center(q * QUAD + j)
                for j in range(QUAD):
                    normalise(q * QUAD + j)
            dve.wait_ge(ffn["xn_ready"], B)
            dve.tensor_reduce(row_max[:, :], xn.rearrange("p b d -> p (b d)"), AX.X, ALU.max, apply_absolute_value=True)\
                .then_inc(ffn["row_max"], 1)
            dve.wait_ge(ffn["max_turned"], 1)
            dve.tensor_reduce(max_one[:, :], ps_a[0:1, 0:S], AX.X, ALU.max).then_inc(ffn["max_one"], 1)
            dve.wait_ge(ffn["max_spread"], 1)
            dve.tensor_copy(gamma[:, 0:1], ps_a[0:S, 0:1]).then_inc(ffn["gamma_ready"], 1)
            dve.wait_ge(ffn["gamma_ready"], 1)
            dve.reciprocal(gamma[:, 1:2], gamma[:, 0:1]).then_inc(ffn["gamma_inverse"], 1)
            dve.wait_ge(ffn["gamma_inverse"], 1)
            dve.tensor_scalar(gamma[:, 2:3], gamma[:, 1:2], QB, None, ALU.mult).then_inc(ffn["gamma_inverse"], 1)
            dve.tensor_scalar(gain[:, 0:1], gamma[:, 0:1], w_beta[0:S, 0:1], 1.0 / QB, ALU.mult, ALU.mult)\
                .then_inc(ffn["gain_ready"], 1)
            dve.wait_ge(ffn["gain_ready"], 1)
            dve.wait_ge(ffn["gamma_inverse"], 1)

            def ffn_clip(b):
                s, i = b[1], number(b)
                dve.wait_ge(ffn["xq_turned"], i + 1)
                at_least(dve, ffn["projected"], i - 1)
                dve.tensor_scalar(xqT[:, s, :, :], ps_probs[:, s, 0:KC * S].rearrange("p (k t) -> p k t", k=KC),
                                  -QB + FFN_EPS, QB - FFN_EPS, ALU.max, ALU.min).then_inc(ffn["xqT_ready"], 1)

            def ffn_add(b):
                s, i = b[1], number(b)
                dve.wait_ge(ffn["projected"], i + 1)
                dve.scalar_tensor_tensor(state[:, i, :], ps_scores[0:S, s, 0:D], gain[:, 0:1], state[:, i, :], ALU.mult, ALU.add)\
                    .then_inc(ffn["y_ready"], 1)

            def ffn_step(work, b, h):
                for n, _ in due(work, "clip", b, h):
                    ffn_clip(n)
                for n, _ in due(work, "add", b, h):
                    ffn_add(n)
                for n, _ in due(work, "take_stats", b, h):
                    dve.wait_ge(ffn["y_ready"], number(n) + 1)
                    state_stats(number(n), ffn["y_stats"], ffn["y_aggregated"])
                for n, _ in due(work, "take_moments", b, h):
                    state_moments(number(n), ffn["y_stats"], ffn["y_aggregated"], ffn["y_moments"])
                for n, _ in due(work, "keep_moments", b, h):
                    keep_moments(number(n), ffn["y_aggregated"], ffn["y_moments"])

            rounds(dve, ffn_work, ffn_step)
            dve.wait_ge(ffn["y_moments"], B)
            guess(ffn["y_root_in"], 1, ffn["y_guess"], all_moments[:, :, 1], LN_EPS, all_root_in[:, :], all_rstd[:, :])
            dve.wait_ge(ffn["y_root_step"], ROOT_STEPS)

            def ffn_out(b):
                dve.tensor_scalar(state[:, b, :], state[:, b, :], all_moments[:, b, 0:1], all_rstd[:, bass.ds(b, 1)],
                                  ALU.subtract, ALU.mult).then_inc(ffn["state_ready"], 1)

            with dve.Fori(0, QUADS) as q:
                for j in range(QUAD):
                    ffn_out(q * QUAD + j)
            attend(sa1, xa1)

            def keep_logits(q):
                i = number(q)
                dve.wait_ge(moe["gated"], i + 1)
                dve.tensor_scalar(logits[:, bass.ds(i * QUAD, QUAD), :],
                                  ps_heads[0:S, 0:QUAD * E].rearrange("p (b e) -> p b e", b=QUAD), 1.0, None, ALU.mult)\
                    .then_inc(moe["logits_ready"], 1)

            over_batches(dve, keep_logits, pairs=QUADS // 2)

            def per_token(t):
                return t[:, :].rearrange("p (b a) -> p b a", a=1).to_broadcast([S, B, E])

            dve.wait_ge(moe["logits_ready"], QUADS)
            dve.tensor_reduce(top[:, :], logits[:, :, :], AX.X, ALU.max).then_inc(moe["top_ready"], 1)
            dve.wait_ge(moe["top_ready"], 1)
            dve.tensor_tensor(shifted[:, :, :], logits[:, :, :], per_token(top), ALU.subtract).then_inc(moe["shifted"], 1)
            dve.tensor_tensor(rank[:, :, :], logits[:, :, :], per_token(top), ALU.is_ge).then_inc(moe["top_found"], 1)
            dve.wait_ge(moe["exp_ready"], 1)
            dve.tensor_reduce(top_weight[:, :], exps[:, :, :], AX.X, ALU.add).then_inc(moe["sum_ready"], 1)
            dve.wait_ge(moe["top_found"], 1)
            by_expert = rank_of[:, :].rearrange("p (a e) -> p a e", a=1).to_broadcast([S, B, E])
            dve.tensor_tensor(hot[:, :, :], rank[:, :, :], by_expert, ALU.mult).then_inc(moe["rank_ready"], 1)
            dve.wait_ge(moe["sum_ready"], 1)
            dve.reciprocal(top_weight[:, :], top_weight[:, :]).then_inc(moe["weight_ready"], 1)
            dve.wait_ge(moe["rank_ready"], 1)
            dve.tensor_reduce(top[:, :], hot[:, :, :], AX.X, ALU.max).then_inc(moe["first_ready"], 1)
            dve.wait_ge(moe["first_ready"], 1)
            dve.tensor_tensor(hot[:, :, :], hot[:, :, :], per_token(top), ALU.is_equal).then_inc(moe["hot_found"], 1)

            dve.wait_ge(moe["counted"], 1)
            in_batch = ps_a[0:S, 0:B * E].rearrange("p (b e) -> p b e", b=B)
            dve.tensor_copy(prefix[:, 0], in_batch).then_inc(moe["prefixed"], 2)
            for n in range(B.bit_length() - 1):
                ahead, now, then = 2 ** n, prefix[:, n % 2], prefix[:, (n + 1) % 2]
                dve.wait_ge(moe["prefixed"], 2 * (n + 1))
                dve.tensor_tensor(then[:, ahead:, :], now[:, ahead:, :], now[:, 0:B - ahead, :], ALU.add)\
                    .then_inc(moe["prefixed"], 1)
                dve.tensor_copy(then[:, 0:ahead, :], now[:, 0:ahead, :]).then_inc(moe["prefixed"], 1)
            up_to = prefix[:, (B.bit_length() - 1) % 2]
            dve.wait_ge(moe["prefixed"], 2 * B.bit_length())
            full, end = room[:, 0, :], room_tmp[:, 0, :]
            dve.tensor_scalar(full, up_to[:, B - 1, :], float(P - 1), 1.0 / P, ALU.add, ALU.mult).then_inc(moe["routed"], 1)
            dve.wait_ge(moe["routed"], 1)
            dve.tensor_scalar(full, full, -(P - 1) / (2.0 * P), ROUND, ALU.add, ALU.add).then_inc(moe["routed"], 1)
            dve.wait_ge(moe["routed"], 2)
            dve.tensor_scalar(full, full, -ROUND, float(P), ALU.add, ALU.mult).then_inc(moe["routed"], 1)
            dve.wait_ge(moe["routed"], 3)
            dve.tensor_copy(end, full).then_inc(moe["routed"], 1)
            for n in range(E.bit_length() - 1):
                ahead, now, then = 2 ** n, room_tmp[:, n % 2, :], room_tmp[:, (n + 1) % 2, :]
                dve.wait_ge(moe["routed"], 4 + 2 * n)
                dve.tensor_tensor(then[:, ahead:], now[:, ahead:], now[:, 0:E - ahead], ALU.add).then_inc(moe["routed"], 1)
                dve.tensor_copy(then[:, 0:ahead], now[:, 0:ahead]).then_inc(moe["routed"], 1)
            end = room_tmp[:, (E.bit_length() - 1) % 2, :]
            routed = 4 + 2 * (E.bit_length() - 1)
            dve.wait_ge(moe["routed"], routed)
            start = room[:, 1, :]
            dve.tensor_tensor(start, end, full, ALU.subtract).then_inc(moe["routed"], 1)
            each = [1, TILES, E]
            dve.tensor_tensor(passed_by[:, :, :], tile_first[:, :].rearrange("p (t a) -> p t a", a=1).to_broadcast(each),
                              end[0:1].rearrange("p (a e) -> p a e", a=1).to_broadcast(each), ALU.is_ge).then_inc(moe["routed"], 1)
            dve.tensor_tensor(place[:, :, :], up_to, in_batch, ALU.subtract).then_inc(moe["routed"], 1)
            dve.wait_ge(moe["routed"], routed + 3)
            dve.tensor_reduce(tile_expert[:, :], passed_by[:, :, :], AX.X, ALU.add).then_inc(moe["routed"], 1)
            dve.tensor_tensor(place[:, :, :], place[:, :, :], ps_b[0:S, 0:B * E].rearrange("p (b e) -> p b e", b=B), ALU.add)\
                .then_inc(moe["routed"], 1)
            dve.wait_ge(moe["routed"], routed + 5)
            dve.tensor_scalar(tile_expert_i[:, :], tile_expert[:, :], float(E - 1), None, ALU.min).then_inc(moe["experts_known"], 1)
            dve.tensor_tensor(place[:, :, :], place[:, :, :],
                              start.rearrange("p (a e) -> p a e", a=1).to_broadcast([S, B, E]), ALU.add).then_inc(moe["routed"], 1)
            dve.wait_ge(moe["routed"], routed + 6)
            dve.tensor_tensor(place[:, :, :], place[:, :, :], hot[:, :, :], ALU.mult).then_inc(moe["routed"], 1)
            dve.wait_ge(moe["routed"], routed + 7)
            dve.tensor_reduce(slot_of[:, :], place[:, :, :], AX.X, ALU.add).then_inc(moe["placed"], 1)
            dve.wait_ge(moe["placed"], 1)

            def put(b):
                s, i = b[1], number(b)
                at_least(dve, scattered[s], 16 * b[0])
                dve.tensor_scalar(slot_now[:, s:s + 1], slot_of[:, bass.ds(i, 1)], 1.0, None, ALU.mult).then_inc(moe["put"], 1)
                dve.tensor_scalar(x_out[:, s, :], state[:, i, :], 1.0, None, ALU.mult).then_inc(moe["put"], 1)

            over_batches(dve, put)

            def copy_act(t):
                s, i = t[1], number(t)
                dve.wait_ge(moe["act_turned"], i + 1)
                at_least(dve, moe["down_done"], i - 1)
                dve.tensor_copy(act_T[:, s, :, :], ps_probs[:, s, 0:D].rearrange("p (k t) -> p k t", k=KC))\
                    .then_inc(moe["act_T_ready"], 1)

            def keep_tile(t):
                s, i = t[1], number(t)
                dve.wait_ge(moe["down_done"], i + 1)
                at_least(dve, tile_stored[s], 16 * t[0])
                dve.tensor_copy(y_tile[:, s, :], (ps_heads if s else ps_a)[:, 0:D]).then_inc(moe["tile_kept"], 1)

            def tile_step(work, b, h):
                for t, _ in due(work, "copy_act_T", b, h):
                    copy_act(t)
                for t, _ in due(work, "keep", b, h):
                    keep_tile(t)

            rounds(dve, moe_tiles, tile_step)

            def place_batch(b):
                s, i = b[1], number(b)
                at_least(dve, fetched[s], 16 * b[0])
                dve.tensor_scalar(slot_now[:, s:s + 1], slot_of[:, bass.ds(i, 1)], 1.0, None, ALU.mult)\
                    .then_inc(moe["slot_placed"], 1)

            def add_experts(b):
                s, i = b[1], number(b)
                dve.wait_ge(fetched[s], 16 * (b[0] + 1))
                dve.scalar_tensor_tensor(state[:, i, :], y_in[:, s, :], top_weight[:, bass.ds(i, 1)], state[:, i, :], ALU.mult,
                                         ALU.add).then_inc(moe["added"], 1)

            def fetch_step(work, b, h):
                for n, _ in due(work, "place", b, h):
                    place_batch(n)
                for n, _ in due(work, "add", b, h):
                    add_experts(n)
                for n, _ in due(work, "take_stats", b, h):
                    dve.wait_ge(moe["added"], number(n) + 1)
                    state_stats(number(n), moe["y_stats"], moe["y_aggregated"])
                for n, _ in due(work, "take_moments", b, h):
                    state_moments(number(n), moe["y_stats"], moe["y_aggregated"], moe["y_moments"])
                for n, _ in due(work, "keep_moments", b, h):
                    keep_moments(number(n), moe["y_aggregated"], moe["y_moments"])

            for s in range(2):
                dve.wait_ge(scattered[s], 16 * PAIRS)
            rounds(dve, moe_fetch, fetch_step)
            dve.wait_ge(moe["y_moments"], B)
            guess(moe["y_root_in"], 1, moe["y_guess"], all_moments[:, :, 1], LN_EPS, all_root_in[:, :], all_rstd[:, :])
            dve.wait_ge(moe["y_root_step"], ROOT_STEPS)
            with dve.Fori(0, QUADS) as q:
                for j in range(QUAD):
                    b = q * QUAD + j
                    dve.tensor_scalar(state[:, b, :], state[:, b, :], all_moments[:, b, 0:1], all_rstd[:, bass.ds(b, 1)],
                                      ALU.subtract, ALU.mult).then_inc(moe["out_ready"], 1)

        @block.gpsimd
        def _(pool):
            pool.memset(zeros, 0.0).then_inc(moe["cleared"], 1)
            for t in on_diagonal.values():
                pool.memset(t[:, :, :], 0.0).then_inc(diag_cleared, 1)
            pool.memset(ident[:, :], 0.0).then_inc(constants, 1)
            pool.memset(ones[:, :], 1.0).then_inc(constants, 1)
            pool.memset(b_zero[:, :], 0.0).then_inc(constants, 1)
            pool.memset(tiny[:, :], 1e-9).then_inc(constants, 1)
            pool.memset(inv_wide[:, :, :, :], 0.0).then_inc(constants, 1)
            for e in range(E):
                pool.memset(rank_of[:, e:e + 1], float(E - e)).then_inc(constants, 1)
            for t in range(TILES):
                pool.memset(tile_first[:, t:t + 1], float(t * P)).then_inc(constants, 1)
            pool.memset(below[:, :], 1.0).then_inc(constants, 1)
            pool.wait_ge(constants, CONSTANTS - 2)
            pool.affine_select(out=below[:, :], in_=below[:, :], compare_op=ALU.is_gt, fill=0.0, base=0,
                               pattern=[[1, S]], channel_multiplier=-1).then_inc(constants, 1)
            pool.affine_select(out=ident[:, :], in_=ident[:, :], compare_op=ALU.not_equal, fill=1.0, base=0,
                               pattern=[[-1, P]], channel_multiplier=1).then_inc(constants, 1)

            def third_of_keys(ph, n, m):
                s, i = n[1], number(n)
                reached(pool, ph, "k_second", KC * i + m + 1)
                pool.tensor_tensor(k_part(ph, s, 2, m), k_rest[:, m, 0:ph.keys], k_part(ph, s, 1, m),
                                   ALU.subtract).then_inc(signal["k_split"], 1)

            def third_of_queries(ph, n):
                s, i = n[1], number(n)
                reached(pool, ph, "q_second", i + 1)
                pool.tensor_tensor(q_parts[:, s, 2, :, :], q_rest[:, :, :], q_parts[:, s, 1, :, :], ALU.subtract)\
                    .then_inc(signal["q_split"], 1)

            def residual(ph, n):
                s, i = n[1], number(n)
                reached(pool, ph, "y_ready", i - 1, alone=True)
                if ph.prev:
                    reached(pool, ph.prev, "state_ready", i + 1, alone=True)
                first = pool.tensor_tensor(x_res[:, s, :], state[:, i, :], ph.bo[:, :], ALU.add)
                if ph.twice:
                    first.then_inc(signal["residual_once"], 1)
                    reached(pool, ph, "residual_once", i + 1, alone=True)
                    first = pool.tensor_tensor(x_res[:, s, :], x_res[:, s, :], state[:, i, :], ALU.add)
                first.then_inc(signal["residual_ready"], 1)

            def root(ph, b):
                i = number(b)
                reached(pool, ph, "guess_ready", i + 1)
                inverse_root(pool, signal["root_step"], ph.base["root_step"] + ROOT_STEPS * i, root_in[:, :], root_tmp[:, :], rstd[:, :])

            def attend_step(ph, b, h):
                for n, _ in due(ph, "root", b, h):
                    root(ph, n)
                for n, _ in due(ph, "residual", b, h):
                    residual(ph, n)
                for n, m in due(ph, "third_of_keys", b, h):
                    third_of_keys(ph, n, m)
                for n, _ in due(ph, "third_of_queries", b, h):
                    third_of_queries(ph, n)

            def attend(first, second):
                attentions(pool, first, second, attend_step)

            pool.wait_ge(b_out_ready, len(value_biases))
            pool.wait_ge(state_loaded, 16)
            attend(sa0, xa0)

            pool.wait_ge(ffn["x_guess"], 1)
            inverse_root(pool, ffn["x_root_step"], 0, all_root_in[:, :], all_root_tmp[:, :], all_rstd[:, :])
            pool.wait_ge(ffn["y_guess"], 1)
            inverse_root(pool, ffn["y_root_step"], 0, all_root_in[:, :], all_root_tmp[:, :], all_rstd[:, :])
            attend(sa1, xa1)
            pool.wait_ge(moe["x_cleared"], 16)

            def scatter(b):
                s, i = b[1], number(b)
                apart(pool, moe["put"], 2 * (i + 1))
                pool.indirect_dma_start(x_sorted, bass.IndirectOffsetOnAxis(ap=slot_now[:, s:s + 1], axis=0), x_out[:, s, :], None)\
                    .then_inc(scattered[s], 16)

            over_batches(pool, scatter)
            for s in range(2):
                pool.wait_ge(tile_stored[s], 16 * (TILES // 2))

            def fetch(b):
                s, i = b[1], number(b)
                at_least(pool, moe["added"], i - 1)
                apart(pool, moe["slot_placed"], i + 1)
                pool.indirect_dma_start(y_in[:, s, :], None, y_sorted, bass.IndirectOffsetOnAxis(ap=slot_now[:, s:s + 1], axis=0))\
                    .then_inc(fetched[s], 16)

            def fetch_step(work, b, h):
                for n, _ in due(work, "fetch", b, h):
                    fetch(n)

            rounds(pool, moe_fetch, fetch_step)
            pool.wait_ge(moe["y_guess"], 1)
            inverse_root(pool, moe["y_root_step"], 0, all_root_in[:, :], all_root_tmp[:, :], all_rstd[:, :])


TURNED = ("L0_attn_w_qkv", "L0_attn_w_o", "L0_xattn_Wq", "L0_xattn_Wk", "L0_xattn_Wv", "L0_xattn_Wo",
          "L1_attn_Wq", "L1_attn_Wk", "L1_attn_Wv", "L1_attn_W_out")
COLUMNS = ("b_v", "L0_xattn_bv", "L1_xattn_bv")
STACKED = ("L0_attn_b_qkv", "L0_xattn_bq", "L0_xattn_bk", "L1_xattn_bq", "L1_xattn_bk")
ORDERED = ("L0_attn_w_qkv", "L0_xattn_Wq", "L0_xattn_Wk", "L1_xattn_Wq", "L1_xattn_Wk")
NAMES = ("x", "ctx_1024", "fside_BxSxS2_0", "L0_attn_w_qkv", "L0_attn_b_qkv", "L0_attn_w_o", "L0_attn_b_o", "L0_xattn_Wq",
         "L0_xattn_bq", "L0_xattn_Wk", "L0_xattn_bk", "L0_xattn_Wv", "L0_xattn_bv", "L0_xattn_Wo", "L0_xattn_bo",
         "L0_xattn_distance_scaling", "L0_ffn_weight", "L0_ffn_ln_gamma", "L0_ffn_ln_beta", "L1_attn_Wq", "L1_attn_Wk",
         "L1_attn_Wv", "L1_attn_W_out", "L1_attn_b_out", "L1_xattn_Wq", "L1_xattn_bq", "L1_xattn_Wk", "L1_xattn_bk",
         "L1_xattn_Wv", "L1_xattn_bv", "L1_xattn_Wo", "L1_xattn_bo", "L1_ffn_Wg", "L1_ffn_bg", "L1_ffn_W1", "L1_ffn_b1",
         "L1_ffn_W2", "L1_ffn_b2", "b_v")


def kernel(**inputs):
    from concourse import bacc
    from concourse.bass_utils import run_bass_kernel_spmd

    nc = bacc.Bacc("TRN2", target_bir_lowering=False, num_devices=1)
    arrays, d = {}, {}
    for name in NAMES:
        a = np.asarray(inputs["L0_attn_b_qkv"][2 * D:] if name == "b_v" else inputs[name])
        if name in TURNED:
            a = a.T
        if name in COLUMNS:
            a = np.moveaxis(a.reshape(*a.shape[:-1], -1, P), -1, 0)
        if name in STACKED:
            a = a.reshape(-1, H // KC, KC, DH).transpose(3, 1, 0, 2).reshape(P, -1)
        if name in ORDERED:
            n = 2 * D if name == "L0_attn_w_qkv" else D
            turned = a[:, 0:n].reshape(D, -1, H // KC, KC, DH).transpose(0, 1, 3, 4, 2).reshape(D, n)
            a = np.concatenate([turned, a[:, n:]], axis=1)
        if name == "ctx_1024":
            a = a.transpose(0, 2, 1)
        a = np.ascontiguousarray(a if a.ndim else a.reshape(1))
        arrays["in_" + name] = a
        d[name] = nc.dram_tensor("in_" + name, a.shape, mybir.dt.from_np(a.dtype), kind="ExternalInput").ap()
    out = nc.dram_tensor("out", (B, S, D), F32, kind="ExternalOutput").ap()
    decoder(nc, d, out)
    return run_bass_kernel_spmd(nc, [arrays], core_ids=[0]).results[0]["out"]
```

```python
from contextlib import ExitStack

import concourse.bass as bass
from concourse import mybir
import numpy as np

F32 = mybir.dt.float32
BF16 = mybir.dt.bfloat16
I32 = mybir.dt.int32
ACT = mybir.ActivationFunctionType
ALU = mybir.AluOpType
AX = mybir.AxisListType

B, S, D, H, SK, E = 32, 100, 256, 16, 361, 8
DH = D // H
P = 128
KC = D // P
TERMS = 3
PRODUCTS = [(0, 3), (1, 2), (2, 1)]
BLOCKS = sum(n for _, n in PRODUCTS)
STACK = BLOCKS * DH
GROUP = 4
P_RING = 8
S_RING = 3
SB_RING = 4
LN_EPS = 1e-5
FFN_LN_EPS = 1e-3
FFN_EPS = 1e-5
QB = 128.0
QUAD = 4
QUADS = B // QUAD
WAVE = 8
WAVES = B // WAVE
TILES = (B * S + E * (P - 1)) // P
ROWS = TILES * P
ROUND = 1.5 * 2.0 ** 23
ROOT_GUESS = float(0x5F3759DF)
ROOT_STEPS = 3 * 4
DIST = B * S * SK // P
PAIRS = B // 2
WORK = 22400
CONSTANTS = 8 + E + TILES
Q_SCALED = 6
W_LOADED = 16 * 4

PACKS = {
    "weights": ("L0_attn_w_o", "L0_xattn_Wq", "L0_xattn_Wk", "L0_xattn_Wv", "L0_xattn_Wo", "L0_ffn_weight", "L1_attn_W_out",
                "L1_xattn_Wq", "L1_xattn_Wk", "L1_xattn_Wv", "L1_xattn_Wo"),
    "columns": ("b_v", "L0_xattn_bq", "L0_xattn_bk", "L0_xattn_bv", "L1_xattn_bq", "L1_xattn_bk", "L1_xattn_bv"),
    "rows": ("L0_attn_b_o", "L0_xattn_bo", "L1_attn_b_out", "L1_xattn_bo", "L0_ffn_ln_gamma", "L0_ffn_ln_beta", "L1_ffn_bg")}

PLAN_SELF = {
    "turn_x": [-39], "copy_xT": [-36], "keys": [-34, -34], "round_keys": [-32, -31], "rest_of_keys": [-30, -29],
    "queries": [-27], "round_queries": [-25], "rest_of_queries": [-24], "third_of_keys": [-28, -27],
    "third_of_queries": [-22], "values": [-7], "copy_values": [-2], "residual": [12], "scores": [0, 4, 8, 12],
    "maximum": [2, 6, 10, 14], "exponentiate": [4, 5, 6, 7, 8, 9, 10, 11, 12, 13, 14, 15, 16, 17, 18, 19],
    "turn_probs": [10, 14, 18, 22], "copy_probs": [13, 16, 21, 25], "sum_heads": [19, 27], "invert": [20],
    "turn_inv": [24], "copy_inv": [24], "scale_heads": [30], "project": [34], "add_residual": [35],
    "take_stats": [37], "take_moments": [39], "guess_root": [39], "root": [39], "norm": [46]}
PLAN_BIASED = {
    "turn_x": [-31], "copy_xT": [-31], "keys": [-29, -24], "round_keys": [-28, -23], "rest_of_keys": [-27, -22],
    "queries": [-19], "round_queries": [-19], "rest_of_queries": [-18], "third_of_keys": [-25, -20],
    "third_of_queries": [-17], "values": [-10, -8, -6], "copy_values": [-9, -7, -5], "residual": [9],
    "scores": [0, 1, 2, 3, 4, 5, 6, 7, 8, 9, 10, 11, 12, 13, 14, 15],
    "maximum": [0, 1, 2, 3, 4, 5, 6, 7, 8, 9, 10, 11, 12, 13, 14, 15],
    "exponentiate": [1, 2, 3, 4, 5, 6, 7, 8, 9, 10, 11, 12, 13, 14, 15, 16],
    "turn_probs": [6, 7, 8, 10, 11, 12, 14, 15, 16, 18, 18, 20],
    "copy_probs": [6, 7, 8, 10, 11, 12, 14, 15, 16, 18, 19, 20], "sum_heads": [16, 21], "invert": [18],
    "turn_inv": [20], "copy_inv": [21], "scale_heads": [21], "project": [30], "add_residual": [32],
    "take_stats": [32], "take_moments": [34], "guess_root": [35], "root": [36], "norm": [40]}
PLAN_CROSS = {
    "turn_x": [-31], "copy_xT": [-31], "keys": [-30, -24], "round_keys": [-27, -22], "rest_of_keys": [-27, -22],
    "queries": [-20], "round_queries": [-18], "rest_of_queries": [-18], "third_of_keys": [-26, -21],
    "third_of_queries": [-16], "values": [-10, -8, -6], "copy_values": [-9, -7, -5], "residual": [9],
    "scores": [0, 1, 2, 3, 4, 5, 6, 7, 8, 9, 10, 11, 12, 13, 14, 15],
    "maximum": [0, 1, 2, 3, 4, 5, 6, 7, 7, 9, 10, 11, 12, 13, 14, 15],
    "exponentiate": [1, 2, 3, 4, 5, 6, 7, 8, 9, 10, 11, 12, 13, 14, 15, 16],
    "turn_probs": [6, 8, 8, 10, 11, 12, 14, 15, 16, 18, 19, 20],
    "copy_probs": [7, 8, 9, 11, 12, 13, 15, 15, 17, 19, 20, 21], "sum_heads": [15, 22], "invert": [17],
    "turn_inv": [20], "copy_inv": [21], "scale_heads": [24], "project": [29], "add_residual": [29],
    "take_stats": [31], "take_moments": [32], "guess_root": [36], "root": [34], "norm": [40]}
PLAN_NEXT = {
    "next_scale": [44], "next_gain": [43], "next_max": [57], "next_store": [48]}
PREPARE = 15
LAG = 6
FFN_STEPS = 6
PLAN_FFN = {"scale": [-10], "turn": [-7], "clip": [-4], "project": [-1], "add": [3], "take_stats": [8],
            "take_moments": [9], "keep_moments": [14]}

TILE_STEPS = 8
PLAN_TILES = {"turn": [-13], "copy_T": [-11], "weights": [-11], "up": [-5], "gelu": [-4, -4], "down": [4], "keep": [7]}


def at_least(eng, sem, value):
    if isinstance(value, int) and value <= 0:
        return
    eng.wait_ge(sem, value)


class Steps:

    def __init__(self, plan, steps):
        self.plan, self.steps = plan, steps


class Attention:

    def __init__(self, keys, cross, wq, wk, wv, wo, bq, bk, bo, q_scale, biased, twice):
        self.keys, self.cross, self.biased = keys, cross, biased
        self.wq, self.wk, self.wv, self.wo = wq, wk, wv, wo
        self.bq, self.bk, self.bo, self.q_scale = bq, bk, bo, q_scale
        self.twice = twice
        self.chunks = -(-keys // P)
        size = -(-keys // self.chunks)
        self.spans = [(c * size, min(size, keys - c * size)) for c in range(self.chunks)]
        self.per_unit = GROUP if GROUP * keys <= 512 else 1
        self.units = H // self.per_unit
        self.fills = (H // GROUP) * self.chunks
        self.by_dve = [self.chunks == 1 or f % self.chunks == 1 or f == self.chunks + 2 for f in range(self.fills)]
        self.plan = (PLAN_BIASED if biased else PLAN_CROSS) if cross else PLAN_SELF
        self.norms = 1 + biased
        if biased:
            self.plan = self.plan | PLAN_NEXT
        self.steps = H
        self.prev = self.next = None
        self.base = {}


def decoder(nc, d, out):
    ctx = ExitStack()

    def sb(name, shape, dt=F32):
        return ctx.enter_context(nc.sbuf_tensor(name, shape, dt))

    def sem(name):
        return ctx.enter_context(nc.semaphore(name))

    with ctx:
        state = sb("state", [S, B, D])
        ident = sb("ident", [P, P])
        ones = sb("ones", [P, P])
        tiny = sb("tiny", [P, 1])
        scaling = sb("scaling", [P, 1])
        neg_abs_ds = sb("neg_abs_ds", [P, 1])

        work = sb("work", [P, WORK])

        def carve(sizes):
            ends = [sum(sizes[:i + 1]) for i in range(len(sizes))]
            assert ends[-1] <= WORK
            return [work[:, e - n:e] for e, n in zip(ends, sizes)]

        k_stack, probs, probs_T, k_parts, ctxT_biased, k_rest, values, q_stack = carve(
            [H * SK, P_RING * SK, 2 * 3 * 2 * GROUP * S, TERMS * KC * SK, 2 * KC * SK + SB_RING * SK, KC * SK,
             2 * 3 * D, H * S])
        ctxT, biased = ctxT_biased[:, 0:2 * KC * SK], ctxT_biased[:, 2 * KC * SK:]
        zeros = k_stack[:, H * SK - D:]
        used = 2 * GROUP * S
        places = [ctxT_biased, k_stack[:, H * S // 2:H * SK // 2], k_stack[:, (H * SK + H * S) // 2:H * SK - D],
                  probs_T[:, used:3 * used], probs_T[:, 4 * used:]]
        ends = [min(DIST, sum(p.shape[1] for p in places[:i + 1])) for i in range(len(places))]
        assert ends[-1] == DIST
        dist = [(first, end - first, p[:, 0:end - first]) for first, end, p in zip([0] + ends, ends, places)]
        k_stack = k_stack[0:STACK].bitcast(BF16).rearrange("p (s n) -> p s n", s=2)
        probs = probs[0:S].rearrange("p (h n) -> p h n", h=P_RING)
        probs_T = probs_T.rearrange("p (a c h n) -> p a c h n", a=2, c=3, h=2 * GROUP)
        k_parts = k_parts.bitcast(BF16).rearrange("p (s n) -> p s n", s=2)
        ctxT = ctxT.rearrange("p (s k n) -> p s k n", s=2, k=KC)
        biased = biased[0:S].rearrange("p (h n) -> p h n", h=SB_RING)
        k_rest = k_rest.rearrange("p (m n) -> p m n", m=KC)
        values = values.rearrange("p (s c n) -> p s c n", s=2, c=3)
        q_stack = q_stack[0:STACK].bitcast(BF16).rearrange("p (s n) -> p s n", s=2)


        xn = work[0:S, 0:2 * D].rearrange("p (s d) -> p s d", s=2)

        UP = KC * D + KC
        (w_up, w_down, b_down, xT_quad, x_tile, tile_T, act_T, y_tile, up_now, prefix, place, x_out, y_in) = carve(
            [E * UP, E * KC * D, E * D, 2 * KC * QUAD * S] + 4 * [2 * D] + [2 * UP, 2 * B * E, B * E] +
            2 * [WAVE * D])
        w_up = w_up.rearrange("p (e n) -> p e n", e=E)
        w_down = w_down.rearrange("p (e k n) -> p e k n", e=E, k=KC)
        b_down = b_down.rearrange("p (e n) -> p e n", e=E)
        up_now = up_now.rearrange("p (s n) -> p s n", s=2)
        xT_quad = xT_quad.rearrange("p (s k n) -> p s k n", s=2, k=KC)
        x_tile, y_tile = (t.rearrange("p (s n) -> p s n", s=2) for t in (x_tile, y_tile))
        x_out, y_in = (t[0:S].rearrange("p (s n) -> p s n", s=WAVE) for t in (x_out, y_in))
        tile_T, act_T = (t.rearrange("p (s k n) -> p s k n", s=2, k=KC) for t in (tile_T, act_T))
        prefix = prefix[0:S].rearrange("p (a b e) -> p a b e", a=2, b=B)
        place = place[0:S].rearrange("p (b e) -> p b e", b=B)

        x_in = sb("x_in", [S, 2, D])
        x_res = sb("x_res", [S, 2, D])
        xT = sb("xT", [P, 2, KC, S])
        q_parts = sb("q_parts", [P, 2, TERMS, KC, S], BF16)
        q_rest = sb("q_rest", [P, KC, S])
        bias = sb("bias", [S, 2, SK])
        neg_max = sb("neg_max", [S, 2, H])
        sums = sb("sums", [S, 2, H])
        inv = sb("inv", [S, H])
        inv_wide = sb("inv_wide", [S, 2, 2, P])
        inv_T = sb("inv_T", [P, 2 * 2 * S])
        heads_par = sb("heads_par", [P, 2, 2, S])
        heads_T = sb("heads_T", [P, KC, S])
        y = sb("y", [S, D])
        stats = sb("stats", [S, 6])
        moments = sb("moments", [S, 2])
        state_stats_of = sb("state_stats", [S, 6])
        state_moments_of = sb("state_moments", [S, 2])
        root_in, root_tmp, rstd = sb("root_in", [S, 2]), sb("root_tmp", [S, 2]), sb("rstd", [S, 2])
        all_moments = sb("all_moments", [S, B, 2])
        all_root_in, all_root_tmp, all_rstd = (sb(n, [S, B]) for n in ("all_root_in", "all_root_tmp", "all_rstd"))

        ps_scores = ctx.enter_context(nc.psum_tensor("ps_scores", [P, S_RING, 512], F32))
        ps_probs = ctx.enter_context(nc.psum_tensor("ps_probs", [P, 2, 512], F32))
        ps_heads = ctx.enter_context(nc.psum_tensor("ps_heads", [P, 512], F32))
        ps_a = ctx.enter_context(nc.psum_tensor("ps_a", [P, 512], F32))
        ps_b = ctx.enter_context(nc.psum_tensor("ps_b", [P, 512], F32))

        w_qkv = sb("w_qkv", [P, KC, 3 * D])
        weights = sb("weights", [P, len(PACKS["weights"]), KC, D])
        w = {n: weights[:, i] for i, n in enumerate(PACKS["weights"])}
        w_diag = {n: sb("wd_" + n, [P, KC, D]) for n in ("L1_attn_Wq", "L1_attn_Wk", "L1_attn_Wv")}
        b_qk = sb("b_qk", [P, 2 * KC])
        columns = sb("columns", [P, len(PACKS["columns"]) * KC])
        b_col = {n: columns[:, i * KC:(i + 1) * KC] for i, n in enumerate(PACKS["columns"])}
        b_zero = sb("b_zero", [P, KC])
        bias_rows = sb("bias_rows", [S, (len(PACKS["rows"]) - 1) * D + E])
        b_row = {n: bias_rows[:, i * D:min((i + 1) * D, bias_rows.shape[1])] for i, n in enumerate(PACKS["rows"])}
        w_gate = sb("w_gate", [P, KC, E])

        k_bounce = nc.dram_tensor("k_bounce", [2, TERMS * D * SK], BF16).ap()
        q_bounce = nc.dram_tensor("q_bounce", [2, TERMS * D * S], BF16).ap()

        bias_dram = nc.dram_tensor("bias_dram", [B, S, SK], F32).ap()

        xn_dram = nc.dram_tensor("xn_dram", [B, S, D], F32).ap()

        constants = sem("constants")
        passed = sem("passed")
        dist_loaded, bias_stored = [sem(f"dist_loaded_{i}") for i in range(len(dist))], sem("bias_stored")
        w_first, state_first, state_rest, diag_loaded, diag_scaled = (
            sem(n) for n in ("w_first", "state_first", "state_rest", "diag_loaded", "diag_scaled"))
        logs_ready = sem("logs_ready")
        bias_scaled = sem("bias_scaled")
        diag_cleared = sem("diag_cleared")
        w_loaded = sem("w_loaded")
        q_scaled = sem("q_scaled")
        ds_ready = sem("ds_ready")
        bv_out = sem("bv_out")
        b_out_ready = sem("b_out_ready")

        def rows(tile, first=0):
            return lambda k: tile[:, k, first:first + D]

        def by_feature(tile, first=0):
            return lambda k, m: tile[:, k, first + m * P:first + (m + 1) * P]

        sa0 = Attention(S, False, by_feature(w_qkv), by_feature(w_qkv, D), rows(w_qkv, 2 * D), w["L0_attn_w_o"],
                        b_qk[:, 0:KC], b_qk[:, KC:2 * KC], b_row["L0_attn_b_o"],
                        (w_qkv[:, :, 0:D], float(D) ** -0.5), False, True)
        xa0 = Attention(SK, True, by_feature(w["L0_xattn_Wq"]), by_feature(w["L0_xattn_Wk"]), rows(w["L0_xattn_Wv"]),
                        w["L0_xattn_Wo"], b_col["L0_xattn_bq"], b_col["L0_xattn_bk"], b_row["L0_xattn_bo"],
                        (w["L0_xattn_Wq"][:, :, :], DH ** -0.5), True, False)
        sa1 = Attention(S, False, by_feature(w_diag["L1_attn_Wq"]), by_feature(w_diag["L1_attn_Wk"]),
                        rows(w_diag["L1_attn_Wv"]), w["L1_attn_W_out"], b_zero, b_zero, b_row["L1_attn_b_out"],
                        (w_diag["L1_attn_Wq"][:, :, :], float(D) ** -0.5), False, False)
        xa1 = Attention(SK, True, by_feature(w["L1_xattn_Wq"]), by_feature(w["L1_xattn_Wk"]), rows(w["L1_xattn_Wv"]),
                        w["L1_xattn_Wo"], b_col["L1_xattn_bq"], b_col["L1_xattn_bk"], b_row["L1_xattn_bo"],
                        (w["L1_xattn_Wq"][:, :, :], DH ** -0.5), False, False)
        phases = [sa0, xa0, sa1, xa1]
        for first, second in ((sa0, xa0), (sa1, xa1)):
            first.next, second.prev = second, first
        value_biases = [(b_col["b_v"], sa0), (b_col["L0_xattn_bv"], xa0), (b_col["L1_xattn_bv"], xa1)]

        once = ["x_turned", "xT_ready", "q_done", "q_second", "q_split", "residual_ready",
                "inv_ready", "inv_turned", "inv_T_ready", "heads_scaled", "heads_ready",
                "out_projected", "y_ready", "stats_ready", "moments_ready", "root_in_ready", "guess_ready", "state_ready"]
        times = {name: lambda ph: 1 for name in once}
        times |= {name: lambda ph: KC for name in
                  ("k_done", "k_rounded", "k_rest_ready", "k_second", "k_split", "q_rounded", "q_rest_ready")}
        times |= {name: lambda ph: ph.chunks for name in ("v_projected", "v_ready")}
        times |= {name: lambda ph: ph.units for name in ("scores_ready", "maxed")}
        times |= {"root_step": lambda ph: ROOT_STEPS}
        times |= {"residual_once": lambda ph: int(ph.twice),
                  "probs_ready": lambda ph: H,
                  "probs_turned": lambda ph: ph.fills,
                  "act_copied": lambda ph: ph.by_dve.count(False),
                  "dve_copied": lambda ph: ph.by_dve.count(True),
                  "heads_summed": lambda ph: 2,
                  "inv_wide_ready": lambda ph: 2}
        signal = {name: sem(name) for name in times}
        dma_times = {"x_loaded": lambda ph: 16, "ctx_loaded": lambda ph: 16 * ph.cross,
                     "bias_loaded": lambda ph: 16 * ph.biased, "bounced": lambda ph: 16 * 2,
                     "stacked": lambda ph: 16 * 2 * len(PRODUCTS)}
        dma_signal = {name: [sem(f"{name}_{s}") for s in range(2)] for name in dma_times}
        for i, ph in enumerate(phases):
            ph.base = {name: sum(B * n(p) for p in phases[:i]) for name, n in times.items()}
            ph.base |= {name: sum(PAIRS * n(p) for p in phases[:i]) for name, n in dma_times.items()}

        def reached(eng, ph, name, count, alone=False, own=False):
            if isinstance(count, int) and count <= 0:
                if own or not ph.prev:
                    return
                mine, its = times[name](ph), times[name](ph.prev)
                count = count if mine == its else its * -(-count // mine) if mine else 0
            (apart if alone else at_least)(eng, signal[name], ph.base[name] + count)

        def arrived(eng, ph, name, b, back=0, alone=False):
            count = dma_times[name](ph) * (b[0] + 1 - back)
            (apart if alone else at_least)(eng, dma_signal[name][b[1]], ph.base[name] + count)

        def values_taken(eng, ph, i):
            if isinstance(i, int) and i > B:
                ph, i = (ph.next, i - B) if ph.next else (ph, B)
            reached(eng, ph, "v_ready", ph.chunks * i)

        ffn_work = Steps(PLAN_FFN, FFN_STEPS)
        ffn = {name: sem("ffn_" + name) for name in
               ("w_sum", "w_total", "w_mean", "w_step", "w_ready",
                "x_root_in", "x_scaled", "gained", "xn_ready", "row_maxed", "row_max", "max_turned", "max_one",
                "max_spread", "gamma_ready", "gain_ready", "xq_scaled", "xq_turned", "xqT_ready",
                "projected", "y_ready", "y_stats", "y_aggregated", "y_moments", "y_root_in", "y_guess", "y_root_step", "state_ready",
                "gamma_inverse")}
        xn_loaded, xn_stored = ([sem(f"ffn_{n}_{s}") for s in range(2)] for n in ("xn_loaded", "xn_stored"))
        row_maxes = sb("row_maxes", [S, B])
        row_max = sb("row_max", [S, 1])
        max_one = sb("max_one", [1, 1])
        gamma = sb("gamma", [S, 3])
        w_sum = sb("w_sum", [P, 1])
        w_beta = sb("w_beta", [P, 3])
        gain = sb("gain", [S, 2])
        xq = sb("xq", [S, 2, D])
        xqT = sb("xqT", [P, 2, KC, S])
        w_tmp = sb("w_tmp", [P, KC, D])

        moe_tiles = Steps(PLAN_TILES, TILE_STEPS)
        moe = {name: sem("moe_" + name) for name in
               ("w_loaded", "cleared", "x_cleared", "x_turned", "xT_ready", "gated", "logits_ready",
                "top_ready", "shifted", "exp_ready", "sum_ready", "weight_ready", "top_found", "rank_ready",
                "hot_found", "counted", "prefixed", "routed", "placed", "experts_known", "put", "tile_turned", "tile_T_ready",
                "up_ready", "up_done", "gelu_done", "down_done", "tile_kept", "slot_placed", "added",
                "y_stats", "y_aggregated", "y_moments", "y_root_in", "y_guess", "y_root_step", "shift_ready", "out_ready", "out_by_act")}
        tile_loaded, tile_stored = ([sem(f"moe_{n}_{s}") for s in range(2)] for n in ("tile_loaded", "tile_stored"))
        moved = [sem(f"moe_moved_{j}") for j in range(WAVE)]
        stored = sem("stored")
        logits = sb("logits", [S, B, E])
        top = sb("top", [S, B])
        shifted = sb("shifted", [S, B, E])
        exps = sb("exps", [S, B, E])
        top_weight = sb("top_weight", [S, B])
        rank = sb("rank", [S, B, E])
        rank_of = sb("rank_of", [S, E])
        hot = sb("hot", [S, B, E])
        below = sb("below", [S, S])
        room, room_tmp = sb("room", [S, 2, E]), sb("room_tmp", [S, 2, E])
        slot_of = sb("slot_of", [S, B])
        slot_now = sb("slot_now", [S, WAVE], I32)
        tile_first = sb("tile_first", [1, TILES])
        passed_by = sb("passed_by", [1, TILES, E])
        tile_expert = sb("tile_expert", [1, TILES])
        tile_expert_i = sb("tile_expert_i", [1, TILES], I32)

        x_sorted = nc.dram_tensor("x_sorted", [ROWS, D], F32).ap()
        y_sorted = nc.dram_tensor("y_sorted", [ROWS, D], F32).ap()

        block = ctx.enter_context(nc.Block())

        def apart(eng, sem, value):
            at_least(eng, sem, value)
            if not isinstance(value, int):
                eng.sem_inc(passed, 1)

        def number(b):
            return b[0] * 2 + b[1]

        def number_is(b, n):
            return isinstance(b[0], int) and number(b) == n

        def later(b, n):
            return (b[0] + (b[1] + n) // 2, (b[1] + n) % 2)

        def exists(b, count=B):
            return not isinstance(b[0], int) or 0 <= number(b) < count

        FIRST, LAST = (0, 0), (PAIRS - 1, 1)

        def over_batches(eng, body, ahead=0, behind=0, pairs=PAIRS):
            last = pairs - 1 - ahead // 2
            for pair in range(-ahead, 1):
                body((pair, 0))
                body((pair, 1))
            with eng.Fori(1, last) as pair:
                body((pair, 0))
                body((pair, 1))
            for pair in range(last, pairs + behind):
                body((pair, 0))
                body((pair, 1))

        def up_bank(s, m):
            return (ps_scores[:, s * KC + m] if s * KC + m < S_RING else ps_b)[:, 0:P]

        def over_waves(eng, body):
            body(0)
            with eng.Fori(1, WAVES - 1) as q:
                body(q)
            body(WAVES - 1)

        def due(ph, name, b, h):
            return [(later(b, -(at // ph.steps)), part) for part, at in enumerate(ph.plan.get(name, []))
                    if at % ph.steps == h and exists(later(b, -(at // ph.steps)))]

        def rounds_of(ph):
            first = min(min(steps) for steps in ph.plan.values())
            last = max(max(steps) for steps in ph.plan.values())
            return -(first // (2 * ph.steps)), -(-(last // ph.steps) // 2)

        def rounds(eng, work, step):
            def one(b):
                for h in range(work.steps):
                    step(work, b, h)
            over_batches(eng, one, *rounds_of(work))

        def over_two(eng, first, second, body, meeting, ahead, behind):
            def over(ph, pairs):
                for pair in pairs:
                    for s in range(2):
                        body(ph, (pair, s))

            over(first, range(-ahead[0], 1))
            meet, last = PAIRS - max(2, *ahead), PAIRS - 1 - ahead[1] // 2
            with eng.Fori(1, meet) as pair:
                over(first, [pair])
            meeting([(pair, s) for pair in range(meet, PAIRS + behind[0]) for s in range(2)])
            whole = max(1, *behind)
            over(second, range(behind[0], whole))
            with eng.Fori(whole, last) as pair:
                over(second, [pair])
            over(second, range(last, PAIRS + behind[1]))

        def attentions(eng, first, second, step):
            def one(ph, b):
                for h in range(H):
                    step(ph, b, h)

            def meeting(turns):
                for t in range(H * len(turns) + LAG):
                    for ph, back, lag in ((first, 0, 0), (second, B, LAG)):
                        turn, h = divmod(t - lag, H)
                        if 0 <= turn < len(turns):
                            step(ph, later(turns[turn], -back), h)

            ends = [rounds_of(ph) for ph in (first, second)]
            over_two(eng, first, second, one, meeting, [e[0] for e in ends], [max(1, e[1]) for e in ends])

        def bank_of(s, u):
            return (u + s) % S_RING

        def k_part(ph, s, t, m):
            first = (t * KC + m) * ph.keys
            return k_parts[:, s, first:first + ph.keys]

        def k_place(ph, m):
            return ps_b[:, 0:SK] if ph.cross else ps_b[:, m * S:(m + 1) * S]

        def copies(ph, b, f, dve):
            mine = [i for i in range(ph.fills) if ph.by_dve[i] == dve]
            return len(mine) * number(b) + sum(i <= f for i in mine)

        def wait_copied(eng, ph, b, f):
            if not exists(b) and ph.prev:
                reached(eng, ph, "dve_copied", 0)
                reached(eng, ph, "act_copied", 0)
                return
            dve = ph.by_dve[f]
            reached(eng, ph, "dve_copied" if dve else "act_copied", copies(ph, b, f, dve))

        def inverse_root(pool, step, before_it, value, scratch, result):
            for n in range(ROOT_STEPS // 4):
                at = before_it + 4 * n
                apart(pool, step, at)
                pool.tensor_tensor(scratch, result, result, ALU.mult).then_inc(step, 1)
                pool.wait_ge(step, at + 1)
                pool.tensor_tensor(scratch, scratch, value, ALU.mult).then_inc(step, 1)
                apart(pool, step, at + 2)
                pool.tensor_scalar(scratch, scratch, -0.5, 1.5, ALU.mult, ALU.add).then_inc(step, 1)
                pool.wait_ge(step, at + 3)
                pool.tensor_tensor(result, result, scratch, ALU.mult).then_inc(step, 1)

        @block.sync
        def _(sp):
            sp.dma_start(w_qkv[:, :, :], d["L0_attn_w_qkv"].rearrange("(k p) n -> p k n", p=P)).then_inc(w_first, 16)
            sp.dma_start(b_qk[:, :], d["L0_attn_b_qkv"][:, 0:2 * KC]).then_inc(w_first, 16)
            sp.dma_start(scaling[:, :], d["L0_xattn_distance_scaling"].rearrange("(a n) -> a n", a=1).to_broadcast([P, 1]))\
                .then_inc(w_first, 16)
            sp.dma_start(state[:, 0:QUAD, :], d["x"][0:QUAD].rearrange("b s d -> s b d")).then_inc(state_first, 16)
            flat = (d["fside_BxSxS2_0"].rearrange("b s k -> (b s k)").rearrange("(p n) -> p n", p=P),
                    bias_dram.rearrange("b s k -> (b s k)").rearrange("(p n) -> p n", p=P))
            for i, (first, size, part) in enumerate(dist):
                sp.dma_start(part, flat[0][:, first:first + size]).then_inc(dist_loaded[i], 16)

            def store_bias(i):
                first, size, part = dist[i]
                sp.wait_ge(bias_scaled, i + 1)
                sp.dma_start(flat[1][:, first:first + size], part).then_inc(bias_stored, 16)

            def clear_rows(b):
                sp.dma_start(x_sorted[bass.ds(number(b) * P, P), :], zeros).then_inc(moe["x_cleared"], 16)

            def load_small():
                sp.wait_ge(diag_cleared, len(w_diag))
                for n, t in w_diag.items():
                    for h in range(H):
                        at, k = h * DH % P, h * DH // P
                        if n == "L1_attn_Wv":
                            columns = t[at:at + DH, k, h * DH:(h + 1) * DH]
                        else:
                            columns = t[at:at + DH, k, :].rearrange("p (r f h) -> p r h f", r=KC, f=DH)[:, h % KC, h // KC]
                        sp.dma_start(columns, d[n], allow_slow_non_contiguous=True).then_inc(diag_loaded, 16)

            def load_x(ph, n):
                s, i = n[1], number(n)
                if ph.prev:
                    reached(sp, ph.prev, "state_ready", i + 1, alone=True)
                if ph is sa1:
                    apart(sp, ffn["state_ready"], i + 1)
                reached(sp, ph, "x_turned", i - 1)
                sp.dma_start(x_in[:, s, :], state[:, i, :]).then_inc(dma_signal["x_loaded"][s], 16)

            def load_context(ph, n):
                s, i = n[1], number(n)
                reached(sp, ph, "v_projected", ph.chunks * (i - 1), own=True)
                sp.dma_start(ctxT[:, s, :, :], d["ctx_1024"][i].rearrange("(k p) n -> p k n", p=P))\
                    .then_inc(dma_signal["ctx_loaded"][s], 16)

            def load_bias(ph, n):
                s, i = n[1], number(n)
                reached(sp, ph, "maxed", ph.units * (i - 1), own=True)
                sp.dma_start(bias[:, s, :], bias_dram[i]).then_inc(dma_signal["bias_loaded"][s], 16)

            def stack(ph, n):
                s, i = n[1], number(n)
                arrived(sp, ph, "stacked", n, back=1, alone=True)
                reached(sp, ph, "k_split", KC * (i + 1))
                def bounce(dram, parts, n):
                    place = dram[s, 0:TERMS * D * n].rearrange("(t p n) -> p t n", t=TERMS, p=P)
                    sp.dma_start(place, parts).then_inc(dma_signal["bounced"][s], 16)
                    return dram[s, 0:TERMS * D * n].rearrange("(t f n) -> t f n", t=TERMS, f=DH)

                kb = bounce(k_bounce, k_parts[:, s, 0:TERMS * KC * ph.keys].rearrange("p (t n) -> p t n", t=TERMS), ph.keys)
                reached(sp, ph, "q_split", i + 1)
                qb = bounce(q_bounce, q_parts[:, s, :, :, :].rearrange("p t m n -> p t (m n)"), S)
                arrived(sp, ph, "bounced", n, alone=True)
                reached(sp, ph, "scores_ready", ph.units * (i - 1))
                first = 0
                for part, meets in PRODUCTS:
                    rows = slice(first * DH, (first + meets) * DH)
                    sp.dma_start(k_stack[rows, s, 0:H * ph.keys], kb[0:meets].rearrange("t f n -> (t f) n"))\
                        .then_inc(dma_signal["stacked"][s], 16)
                    sp.dma_start(q_stack[rows, s, :], qb[part:part + 1].to_broadcast([meets, DH, H * S]))\
                        .then_inc(dma_signal["stacked"][s], 16)
                    first += meets

            def attend(first, second):
                def body(ph, b):
                    if ph is sa0 and number_is(b, 0):
                        sp.wait_ge(state_rest, 16)
                        for i in range(len(dist)):
                            store_bias(i)
                    if ph is sa0 and exists(b):
                        clear_rows(b)
                    if exists(later(b, 3)):
                        load_x(ph, later(b, 3))
                    if exists(later(b, 1)):
                        if ph.biased and number_is(later(b, 1), 0):
                            sp.wait_ge(bias_stored, 16 * len(dist))
                            sp.wait_ge(moe["x_cleared"], 16 * TILES)
                        if ph.biased:
                            load_bias(ph, later(b, 1))
                        stack(ph, later(b, 1))
                    if ph.cross and exists(later(b, 3)):
                        load_context(ph, later(b, 3))

                def meeting(turns):
                    for b in turns:
                        body(first, b)
                        body(second, later(b, -B))

                over_two(sp, first, second, body, meeting, (2, 2), (1, 0))
                if second is xa0:
                    load_small()
                reached(sp, second, "state_ready", B)

            sp.wait_ge(state_first, 16)
            sp.wait_ge(moe["cleared"], 1)
            assert TILES == B
            attend(sa0, xa0)
            def load_xn(n):
                s, i = n[1], number(n)
                at_least(sp, ffn["xq_scaled"], i - 1)
                sp.dma_start(xn[:, s, :], xn_dram[i]).then_inc(xn_loaded[s], 16)

            for s in range(2):
                sp.wait_ge(xn_stored[s], 16 * PAIRS)
            load_xn((0, 0))
            load_xn((0, 1))
            with sp.Fori(1, PAIRS) as pair:
                load_xn((pair, 0))
                load_xn((pair, 1))
            attend(sa1, xa1)
            for e in range(E):
                sp.dma_start(w_up[:, e, 0:KC * D].rearrange("p (k n) -> p k n", k=KC),
                             d["L1_ffn_W1"][e].rearrange("(k p) n -> p k n", p=P)).then_inc(moe["w_loaded"], 16)
                sp.dma_start(w_down[:, e], d["L1_ffn_W2"][e].rearrange("(k p) n -> p k n", p=P)).then_inc(moe["w_loaded"], 16)
            sp.dma_start(w_up[:, :, KC * D:], d["L1_ffn_b1"]).then_inc(moe["w_loaded"], 16)
            sp.dma_start(b_down[:, :, :], d["L1_ffn_b2"].rearrange("(a e) n -> a e n", a=1).to_broadcast([P, E, D]))\
                .then_inc(moe["w_loaded"], 16)

            for j in range(WAVE):
                sp.wait_ge(moved[j], 16 * WAVES)

            def load_tile(t):
                at_least(sp, moe["tile_turned"], number(t) - 1)
                sp.dma_start(x_tile[:, t[1], :], x_sorted[bass.ds(number(t) * P, P), :]).then_inc(tile_loaded[t[1]], 16)

            def store_tile(t):
                sp.wait_ge(moe["tile_kept"], number(t) + 1)
                sp.dma_start(y_sorted[bass.ds(number(t) * P, P), :], y_tile[:, t[1], :]).then_inc(tile_stored[t[1]], 16)

            def tiles(t):
                if exists(later(t, 2)):
                    load_tile(later(t, 2))
                if exists(later(t, -2)):
                    store_tile(later(t, -2))

            over_batches(sp, tiles, 1, 1)

            def store(q):
                sp.wait_ge(moe["out_ready"], QUAD // 2 * (q + 1))
                sp.wait_ge(moe["out_by_act"], QUAD // 2 * (q + 1))
                those = bass.ds(q * QUAD, QUAD)
                sp.dma_start(out[those].rearrange("b s d -> s b d"), state[:, those, :]).then_inc(stored, 16)

            with sp.Fori(0, QUADS) as q:
                store(q)
            sp.wait_ge(stored, 16 * QUADS)

        @block.tensor
        def _(pe):
            pe.wait_ge(constants, CONSTANTS)
            pe.wait_ge(w_first, 16 * 3)
            pe.wait_ge(q_scaled, 2)

            def prepare():
                pe.wait_ge(w_loaded, W_LOADED)
                for i, (bv, ph) in enumerate(value_biases):
                    at_least(pe, b_out_ready, i)
                    for k in range(KC):
                        mm = pe.matmul(ps_heads[0:S, 0:D], bv[:, k:k + 1].to_broadcast([P, S]), ph.wo[:, k, :],
                                       start=(k == 0), stop=(k == KC - 1))
                    mm.then_inc(bv_out, 1)
                pe.wait_ge(b_out_ready, len(value_biases))
                pe.wait_ge(ffn["w_sum"], 1)
                pe.matmul(ps_heads[:, 0:1], ones[:, :], w_sum[:, :], start=True, stop=True).then_inc(ffn["w_total"], 1)
                pe.wait_ge(ffn["w_mean"], 1)
                pe.wait_ge(q_scaled, Q_SCALED)

            def turn_x(ph, n):
                s, i = n[1], number(n)
                arrived(pe, ph, "x_loaded", n)
                reached(pe, ph, "q_rest_ready", KC * i)
                for k in range(KC):
                    mm = pe.transpose(ps_b[:, k * S:(k + 1) * S], x_in[:, s, k * P:(k + 1) * P], ident[0:S, 0:S])
                mm.then_inc(signal["x_turned"], 1)

            def keys_of(ph, n, m):
                s, i = n[1], number(n)
                if m == 0:
                    reached(pe, ph, "xT_ready", i + 1)
                    if ph.cross:
                        arrived(pe, ph, "ctx_loaded", n)
                elif ph.cross:
                    reached(pe, ph, "k_rest_ready", KC * i + m)
                source = ctxT if ph.cross else xT
                for k in range(KC):
                    mm = pe.matmul(k_place(ph, m), ph.wk(k, m), source[:, s, k, :], start=(k == 0), stop=(k == KC - 1))
                mm.then_inc(signal["k_done"], 1)

            def queries_of(ph, n):
                s, i = n[1], number(n)
                reached(pe, ph, "k_rest_ready", KC * (i + 1))
                for m in range(KC):
                    for k in range(KC):
                        mm = pe.matmul(ps_b[:, m * S:(m + 1) * S], ph.wq(k, m), xT[:, s, k, :],
                                       start=(k == 0), stop=(k == KC - 1))
                mm.then_inc(signal["q_done"], 1)

            def values_of(ph, n, c):
                s, i = n[1], number(n)
                source = ctxT if ph.cross else xT
                first, size = ph.spans[c]
                if c == 0:
                    reached(pe, ph, "xT_ready", i + 1)
                    if ph.cross:
                        arrived(pe, ph, "ctx_loaded", n)
                    reached(pe, ph, "inv_T_ready", i - 1)
                reached(pe, ph, "v_ready", ph.chunks * i + c)
                for k in range(KC):
                    lhsT = source[:, s, k, first:first + size]
                    mm = pe.matmul(ps_a[0:size, 0:D], lhsT, ph.wv(k), start=(k == 0), stop=(k == KC - 1))
                mm.then_inc(signal["v_projected"], 1)

            def scores_of(ph, b, u):
                s, i = b[1], number(b)
                if u == 0:
                    arrived(pe, ph, "stacked", b)
                if u >= S_RING:
                    held, at = u - S_RING, i
                else:
                    held, at = max(v for v in range(ph.units) if bank_of(1 - s, v) == bank_of(s, u)), i - 1
                if isinstance(at, int) and at < 0 and ph.prev:
                    held = max(v for v in range(ph.prev.units) if bank_of(1 - s, v) == bank_of(s, u))
                    reached(pe, ph.prev, "probs_ready", (B - 1) * H + (held + 1) * ph.prev.per_unit)
                elif ph.biased:
                    reached(pe, ph, "maxed", at * ph.units + held + 1)
                else:
                    reached(pe, ph, "probs_ready", at * H + (held + 1) * ph.per_unit)
                for j in range(ph.per_unit):
                    h = u * ph.per_unit + j
                    mm = pe.matmul(ps_scores[0:S, bank_of(s, u), j * ph.keys:(j + 1) * ph.keys],
                                   q_stack[:, s, h * S:(h + 1) * S], k_stack[:, s, h * ph.keys:(h + 1) * ph.keys], start=True, stop=True)
                mm.then_inc(signal["scores_ready"], 1)

            def turn_probs(ph, b, g, c):
                f = g * ph.chunks + c
                first, size = ph.spans[c]
                reached(pe, ph, "probs_ready", H * number(b) + GROUP * (g + 1))
                if f >= 2:
                    wait_copied(pe, ph, b, f - 2)
                else:
                    wait_copied(pe, ph, later(b, -1), ph.fills + f - 2)
                for j in range(GROUP):
                    mm = pe.transpose(ps_probs[0:size, f % 2, j * S:(j + 1) * S],
                                      probs[:, (g * GROUP + j) % P_RING, first:first + size], ident[0:S, 0:S])
                mm.then_inc(signal["probs_turned"], 1)

            def sum_heads(ph, b, half):
                s, i = b[1], number(b)
                last = (half + 1) * ph.fills // 2 - 1
                for dve in (False, True):
                    if dve in ph.by_dve:
                        reached(pe, ph, "dve_copied" if dve else "act_copied", copies(ph, b, last, dve))
                if half == 0:
                    reached(pe, ph, "v_ready", ph.chunks * (i + 1))
                    reached(pe, ph, "heads_scaled", i)
                for c, (first, size) in enumerate(ph.spans):
                    for j in range(4):
                        at = (4 * half + j) * 2 * DH
                        mm = pe.matmul(ps_heads[32 * j:32 * j + 32, half * 2 * S:(half + 1) * 2 * S],
                                       values[0:size, s, c, at:at + 2 * DH], probs_T[0:size, half, c, 2 * j:2 * j + 2, :],
                                       start=(c == 0), stop=(c == ph.chunks - 1))
                mm.then_inc(signal["heads_summed"], 1)

            def turn_inv(ph, b):
                i = number(b)
                reached(pe, ph, "inv_wide_ready", 2 * (i + 1))
                reached(pe, ph, "y_ready", i)
                values_taken(pe, ph, i + 2)
                for j in range(4):
                    mm = pe.transpose(ps_a[:, j * S:(j + 1) * S], inv_wide[:, j // 2, j % 2, :], ident[0:S, 0:S])
                mm.then_inc(signal["inv_turned"], 1)

            def project(ph, b):
                i = number(b)
                reached(pe, ph, "heads_ready", i + 1)
                values_taken(pe, ph, i + 3)
                for k in range(KC):
                    mm = pe.matmul(ps_a[0:S, 0:D], heads_T[:, k, :], ph.wo[:, k, :], start=(k == 0), stop=(k == KC - 1))
                mm.then_inc(signal["out_projected"], 1)

            def attend_step(ph, b, h):
                if ph is sa0 and number_is(b, 0) and h == PREPARE:
                    prepare()
                for n, u in due(ph, "scores", b, h):
                    scores_of(ph, n, u)
                for n, f in due(ph, "turn_probs", b, h):
                    turn_probs(ph, n, f // ph.chunks, f % ph.chunks)
                for n, _ in due(ph, "turn_inv", b, h):
                    turn_inv(ph, n)
                for n, half in due(ph, "sum_heads", b, h):
                    sum_heads(ph, n, half)
                for n, c in due(ph, "values", b, h):
                    values_of(ph, n, c)
                for n, _ in due(ph, "turn_x", b, h):
                    turn_x(ph, n)
                for n, m in due(ph, "keys", b, h):
                    keys_of(ph, n, m)
                for n, _ in due(ph, "queries", b, h):
                    queries_of(ph, n)
                for n, _ in due(ph, "project", b, h):
                    project(ph, n)

            def attend(first, second):
                attentions(pe, first, second, attend_step)
                reached(pe, second, "state_ready", B)

            attend(sa0, xa0)

            pe.wait_ge(ffn["row_max"], 1)
            pe.transpose(ps_a[0:1, 0:S], row_max[:, :], ident[0:S, 0:S]).then_inc(ffn["max_turned"], 1)
            pe.wait_ge(ffn["max_one"], 1)
            pe.matmul(ps_a[0:S, 0:1], ones[0:1, 0:S], max_one[:, :], start=True, stop=True).then_inc(ffn["max_spread"], 1)
            pe.wait_ge(ffn["w_ready"], 1)

            def ffn_turn(b):
                s, i = b[1], number(b)
                pe.wait_ge(ffn["xq_scaled"], i + 1)
                at_least(pe, ffn["xqT_ready"], i - 1)
                for k in range(KC):
                    mm = pe.transpose(ps_probs[:, s, k * S:(k + 1) * S], xq[:, s, k * P:(k + 1) * P], ident[0:S, 0:S])
                mm.then_inc(ffn["xq_turned"], 1)

            def ffn_project(b):
                s, i = b[1], number(b)
                pe.wait_ge(ffn["xqT_ready"], i + 1)
                at_least(pe, ffn["y_ready"], i - 1)
                for k in range(KC):
                    mm = pe.matmul(ps_scores[0:S, s, 0:D], xqT[:, s, k, :], w["L0_ffn_weight"][:, k, :],
                                   start=(k == 0), stop=(k == KC - 1))
                mm.then_inc(ffn["projected"], 1)

            def ffn_step(work, b, h):
                for n, _ in due(work, "turn", b, h):
                    ffn_turn(n)
                for n, _ in due(work, "project", b, h):
                    ffn_project(n)

            rounds(pe, ffn_work, ffn_step)
            pe.wait_ge(ffn["y_ready"], B)
            pe.wait_ge(diag_scaled, 1)
            attend(sa1, xa1)

            def turn_quad(q):
                s, i = q[1], number(q)
                at_least(pe, moe["xT_ready"], KC * (i - 1))
                for k in range(KC):
                    for j in range(QUAD):
                        mm = pe.transpose((ps_probs if s else ps_scores)[:, k, j * S:(j + 1) * S],
                                          state[:, i * QUAD + j, k * P:(k + 1) * P], ident[0:S, 0:S])
                mm.then_inc(moe["x_turned"], 1)

            def gate(q):
                s, i = q[1], number(q)
                if exists(later(q, 1), QUADS):
                    turn_quad(later(q, 1))
                pe.wait_ge(moe["xT_ready"], KC * (i + 1))
                at_least(pe, moe["logits_ready"], i - 1)
                for j in range(QUAD):
                    at = (ps_a if s else ps_heads)[0:S, j * E:(j + 1) * E]
                    for k in range(KC):
                        mm = pe.matmul(at, xT_quad[:, s, k, j * S:(j + 1) * S], w_gate[:, k, :], start=(k == 0),
                                       stop=(k == KC - 1))
                mm.then_inc(moe["gated"], 1)

            turn_quad((0, 0))
            for i in range(QUADS):
                gate((i // 2, i % 2))

            pe.wait_ge(moe["hot_found"], 1)
            chosen = hot[:, :, :].rearrange("p b e -> p (b e)")
            pe.matmul(ps_a[0:S, 0:B * E], ones[0:S, 0:S], chosen, start=True, stop=True)
            pe.matmul(ps_b[0:S, 0:B * E], below[:, :], chosen, start=True, stop=True).then_inc(moe["counted"], 1)
            pe.wait_ge(moe["placed"], 1)
            pe.wait_ge(moe["w_loaded"], 16 * (2 * E + 2))
            pe.wait_ge(moe["experts_known"], 1)

            def turn_tile(t):
                s, i = t[1], number(t)
                pe.wait_ge(tile_loaded[s], 16 * (t[0] + 1))
                at_least(pe, moe["tile_T_ready"], i - 1)
                for k in range(KC):
                    mm = pe.transpose(ps_probs[:, s, k * P:(k + 1) * P], x_tile[:, s, k * P:(k + 1) * P], ident[:, :])
                mm.then_inc(moe["tile_turned"], 1)

            def up(t):
                s, i = t[1], number(t)
                pe.wait_ge(moe["tile_T_ready"], i + 1)
                pe.wait_ge(moe["up_ready"], i + 1)
                at_least(pe, moe["gelu_done"], KC * (i - 1))
                for m in range(KC):
                    for k in range(KC):
                        pe.matmul(up_bank(s, m), up_now[:, s, k * D + m * P:k * D + (m + 1) * P],
                                  tile_T[:, s, k, :], start=(k == 0), stop=(k == KC - 1)).then_inc(moe["up_done"], 1)

            def down(t):
                s, i = t[1], number(t)
                e = pe.value_load(tile_expert_i[0:1, bass.ds(i, 1)], min_val=0, max_val=E - 1)
                pe.wait_ge(moe["gelu_done"], KC * (i + 1))
                at_least(pe, moe["tile_kept"], i - 1)
                for k in range(KC):
                    mm = pe.matmul((ps_heads if s else ps_a)[:, 0:D], act_T[:, s, k, :],
                                   w_down[:, bass.ds(e, 1), k, :].rearrange("p a n -> p (a n)"), start=(k == 0),
                                   stop=(k == KC - 1))
                mm.then_inc(moe["down_done"], 1)

            def tile_step(work, b, h):
                for t, _ in due(work, "up", b, h):
                    up(t)
                for t, _ in due(work, "turn", b, h):
                    turn_tile(t)
                for t, _ in due(work, "down", b, h):
                    down(t)

            rounds(pe, moe_tiles, tile_step)

        @block.scalar
        def _(act):
            def copy_xT(ph, n):
                s, i = n[1], number(n)
                reached(act, ph, "x_turned", i + 1)
                reached(act, ph, "q_done", i - 1)
                if not ph.cross or (ph.prev and isinstance(i, int)):
                    reached(act, ph, "v_projected", ph.chunks * (i - 1))
                act.activation(xT[:, s, :, :], ps_b[:, 0:KC * S].rearrange("p (k t) -> p k t", k=KC), ACT.Copy)\
                    .then_inc(signal["xT_ready"], 1)

            def round_keys(ph, n, m):
                s, i = n[1], number(n)
                if m == 0:
                    arrived(act, ph, "bounced", n, back=1)
                reached(act, ph, "k_done", KC * i + m + 1 if ph.cross else KC * (i + 1))
                act.activation(k_part(ph, s, 0, m), k_place(ph, m), ACT.Identity, bias=ph.bk[:, m:m + 1])\
                    .then_inc(signal["k_rounded"], 1)

            def round_queries(ph, n):
                s, i = n[1], number(n)
                reached(act, ph, "q_done", i + 1)
                for m in range(KC):
                    act.activation(q_parts[:, s, 0, m, :], ps_b[:, m * S:(m + 1) * S], ACT.Identity, bias=ph.bq[:, m:m + 1])\
                        .then_inc(signal["q_rounded"], 1)

            def copy_values(ph, n, c):
                s, i = n[1], number(n)
                first, size = ph.spans[c]
                reached(act, ph, "v_projected", ph.chunks * i + c + 1)
                reached(act, ph, "heads_summed", 2 * (i - 1))
                act.activation(values[0:size, s, c, :], ps_a[0:size, 0:D], ACT.Copy).then_inc(signal["v_ready"], 1)

            def exponentiate(ph, b, h):
                s, i = b[1], number(b)
                u, j = divmod(h, ph.per_unit)
                reached(act, ph, "maxed", ph.units * i + u + 1)
                if h % GROUP == 0:
                    if h >= P_RING:
                        reached(act, ph, "probs_turned", ph.fills * i + ph.chunks * ((h - P_RING) // GROUP + 1))
                    elif isinstance(i, int) and i == 0 and ph.prev:
                        reached(act, ph.prev, "probs_turned", ph.prev.fills * (B - 1) + ph.prev.chunks * ((h + P_RING) // GROUP + 1))
                    else:
                        reached(act, ph, "probs_turned", ph.fills * (i - 1) + ph.chunks * ((h + P_RING) // GROUP + 1))
                if ph.biased:
                    source, sign = biased[:, h % SB_RING, :], -1.0
                else:
                    source, sign = ps_scores[0:S, bank_of(s, u), j * ph.keys:(j + 1) * ph.keys], 1.0
                act.activation(probs[:, h % P_RING, 0:ph.keys], source, ACT.Exp, bias=neg_max[:, s, h:h + 1], scale=sign,
                               accum_out=sums[:, s, h:h + 1]).then_inc(signal["probs_ready"], 1)

            def copy_probs(ph, b, g, c):
                f, half = g * ph.chunks + c, g // 2
                first, size = ph.spans[c]
                if ph.by_dve[f]:
                    return
                reached(act, ph, "probs_turned", ph.fills * number(b) + f + 1)
                reached(act, ph, "heads_summed", 2 * (number(b) - 1) + half + 1)
                act.activation(probs_T[0:size, half, c, (g % 2) * GROUP:(g % 2 + 1) * GROUP, :],
                               ps_probs[0:size, f % 2, 0:GROUP * S].rearrange("p (h t) -> p h t", h=GROUP), ACT.Copy)\
                    .then_inc(signal["act_copied"], 1)

            def next_scale(ph, n):
                s, i = n[1], number(n)
                at_least(act, ffn["row_maxed"], i - 1)
                at_least(act, xn_stored[s], 16 * n[0])
                reached(act, ph, "state_ready", i + 1)
                act.activation(xq[:, s, :], state[:, i, :], ACT.Copy, scale=rstd[:, 1:2]).then_inc(ffn["x_scaled"], 1)

            def next_store(n):
                act.wait_ge(ffn["xn_ready"], number(n) + 1)
                act.dma_start(xn_dram[number(n)], xq[:, n[1], :]).then_inc(xn_stored[n[1]], 16)

            def copy_inv(ph, b):
                reached(act, ph, "inv_turned", number(b) + 1)
                reached(act, ph, "heads_scaled", number(b))
                act.activation(inv_T[:, :], ps_a[:, 0:4 * S], ACT.Copy).then_inc(signal["inv_T_ready"], 1)

            def attend_step(ph, b, h):
                if ph is sa0 and number_is(b, 0) and h == PREPARE:
                    act.wait_ge(w_loaded, W_LOADED)
                    act.wait_ge(q_scaled, Q_SCALED)
                for n, f in due(ph, "copy_probs", b, h):
                    copy_probs(ph, n, f // ph.chunks, f % ph.chunks)
                for n, _ in due(ph, "copy_inv", b, h):
                    copy_inv(ph, n)
                for n, c in due(ph, "copy_values", b, h):
                    copy_values(ph, n, c)
                for n, _ in due(ph, "copy_xT", b, h):
                    copy_xT(ph, n)
                for n, m in due(ph, "round_keys", b, h):
                    round_keys(ph, n, m)
                for n, _ in due(ph, "round_queries", b, h):
                    round_queries(ph, n)
                for n, head in due(ph, "exponentiate", b, h):
                    exponentiate(ph, n, head)
                for n, _ in due(ph, "next_scale", b, h):
                    next_scale(ph, n)
                for n, _ in due(ph, "next_store", b, h):
                    next_store(n)

            def attend(first, second):
                attentions(act, first, second, attend_step)

            act.wait_ge(constants, CONSTANTS)
            for i, (_, _, part) in enumerate(dist):
                act.wait_ge(dist_loaded[i], 16)
                act.activation(part, part, ACT.Ln, bias=tiny[:, :]).then_inc(logs_ready, 1)
            act.dma_start(state[:, QUAD:, :], d["x"][QUAD:].rearrange("b s d -> s b d")).then_inc(state_rest, 16)
            loads = [(weights[:, :, :, :].rearrange("p w k n -> p (w k) n"), d["weights"].rearrange("(w k p) n -> p (w k) n", k=KC, p=P)),
                     (columns[:, :], d["columns"]),
                     (bias_rows[:, :], d["rows"].rearrange("(a n) -> a n", a=1).to_broadcast([S, bias_rows.shape[1]])),
                     (w_gate[:, :, :], d["L1_ffn_Wg"].rearrange("(k p) e -> p k e", p=P))]
            for tile, source in loads:
                act.dma_start(tile, source).then_inc(w_loaded, 16)
            assert 16 * len(loads) == W_LOADED
            act.wait_ge(w_first, 16 * 3)
            act.wait_ge(q_scaled, 2)
            attend(sa0, xa0)

            def ffn_scale(b):
                s, i = b[1], number(b)
                act.wait_ge(xn_loaded[s], 16 * (b[0] + 1))
                at_least(act, ffn["xq_turned"], i - 1)
                act.activation(xq[:, s, :], xn[:, s, :], ACT.Copy, scale=gamma[:, 2:3]).then_inc(ffn["xq_scaled"], 1)

            def ffn_step(work, b, h):
                for n, _ in due(work, "scale", b, h):
                    ffn_scale(n)

            act.wait_ge(ffn["gamma_inverse"], 2)
            rounds(act, ffn_work, ffn_step)
            attend(sa1, xa1)

            def copy_quad(q):
                i = number(q)
                act.wait_ge(moe["x_turned"], i + 1)
                at_least(act, moe["gated"], i - 1)
                for k in range(KC):
                    act.activation(xT_quad[:, q[1], k, :], (ps_probs if q[1] else ps_scores)[:, k, 0:QUAD * S], ACT.Copy)\
                        .then_inc(moe["xT_ready"], 1)

            over_batches(act, copy_quad, pairs=QUADS // 2)
            act.wait_ge(moe["shifted"], 1)
            act.activation(exps[:, :, :], shifted[:, :, :], ACT.Exp).then_inc(moe["exp_ready"], 1)

            def copy_tile(t):
                s, i = t[1], number(t)
                act.wait_ge(moe["tile_turned"], i + 1)
                at_least(act, moe["up_done"], KC * KC * (i - 1))
                act.activation(tile_T[:, s, :, :], ps_probs[:, s, 0:D].rearrange("p (k t) -> p k t", k=KC), ACT.Copy)\
                    .then_inc(moe["tile_T_ready"], 1)

            def gelu(t, m):
                s, i = t[1], number(t)
                act.wait_ge(moe["up_done"], KC * KC * i + KC * (m + 1))
                if m == 0:
                    at_least(act, moe["down_done"], i - 1)
                act.activation(act_T[:, s, m, :], up_bank(s, m), ACT.Gelu,
                               bias=up_now[:, s, KC * D + m:KC * D + m + 1]).then_inc(moe["gelu_done"], 1)

            def tile_step(work, b, h):
                for t, _ in due(work, "copy_T", b, h):
                    copy_tile(t)
                for t, m in due(work, "gelu", b, h):
                    gelu(t, m)

            rounds(act, moe_tiles, tile_step)

            act.wait_ge(moe["shift_ready"], 1)
            for b in range(1, B, 2):
                act.activation(state[:, b, :], state[:, b, :], ACT.Identity, bias=all_root_in[:, b:b + 1],
                               scale=all_rstd[:, b:b + 1]).then_inc(moe["out_by_act"], 1)

        @block.vector
        def _(dve):
            dve.wait_ge(w_first, 16 * 3)
            def scale(tiles):
                for tile, by in tiles:
                    dve.tensor_scalar(tile, tile, float(by), None, ALU.mult).then_inc(q_scaled, 1)

            scale([sa0.q_scale, (sa0.bq[:, :], sa0.q_scale[1])])
            dve.scalar_tensor_tensor(neg_abs_ds[:, :], scaling[:, :], -1.0, scaling[:, :], ALU.mult, ALU.min).then_inc(ds_ready, 1)
            dve.wait_ge(ds_ready, 1)
            for i, (_, _, logs) in enumerate(dist):
                dve.wait_ge(logs_ready, i + 1)
                dve.tensor_scalar(logs, logs, neg_abs_ds[:, :], None, ALU.mult).then_inc(bias_scaled, 1)

            def prepare():
                dve.wait_ge(w_loaded, W_LOADED)
                dve.wait_ge(constants, CONSTANTS)
                scale([ph.q_scale for ph in (xa0, xa1)] + [(ph.bq[:, :], ph.q_scale[1]) for ph in (xa0, xa1)])
                for i, (bv, ph) in enumerate(value_biases):
                    dve.wait_ge(bv_out, i + 1)
                    dve.tensor_tensor(ph.bo[:, :], ph.bo[:, :], ps_heads[0:S, 0:D], ALU.add).then_inc(b_out_ready, 1)

                wf = w["L0_ffn_weight"][:, :, :].rearrange("p k n -> p (k n)")
                wt = w_tmp[:, :, :].rearrange("p k n -> p (k n)")
                dve.tensor_reduce(w_sum[:, :], wf, AX.X, ALU.add, apply_absolute_value=True).then_inc(ffn["w_sum"], 1)
                dve.wait_ge(ffn["w_total"], 1)
                dve.tensor_scalar(w_beta[:, 0:1], ps_heads[:, 0:1], 1.0 / (D * D), None, ALU.mult).then_inc(ffn["w_mean"], 1)
                dve.wait_ge(ffn["w_mean"], 1)
                dve.tensor_scalar(w_beta[:, 1:2], w_beta[:, 0:1], FFN_EPS, None, ALU.add).then_inc(ffn["w_step"], 1)
                dve.wait_ge(ffn["w_step"], 1)
                dve.reciprocal(w_beta[:, 2:3], w_beta[:, 1:2]).then_inc(ffn["w_step"], 1)
                dve.wait_ge(ffn["w_step"], 2)
                dve.tensor_scalar(wt, wf, w_beta[:, 2:3], None, ALU.mult).then_inc(ffn["w_step"], 1)
                dve.wait_ge(ffn["w_step"], 3)
                dve.tensor_scalar(wf, wt, ROUND, -ROUND, ALU.add, ALU.add).then_inc(ffn["w_step"], 1)
                dve.wait_ge(ffn["w_step"], 4)
                dve.tensor_scalar(wf, wf, -1.0, 1.0, ALU.max, ALU.min).then_inc(ffn["w_ready"], 1)

            def scale_small():
                dve.wait_ge(diag_loaded, 16 * len(w_diag) * H)
                tile, by = sa1.q_scale
                dve.tensor_scalar(tile, tile, float(by), None, ALU.mult).then_inc(diag_scaled, 1)

            def state_stats(b, stats_ready, aggregated):
                apart(dve, aggregated, b)
                dve.bn_stats(state_stats_of[:, :], state[:, b, :]).then_inc(stats_ready, 1)

            def state_moments(b, stats_ready, aggregated, kept):
                at_least(dve, kept, b)
                apart(dve, stats_ready, b + 1)
                dve.bn_aggr(state_moments_of[:, :], state_stats_of[:, :]).then_inc(aggregated, 1)

            def keep_moments(b, aggregated, kept):
                dve.wait_ge(aggregated, b + 1)
                dve.tensor_scalar(all_moments[:, b, :], state_moments_of[:, :], 1.0, None, ALU.mult).then_inc(kept, 1)

            def next_max(n):
                i = number(n)
                dve.wait_ge(ffn["xn_ready"], i + 1)
                dve.tensor_reduce(row_maxes[:, bass.ds(i, 1)], xq[:, n[1], :], AX.X, ALU.max, apply_absolute_value=True)\
                    .then_inc(ffn["row_maxed"], 1)

            def maximum(ph, b, u):
                s, i = b[1], number(b)
                if ph.biased:
                    if u == 0:
                        arrived(dve, ph, "bias_loaded", b)
                    reached(dve, ph, "probs_ready", H * i + u - SB_RING + 1, own=True)
                reached(dve, ph, "scores_ready", ph.units * i + u + 1, alone=ph.biased)
                if ph.biased:
                    dve.tensor_tensor_reduce(biased[:, u % SB_RING, :], ps_scores[0:S, bank_of(s, u), 0:ph.keys], bias[:, s, :],
                                             -1.0, 3.0e38, ALU.add, ALU.min, neg_max[:, s, u:u + 1])\
                        .then_inc(signal["maxed"], 1)
                else:
                    dve.tensor_reduce(neg_max[:, s, u * ph.per_unit:(u + 1) * ph.per_unit],
                                      ps_scores[0:S, bank_of(s, u), 0:ph.per_unit * ph.keys]
                                      .rearrange("p (h k) -> p h k", h=ph.per_unit),
                                      AX.X, ALU.max, negate=True).then_inc(signal["maxed"], 1)

            def copy_probs(ph, b, g, c):
                f, half = g * ph.chunks + c, g // 2
                first, size = ph.spans[c]
                if not ph.by_dve[f]:
                    return
                reached(dve, ph, "probs_turned", ph.fills * number(b) + f + 1)
                reached(dve, ph, "heads_summed", 2 * (number(b) - 1) + half + 1)
                dve.tensor_copy(probs_T[0:size, half, c, (g % 2) * GROUP:(g % 2 + 1) * GROUP, :],
                                ps_probs[0:size, f % 2, 0:GROUP * S].rearrange("p (h t) -> p h t", h=GROUP))\
                    .then_inc(signal["dve_copied"], 1)

            def rest_of_keys(ph, n, m):
                s, i = n[1], number(n)
                reached(dve, ph, "k_rounded", KC * i + m + 1 if ph.cross else KC * (i + 1))
                reached(dve, ph, "k_split", KC * (i - 1) + m + 1)
                dve.scalar_tensor_tensor(k_rest[:, m, 0:ph.keys], k_place(ph, m), ph.bk[:, m:m + 1],
                                         k_part(ph, s, 0, m), ALU.add, ALU.subtract)\
                    .then_inc(signal["k_rest_ready"], 1)

            def rest_of_queries(ph, n):
                s, i = n[1], number(n)
                reached(dve, ph, "q_split", i)
                reached(dve, ph, "q_rounded", KC * (i + 1))
                for m in range(KC):
                    dve.scalar_tensor_tensor(q_rest[:, m, :], ps_b[:, m * S:(m + 1) * S], ph.bq[:, m:m + 1],
                                             q_parts[:, s, 0, m, :], ALU.add, ALU.subtract)\
                        .then_inc(signal["q_rest_ready"], 1)

            def invert(ph, b):
                s, i = b[1], number(b)
                reached(dve, ph, "probs_ready", H * (i + 1))
                dve.reciprocal(inv[:, :], sums[:, s, :]).then_inc(signal["inv_ready"], 1)
                reached(dve, ph, "inv_ready", i + 1)
                reached(dve, ph, "inv_turned", i)
                for parity in range(2):
                    rows = inv_wide[:, :, parity, :].rearrange("p a (j r f) -> p a j r f", j=4, r=2)[:, :, :, parity, :]
                    by_head = inv[:, :].rearrange("p (a j r) -> p a j r", a=2, j=4)[:, :, :, parity:parity + 1]
                    dve.tensor_copy(rows, by_head.to_broadcast([S, 2, 4, DH])).then_inc(signal["inv_wide_ready"], 1)

            def scale_heads(ph, b):
                i = number(b)
                reached(dve, ph, "heads_summed", 2 * (i + 1))
                reached(dve, ph, "inv_T_ready", i + 1)
                reached(dve, ph, "heads_ready", i)
                wide = heads_par[:, :, :, :].rearrange("p a r t -> p (a r t)")
                dve.tensor_tensor(wide, ps_heads[:, 0:4 * S], inv_T[:, :], ALU.mult).then_inc(signal["heads_scaled"], 1)
                reached(dve, ph, "heads_scaled", i + 1)
                reached(dve, ph, "out_projected", i)
                dve.tensor_tensor(heads_T[:, :, :], heads_par[:, :, 0, :], heads_par[:, :, 1, :], ALU.add)\
                    .then_inc(signal["heads_ready"], 1)

            def add_residual(ph, b):
                s, i = b[1], number(b)
                reached(dve, ph, "out_projected", i + 1)
                reached(dve, ph, "residual_ready", i + 1)
                reached(dve, ph, "state_ready", i)
                dve.tensor_tensor(y[:, :], ps_a[0:S, 0:D], x_res[:, s, :], ALU.add).then_inc(signal["y_ready"], 1)

            def take_stats(ph, b):
                reached(dve, ph, "y_ready", number(b) + 1)
                dve.bn_stats(stats[:, :], y[:, :]).then_inc(signal["stats_ready"], 1)

            def take_moments(ph, b):
                reached(dve, ph, "stats_ready", number(b) + 1, alone=True)
                dve.bn_aggr(moments[:, :], stats[:, :]).then_inc(signal["moments_ready"], 1)

            def guess_root(ph, b):
                i = number(b)
                reached(dve, ph, "moments_ready", i + 1)
                reached(dve, ph, "root_step", ROOT_STEPS * i)
                dve.tensor_scalar(root_in[:, 0:1], moments[:, 1:2], LN_EPS, None, ALU.add).then_inc(signal["root_in_ready"], 1)
                reached(dve, ph, "root_in_ready", i + 1)
                if ph.biased:
                    dve.reciprocal(root_in[:, 1:2], root_in[:, 0:1]).then_inc(ffn["x_root_in"], 1)
                    apart(dve, ffn["x_root_in"], 2 * i + 1)
                    dve.tensor_scalar(root_in[:, 1:2], root_in[:, 1:2], moments[:, 1:2], FFN_LN_EPS, ALU.mult, ALU.add)\
                        .then_inc(ffn["x_root_in"], 1)
                    at_least(dve, ffn["x_scaled"], i)
                    dve.wait_ge(ffn["x_root_in"], 2 * i + 2)
                n = ph.norms
                dve.tensor_scalar(rstd[:, 0:n].bitcast(I32), root_in[:, 0:n].bitcast(I32), -0.5, ROOT_GUESS, ALU.mult, ALU.add)\
                    .then_inc(signal["guess_ready"], 1)

            def norm(ph, b):
                i = number(b)
                reached(dve, ph, "root_step", ROOT_STEPS * (i + 1))
                dve.tensor_scalar(state[:, i, :], y[:, :], moments[:, 0:1], rstd[:, 0:1], ALU.subtract, ALU.mult)\
                    .then_inc(signal["state_ready"], 1)

            def attend_step(ph, b, h):
                if ph is sa0 and number_is(b, 0) and h == PREPARE:
                    prepare()
                for n, u in due(ph, "maximum", b, h):
                    maximum(ph, n, u)
                for n, f in due(ph, "copy_probs", b, h):
                    copy_probs(ph, n, f // ph.chunks, f % ph.chunks)
                for n, _ in due(ph, "invert", b, h):
                    invert(ph, n)
                for n, _ in due(ph, "scale_heads", b, h):
                    scale_heads(ph, n)
                for n, m in due(ph, "rest_of_keys", b, h):
                    rest_of_keys(ph, n, m)
                for n, _ in due(ph, "rest_of_queries", b, h):
                    rest_of_queries(ph, n)
                for n, _ in due(ph, "add_residual", b, h):
                    add_residual(ph, n)
                for n, _ in due(ph, "take_stats", b, h):
                    take_stats(ph, n)
                for n, _ in due(ph, "take_moments", b, h):
                    take_moments(ph, n)
                for n, _ in due(ph, "guess_root", b, h):
                    guess_root(ph, n)
                for n, _ in due(ph, "norm", b, h):
                    norm(ph, n)
                for n, _ in due(ph, "next_max", b, h):
                    next_max(n)

            def attend(first, second):
                attentions(dve, first, second, attend_step)

            def guess(root_in_ready, count, guess_ready, variance, eps, value, result):
                dve.tensor_scalar(value, variance, eps, None, ALU.add).then_inc(root_in_ready, 1)
                dve.wait_ge(root_in_ready, count)
                dve.tensor_scalar(result.bitcast(I32), value.bitcast(I32), -0.5, ROOT_GUESS, ALU.mult, ALU.add)\
                    .then_inc(guess_ready, 1)

            attend(sa0, xa0)

            dve.wait_ge(ffn["row_maxed"], B)
            dve.tensor_reduce(row_max[:, :], row_maxes[:, :], AX.X, ALU.max).then_inc(ffn["row_max"], 1)
            dve.wait_ge(ffn["max_turned"], 1)
            dve.tensor_reduce(max_one[:, :], ps_a[0:1, 0:S], AX.X, ALU.max).then_inc(ffn["max_one"], 1)
            dve.wait_ge(ffn["max_spread"], 1)
            dve.tensor_copy(gamma[:, 0:1], ps_a[0:S, 0:1]).then_inc(ffn["gamma_ready"], 1)
            dve.wait_ge(ffn["gamma_ready"], 1)
            dve.reciprocal(gamma[:, 1:2], gamma[:, 0:1]).then_inc(ffn["gamma_inverse"], 1)
            dve.wait_ge(ffn["gamma_inverse"], 1)
            dve.tensor_scalar(gamma[:, 2:3], gamma[:, 1:2], QB, None, ALU.mult).then_inc(ffn["gamma_inverse"], 1)
            dve.tensor_scalar(gain[:, 0:1], gamma[:, 0:1], w_beta[0:S, 0:1], 1.0 / QB, ALU.mult, ALU.mult)\
                .then_inc(ffn["gain_ready"], 1)
            dve.wait_ge(ffn["gain_ready"], 1)
            dve.wait_ge(ffn["gamma_inverse"], 1)

            def ffn_clip(b):
                s, i = b[1], number(b)
                dve.wait_ge(ffn["xq_turned"], i + 1)
                at_least(dve, ffn["projected"], i - 1)
                dve.tensor_scalar(xqT[:, s, :, :], ps_probs[:, s, 0:KC * S].rearrange("p (k t) -> p k t", k=KC),
                                  -QB + FFN_EPS, QB - FFN_EPS, ALU.max, ALU.min).then_inc(ffn["xqT_ready"], 1)

            def ffn_add(b):
                s, i = b[1], number(b)
                dve.wait_ge(ffn["projected"], i + 1)
                dve.scalar_tensor_tensor(state[:, i, :], ps_scores[0:S, s, 0:D], gain[:, 0:1], state[:, i, :], ALU.mult, ALU.add)\
                    .then_inc(ffn["y_ready"], 1)

            def ffn_step(work, b, h):
                for n, _ in due(work, "clip", b, h):
                    ffn_clip(n)
                for n, _ in due(work, "add", b, h):
                    ffn_add(n)
                for n, _ in due(work, "take_stats", b, h):
                    dve.wait_ge(ffn["y_ready"], number(n) + 1)
                    state_stats(number(n), ffn["y_stats"], ffn["y_aggregated"])
                for n, _ in due(work, "take_moments", b, h):
                    state_moments(number(n), ffn["y_stats"], ffn["y_aggregated"], ffn["y_moments"])
                for n, _ in due(work, "keep_moments", b, h):
                    keep_moments(number(n), ffn["y_aggregated"], ffn["y_moments"])

            scale_small()
            rounds(dve, ffn_work, ffn_step)
            dve.wait_ge(ffn["y_moments"], B)
            guess(ffn["y_root_in"], 1, ffn["y_guess"], all_moments[:, :, 1], LN_EPS, all_root_in[:, :], all_rstd[:, :])
            dve.wait_ge(ffn["y_root_step"], ROOT_STEPS)

            def ffn_out(b):
                dve.tensor_scalar(state[:, b, :], state[:, b, :], all_moments[:, b, 0:1], all_rstd[:, bass.ds(b, 1)],
                                  ALU.subtract, ALU.mult).then_inc(ffn["state_ready"], 1)

            for b in range(B):
                ffn_out(b)
            attend(sa1, xa1)

            def keep_logits(q):
                i = number(q)
                dve.wait_ge(moe["gated"], i + 1)
                dve.tensor_tensor(logits[:, bass.ds(i * QUAD, QUAD), :],
                                  (ps_a if q[1] else ps_heads)[0:S, 0:QUAD * E].rearrange("p (b e) -> p b e", b=QUAD),
                                  b_row["L1_ffn_bg"].rearrange("p (a e) -> p a e", a=1).to_broadcast([S, QUAD, E]), ALU.add)\
                    .then_inc(moe["logits_ready"], 1)

            over_batches(dve, keep_logits, pairs=QUADS // 2)

            def per_token(t):
                return t[:, :].rearrange("p (b a) -> p b a", a=1).to_broadcast([S, B, E])

            dve.wait_ge(moe["logits_ready"], QUADS)
            dve.tensor_reduce(top[:, :], logits[:, :, :], AX.X, ALU.max).then_inc(moe["top_ready"], 1)
            dve.wait_ge(moe["top_ready"], 1)
            dve.tensor_tensor(shifted[:, :, :], logits[:, :, :], per_token(top), ALU.subtract).then_inc(moe["shifted"], 1)
            dve.tensor_tensor(rank[:, :, :], logits[:, :, :], per_token(top), ALU.is_ge).then_inc(moe["top_found"], 1)
            dve.wait_ge(moe["exp_ready"], 1)
            dve.tensor_reduce(top_weight[:, :], exps[:, :, :], AX.X, ALU.add).then_inc(moe["sum_ready"], 1)
            dve.wait_ge(moe["top_found"], 1)
            by_expert = rank_of[:, :].rearrange("p (a e) -> p a e", a=1).to_broadcast([S, B, E])
            dve.tensor_tensor(hot[:, :, :], rank[:, :, :], by_expert, ALU.mult).then_inc(moe["rank_ready"], 1)
            dve.wait_ge(moe["sum_ready"], 1)
            dve.reciprocal(top_weight[:, :], top_weight[:, :]).then_inc(moe["weight_ready"], 1)
            dve.wait_ge(moe["rank_ready"], 1)
            dve.tensor_reduce(top[:, :], hot[:, :, :], AX.X, ALU.max).then_inc(moe["top_ready"], 1)
            dve.wait_ge(moe["top_ready"], 2)
            dve.tensor_tensor(hot[:, :, :], hot[:, :, :], per_token(top), ALU.is_equal).then_inc(moe["hot_found"], 1)

            dve.wait_ge(moe["counted"], 1)
            in_batch = ps_a[0:S, 0:B * E].rearrange("p (b e) -> p b e", b=B)
            dve.tensor_copy(prefix[:, 0], in_batch).then_inc(moe["prefixed"], 2)
            for n in range(B.bit_length() - 1):
                ahead, now, then = 2 ** n, prefix[:, n % 2], prefix[:, (n + 1) % 2]
                dve.wait_ge(moe["prefixed"], 2 * (n + 1))
                dve.tensor_tensor(then[:, ahead:, :], now[:, ahead:, :], now[:, 0:B - ahead, :], ALU.add)\
                    .then_inc(moe["prefixed"], 1)
                dve.tensor_copy(then[:, 0:ahead, :], now[:, 0:ahead, :]).then_inc(moe["prefixed"], 1)
            up_to = prefix[:, (B.bit_length() - 1) % 2]
            dve.wait_ge(moe["prefixed"], 2 * B.bit_length())
            full, end = room[:, 0, :], room_tmp[:, 0, :]
            dve.tensor_scalar(full, up_to[:, B - 1, :], float(P - 1), 1.0 / P, ALU.add, ALU.mult).then_inc(moe["routed"], 1)
            dve.wait_ge(moe["routed"], 1)
            dve.tensor_scalar(full, full, -(P - 1) / (2.0 * P), ROUND, ALU.add, ALU.add).then_inc(moe["routed"], 1)
            dve.wait_ge(moe["routed"], 2)
            dve.tensor_scalar(full, full, -ROUND, float(P), ALU.add, ALU.mult).then_inc(moe["routed"], 1)
            dve.wait_ge(moe["routed"], 3)
            dve.tensor_copy(end, full).then_inc(moe["routed"], 1)
            for n in range(E.bit_length() - 1):
                ahead, now, then = 2 ** n, room_tmp[:, n % 2, :], room_tmp[:, (n + 1) % 2, :]
                dve.wait_ge(moe["routed"], 4 + 2 * n)
                dve.tensor_tensor(then[:, ahead:], now[:, ahead:], now[:, 0:E - ahead], ALU.add).then_inc(moe["routed"], 1)
                dve.tensor_copy(then[:, 0:ahead], now[:, 0:ahead]).then_inc(moe["routed"], 1)
            end = room_tmp[:, (E.bit_length() - 1) % 2, :]
            routed = 4 + 2 * (E.bit_length() - 1)
            dve.wait_ge(moe["routed"], routed)
            start = room[:, 1, :]
            dve.tensor_tensor(start, end, full, ALU.subtract).then_inc(moe["routed"], 1)
            each = [1, TILES, E]
            dve.tensor_tensor(passed_by[:, :, :], tile_first[:, :].rearrange("p (t a) -> p t a", a=1).to_broadcast(each),
                              end[0:1].rearrange("p (a e) -> p a e", a=1).to_broadcast(each), ALU.is_ge).then_inc(moe["routed"], 1)
            dve.tensor_tensor(place[:, :, :], up_to, in_batch, ALU.subtract).then_inc(moe["routed"], 1)
            dve.wait_ge(moe["routed"], routed + 3)
            dve.tensor_reduce(tile_expert[:, :], passed_by[:, :, :], AX.X, ALU.add).then_inc(moe["routed"], 1)
            dve.tensor_tensor(place[:, :, :], place[:, :, :], ps_b[0:S, 0:B * E].rearrange("p (b e) -> p b e", b=B), ALU.add)\
                .then_inc(moe["routed"], 1)
            dve.wait_ge(moe["routed"], routed + 5)
            dve.tensor_scalar(tile_expert_i[:, :], tile_expert[:, :], float(E - 1), None, ALU.min).then_inc(moe["experts_known"], 1)
            dve.tensor_tensor(place[:, :, :], place[:, :, :],
                              start.rearrange("p (a e) -> p a e", a=1).to_broadcast([S, B, E]), ALU.add).then_inc(moe["routed"], 1)
            dve.wait_ge(moe["routed"], routed + 6)
            dve.tensor_tensor(place[:, :, :], place[:, :, :], hot[:, :, :], ALU.mult).then_inc(moe["routed"], 1)
            dve.wait_ge(moe["routed"], routed + 7)
            dve.tensor_reduce(slot_of[:, :], place[:, :, :], AX.X, ALU.add).then_inc(moe["placed"], 1)
            dve.wait_ge(moe["placed"], 1)

            def place_row(q, j):
                return dve.tensor_scalar(slot_now[:, j:j + 1], slot_of[:, bass.ds(q * WAVE + j, 1)], 1.0, None, ALU.mult)

            def put(q):
                for j in range(WAVE):
                    at_least(dve, moved[j], 16 * q)
                    place_row(q, j).then_inc(moe["put"], 1)
                    dve.tensor_scalar(x_out[:, j, :], state[:, q * WAVE + j, :], 1.0, None, ALU.mult).then_inc(moe["put"], 1)

            over_waves(dve, put)

            dve.wait_ge(moe["w_loaded"], 16 * (2 * E + 2))

            def expert_of(t):
                return dve.value_load(tile_expert_i[0:1, bass.ds(number(t), 1)], min_val=0, max_val=E - 1)

            def put_weight(t):
                s, i = t[1], number(t)
                e = expert_of(t)
                at_least(dve, moe["gelu_done"], KC * (i - 1))
                dve.tensor_copy(up_now[:, s, :], w_up[:, bass.ds(e, 1), :].rearrange("p a n -> p (a n)"))\
                    .then_inc(moe["up_ready"], 1)

            def keep_tile(t):
                s, i = t[1], number(t)
                e = expert_of(t)
                dve.wait_ge(moe["down_done"], i + 1)
                at_least(dve, tile_stored[s], 16 * t[0])
                dve.tensor_tensor(y_tile[:, s, :], (ps_heads if s else ps_a)[:, 0:D],
                                  b_down[:, bass.ds(e, 1), :].rearrange("p a n -> p (a n)"), ALU.add).then_inc(moe["tile_kept"], 1)

            def tile_step(work, b, h):
                for t, _ in due(work, "weights", b, h):
                    put_weight(t)
                for t, _ in due(work, "keep", b, h):
                    keep_tile(t)

            rounds(dve, moe_tiles, tile_step)

            def add_experts(q, j):
                i = q * WAVE + j
                dve.wait_ge(moved[j], 16 * (WAVES + q + 1))
                dve.scalar_tensor_tensor(state[:, i, :], y_in[:, j, :], top_weight[:, bass.ds(i, 1)], state[:, i, :], ALU.mult,
                                         ALU.add).then_inc(moe["added"], 1)
                if not isinstance(q, int) or q + 1 < WAVES:
                    place_row(q + 1, j).then_inc(moe["slot_placed"], 1)

            def take_stats(i):
                dve.wait_ge(moe["added"], i + 1)
                state_stats(i, moe["y_stats"], moe["y_aggregated"])

            def add_wave(q):
                first = q * WAVE
                for j in range(WAVE + 3):
                    if j < WAVE:
                        add_experts(q, j)
                    if 0 <= j - 3:
                        keep_moments(first + j - 3, moe["y_aggregated"], moe["y_moments"])
                    if 0 <= j - 2 < WAVE:
                        state_moments(first + j - 2, moe["y_stats"], moe["y_aggregated"], moe["y_moments"])
                    if 0 <= j - 1 < WAVE:
                        take_stats(first + j - 1)

            for j in range(WAVE):
                dve.wait_ge(moved[j], 16 * WAVES)
                place_row(0, j).then_inc(moe["slot_placed"], 1)
            over_waves(dve, add_wave)
            dve.wait_ge(moe["y_moments"], B)
            guess(moe["y_root_in"], 1, moe["y_guess"], all_moments[:, :, 1], LN_EPS, all_root_in[:, :], all_rstd[:, :])
            dve.wait_ge(moe["y_root_step"], ROOT_STEPS)
            dve.scalar_tensor_tensor(all_root_in[:, :], all_moments[:, :, 0], -1.0, all_rstd[:, :], ALU.mult, ALU.mult)\
                .then_inc(moe["shift_ready"], 1)
            for b in range(0, B, 2):
                dve.tensor_scalar(state[:, b, :], state[:, b, :], all_moments[:, b, 0:1], all_rstd[:, b:b + 1],
                                  ALU.subtract, ALU.mult).then_inc(moe["out_ready"], 1)

        @block.gpsimd
        def _(pool):
            pool.memset(zeros, 0.0).then_inc(moe["cleared"], 1)
            pool.memset(ident[:, :], 0.0).then_inc(constants, 1)
            pool.memset(ones[:, :], 1.0).then_inc(constants, 1)
            pool.memset(b_zero[:, :], 0.0).then_inc(constants, 1)
            pool.memset(tiny[:, :], 1e-9).then_inc(constants, 1)
            pool.memset(inv_wide[:, :, :, :], 0.0).then_inc(constants, 1)
            for e in range(E):
                pool.memset(rank_of[:, e:e + 1], float(E - e)).then_inc(constants, 1)
            for t in range(TILES):
                pool.memset(tile_first[:, t:t + 1], float(t * P)).then_inc(constants, 1)
            pool.memset(below[:, :], 1.0).then_inc(constants, 1)
            pool.wait_ge(constants, CONSTANTS - 2)
            pool.affine_select(out=below[:, :], in_=below[:, :], compare_op=ALU.is_gt, fill=0.0, base=0,
                               pattern=[[1, S]], channel_multiplier=-1).then_inc(constants, 1)
            pool.affine_select(out=ident[:, :], in_=ident[:, :], compare_op=ALU.not_equal, fill=1.0, base=0,
                               pattern=[[-1, P]], channel_multiplier=1).then_inc(constants, 1)

            for t in w_diag.values():
                pool.memset(t[:, :, :], 0.0).then_inc(diag_cleared, 1)

            def third_of_keys(ph, n, m):
                s, i = n[1], number(n)
                reached(pool, ph, "k_rest_ready", KC * i + m + 1, alone=True)
                pool.tensor_copy(k_part(ph, s, 1, m), k_rest[:, m, 0:ph.keys]).then_inc(signal["k_second"], 1)
                reached(pool, ph, "k_second", KC * i + m + 1)
                pool.tensor_tensor(k_part(ph, s, 2, m), k_rest[:, m, 0:ph.keys], k_part(ph, s, 1, m),
                                   ALU.subtract).then_inc(signal["k_split"], 1)

            def third_of_queries(ph, n):
                s, i = n[1], number(n)
                reached(pool, ph, "q_rest_ready", KC * (i + 1), alone=True)
                pool.tensor_copy(q_parts[:, s, 1, :, :], q_rest[:, :, :]).then_inc(signal["q_second"], 1)
                reached(pool, ph, "q_second", i + 1)
                pool.tensor_tensor(q_parts[:, s, 2, :, :], q_rest[:, :, :], q_parts[:, s, 1, :, :], ALU.subtract)\
                    .then_inc(signal["q_split"], 1)

            def residual(ph, n):
                s, i = n[1], number(n)
                if ph is sa0 and number_is(n, 0):
                    pool.wait_ge(b_out_ready, len(value_biases))
                    pool.wait_ge(state_first, 16)
                    pool.wait_ge(state_rest, 16)
                reached(pool, ph, "y_ready", i - 1, alone=True)
                if ph.prev:
                    reached(pool, ph.prev, "state_ready", i + 1, alone=True)
                first = pool.tensor_tensor(x_res[:, s, :], state[:, i, :], ph.bo[:, :], ALU.add)
                if ph.twice:
                    first.then_inc(signal["residual_once"], 1)
                    reached(pool, ph, "residual_once", i + 1, alone=True)
                    first = pool.tensor_tensor(x_res[:, s, :], x_res[:, s, :], state[:, i, :], ALU.add)
                first.then_inc(signal["residual_ready"], 1)

            def root(ph, b):
                i = number(b)
                reached(pool, ph, "guess_ready", i + 1)
                n = ph.norms
                inverse_root(pool, signal["root_step"], ph.base["root_step"] + ROOT_STEPS * i,
                             root_in[:, 0:n], root_tmp[:, 0:n], rstd[:, 0:n])

            def next_gain(n):
                s, i = n[1], number(n)
                pool.wait_ge(ffn["x_scaled"], i + 1)
                pool.tensor_tensor(xq[:, s, :], xq[:, s, :], b_row["L0_ffn_ln_gamma"], ALU.mult).then_inc(ffn["gained"], 1)
                pool.wait_ge(ffn["gained"], i + 1)
                pool.tensor_tensor(xq[:, s, :], xq[:, s, :], b_row["L0_ffn_ln_beta"], ALU.add).then_inc(ffn["xn_ready"], 1)

            def attend_step(ph, b, h):
                for n, _ in due(ph, "next_gain", b, h):
                    next_gain(n)
                for n, _ in due(ph, "root", b, h):
                    root(ph, n)
                for n, _ in due(ph, "residual", b, h):
                    residual(ph, n)
                for n, m in due(ph, "third_of_keys", b, h):
                    third_of_keys(ph, n, m)
                for n, _ in due(ph, "third_of_queries", b, h):
                    third_of_queries(ph, n)

            def attend(first, second):
                attentions(pool, first, second, attend_step)

            attend(sa0, xa0)
            pool.wait_ge(ffn["y_guess"], 1)
            inverse_root(pool, ffn["y_root_step"], 0, all_root_in[:, :], all_root_tmp[:, :], all_rstd[:, :])
            attend(sa1, xa1)
            pool.wait_ge(moe["x_cleared"], 16 * TILES)

            def scatter(q):
                for j in range(WAVE):
                    apart(pool, moe["put"], 2 * (q * WAVE + j + 1))
                    pool.indirect_dma_start(x_sorted, bass.IndirectOffsetOnAxis(ap=slot_now[:, j:j + 1], axis=0),
                                            x_out[:, j, :], None).then_inc(moved[j], 16)

            over_waves(pool, scatter)
            for s in range(2):
                pool.wait_ge(tile_stored[s], 16 * (TILES // 2))

            def fetch(q):
                for j in range(WAVE):
                    i = q * WAVE + j
                    at_least(pool, moe["added"], i + 1 - WAVE)
                    apart(pool, moe["slot_placed"], i + 1)
                    pool.indirect_dma_start(y_in[:, j, :], None, y_sorted,
                                            bass.IndirectOffsetOnAxis(ap=slot_now[:, j:j + 1], axis=0)).then_inc(moved[j], 16)

            over_waves(pool, fetch)
            pool.wait_ge(moe["y_guess"], 1)
            inverse_root(pool, moe["y_root_step"], 0, all_root_in[:, :], all_root_tmp[:, :], all_rstd[:, :])


TURNED = ("L0_attn_w_qkv", "L0_attn_w_o", "L0_xattn_Wq", "L0_xattn_Wk", "L0_xattn_Wv", "L0_xattn_Wo",
          "L1_attn_Wq", "L1_attn_Wk", "L1_attn_Wv", "L1_attn_W_out")
COLUMNS = ("b_v", "L0_xattn_bv", "L1_xattn_bv", "L1_ffn_b1")
STACKED = ("L0_attn_b_qkv", "L0_xattn_bq", "L0_xattn_bk", "L1_xattn_bq", "L1_xattn_bk")
ORDERED = ("L0_attn_w_qkv", "L0_xattn_Wq", "L0_xattn_Wk", "L1_xattn_Wq", "L1_xattn_Wk")
NAMES = ("x", "ctx_1024", "fside_BxSxS2_0", "L0_attn_w_qkv", "L0_attn_b_qkv", "L0_attn_w_o", "L0_attn_b_o", "L0_xattn_Wq",
         "L0_xattn_bq", "L0_xattn_Wk", "L0_xattn_bk", "L0_xattn_Wv", "L0_xattn_bv", "L0_xattn_Wo", "L0_xattn_bo",
         "L0_xattn_distance_scaling", "L0_ffn_weight", "L0_ffn_ln_gamma", "L0_ffn_ln_beta", "L1_attn_Wq", "L1_attn_Wk",
         "L1_attn_Wv", "L1_attn_W_out", "L1_attn_b_out", "L1_xattn_Wq", "L1_xattn_bq", "L1_xattn_Wk", "L1_xattn_bk",
         "L1_xattn_Wv", "L1_xattn_bv", "L1_xattn_Wo", "L1_xattn_bo", "L1_ffn_Wg", "L1_ffn_bg", "L1_ffn_W1", "L1_ffn_b1",
         "L1_ffn_W2", "L1_ffn_b2", "b_v")


def lay_out(inputs):
    arrays = {}
    for name in NAMES:
        a = np.asarray(inputs["L0_attn_b_qkv"][2 * D:] if name == "b_v" else inputs[name])
        if name in TURNED:
            a = a.T
        if name in COLUMNS:
            a = np.moveaxis(a.reshape(*a.shape[:-1], -1, P), -1, 0)
        if name in STACKED:
            a = a.reshape(-1, H // KC, KC, DH).transpose(3, 1, 0, 2).reshape(P, -1)
        if name in ORDERED:
            n = 2 * D if name == "L0_attn_w_qkv" else D
            turned = a[:, 0:n].reshape(D, -1, H // KC, KC, DH).transpose(0, 1, 3, 4, 2).reshape(D, n)
            a = np.concatenate([turned, a[:, n:]], axis=1)
        if name == "ctx_1024":
            a = a.transpose(0, 2, 1)
        arrays[name] = a if a.ndim else a.reshape(1)
    for pack, names in PACKS.items():
        arrays[pack] = np.concatenate([arrays.pop(n) for n in names], axis=1 if pack == "columns" else 0)
    return {name: np.ascontiguousarray(a) for name, a in arrays.items()}


def kernel(**inputs):
    from concourse import bacc
    from concourse.bass_utils import run_bass_kernel_spmd

    nc = bacc.Bacc("TRN2", target_bir_lowering=False, num_devices=1)
    arrays, d = lay_out(inputs), {}
    for name, a in arrays.items():
        d[name] = nc.dram_tensor("in_" + name, a.shape, mybir.dt.from_np(a.dtype), kind="ExternalInput").ap()
    out = nc.dram_tensor("out", (B, S, D), F32, kind="ExternalOutput").ap()
    decoder(nc, d, out)
    return run_bass_kernel_spmd(nc, [{"in_" + name: a for name, a in arrays.items()}], core_ids=[0]).results[0]["out"]
```
